# Optimizing a Trainium2 kernel written in Bass

```python
import numpy as np
import jax
import jax.numpy as jnp

def _softmax(x, axis=-1):
    return jax.nn.softmax(x, axis=axis)

def _gelu(x):
    return jax.nn.gelu(x, approximate=True)

def _silu(x):
    return jax.nn.silu(x)

def _sigmoid(x):
    return jax.nn.sigmoid(x)

def _layernorm(x, axis=-1, eps=1e-05):
    m = jnp.mean(x, axis=axis, keepdims=True)
    v = jnp.var(x, axis=axis, keepdims=True)
    return (x - m) / jnp.sqrt(v + eps)

def _scatter_add(tgt, idx, src, axis=0):
    return tgt.at[idx].add(src)

def _segment_sum(src, seg, n):
    return jax.ops.segment_sum(src, seg, n)
kernel_name = 'mk_seq_preln_d1_jaxref_r8_1cd66c'

def setup_inputs(seed: int=0):
    np.random.seed(seed)
    _w = jnp.asarray

    def _L0_attn_setup():
        import jax, jax.numpy as jnp
        import numpy as np
        B, S, D, H, L, F = (4, 256, 128, 16, 8, 512)
        DH = D // H

        def _ln(x, g, b):
            m = jnp.mean(x, axis=-1, keepdims=True)
            v = jnp.mean((x - m) ** 2, axis=-1, keepdims=True)
            return (x - m) * jax.lax.rsqrt(v + 1e-05) * g + b

        def _phi(t):
            return jax.nn.elu(t) + 1.0
        key = jax.random.key(seed)
        ks = jax.random.split(key, 12)
        s = 0.02
        n = jax.random.normal
        return {'x': n(ks[0], (B, S, D), jnp.float32), 'Wq': n(ks[1], (L, D, D), jnp.float32) * s, 'bq': jnp.zeros((L, D), jnp.float32), 'Wk': n(ks[2], (L, D, D), jnp.float32) * s, 'bk': jnp.zeros((L, D), jnp.float32), 'Wv': n(ks[3], (L, D, D), jnp.float32) * s, 'bv': jnp.zeros((L, D), jnp.float32), 'Wo': n(ks[4], (L, D, D), jnp.float32) * s, 'bo': jnp.zeros((L, D), jnp.float32), 'g1': jnp.ones((L, D), jnp.float32), 'be1': jnp.zeros((L, D), jnp.float32), 'g2': jnp.ones((L, D), jnp.float32), 'be2': jnp.zeros((L, D), jnp.float32), 'W1': n(ks[5], (L, D, F), jnp.float32) * s, 'c1': jnp.zeros((L, F), jnp.float32), 'W2': n(ks[6], (L, F, D), jnp.float32) * s, 'c2': jnp.zeros((L, D), jnp.float32), 'gf': jnp.ones((D,), jnp.float32), 'bef': jnp.zeros((D,), jnp.float32)}
    _L0_attn_in = _L0_attn_setup()

    def _L0_ffn_setup():
        import jax, jax.numpy as jnp
        import numpy as np
        E = 8
        K = 2
        D = 128
        H = 4 * D
        EPS = 1e-05
        TEMP = 1.5
        key = jax.random.key(seed)
        ks = jax.random.split(key, 6)
        B, T = (2, 256)
        x = jax.random.normal(ks[0], (B, T, D), dtype=jnp.float32)
        gamma = jnp.ones((D,), dtype=jnp.float32)
        beta = jnp.zeros((D,), dtype=jnp.float32)
        router_w = jax.random.normal(ks[1], (E, D), dtype=jnp.float32) * 0.02
        W1 = jax.random.normal(ks[2], (E, D, H), dtype=jnp.float32) * 0.02
        W2 = jax.random.normal(ks[3], (E, H, D), dtype=jnp.float32) * 0.02
        return {'x': x, 'gamma': gamma, 'beta': beta, 'router_w': router_w, 'W1': W1, 'W2': W2}
    _L0_ffn_in = _L0_ffn_setup()
    _d = {'L0_attn_x': _L0_attn_in['x'], 'L0_attn_Wq': _L0_attn_in['Wq'], 'L0_attn_bq': _L0_attn_in['bq'], 'L0_attn_Wk': _L0_attn_in['Wk'], 'L0_attn_bk': _L0_attn_in['bk'], 'L0_attn_Wv': _L0_attn_in['Wv'], 'L0_attn_bv': _L0_attn_in['bv'], 'L0_attn_Wo': _L0_attn_in['Wo'], 'L0_attn_bo': _L0_attn_in['bo'], 'L0_attn_g1': _L0_attn_in['g1'], 'L0_attn_be1': _L0_attn_in['be1'], 'L0_attn_g2': _L0_attn_in['g2'], 'L0_attn_be2': _L0_attn_in['be2'], 'L0_attn_W1': _L0_attn_in['W1'], 'L0_attn_c1': _L0_attn_in['c1'], 'L0_attn_W2': _L0_attn_in['W2'], 'L0_attn_c2': _L0_attn_in['c2'], 'L0_attn_gf': _L0_attn_in['gf'], 'L0_attn_bef': _L0_attn_in['bef'], 'L0_ffn_gamma': _L0_ffn_in['gamma'], 'L0_ffn_beta': _L0_ffn_in['beta'], 'L0_ffn_router_w': _L0_ffn_in['router_w'], 'L0_ffn_W1': _L0_ffn_in['W1'], 'L0_ffn_W2': _L0_ffn_in['W2']}
    _x0 = _d['L0_attn_x']
    _d['L0_attn_x'] = jax.random.normal(jax.random.fold_in(jax.random.key(seed), 1), (16, 256, 128), dtype=_x0.dtype)
    del _x0
    return _d

def reference(L0_attn_x, L0_attn_Wq, L0_attn_bq, L0_attn_Wk, L0_attn_bk, L0_attn_Wv, L0_attn_bv, L0_attn_Wo, L0_attn_bo, L0_attn_g1, L0_attn_be1, L0_attn_g2, L0_attn_be2, L0_attn_W1, L0_attn_c1, L0_attn_W2, L0_attn_c2, L0_attn_gf, L0_attn_bef, L0_ffn_gamma, L0_ffn_beta, L0_ffn_router_w, L0_ffn_W1, L0_ffn_W2):

    def _L0_attn_ref(x, Wq, bq, Wk, bk, Wv, bv, Wo, bo, g1, be1, g2, be2, W1, c1, W2, c2, gf, bef):
        import jax, jax.numpy as jnp
        import numpy as np
        B, S, D, H, L, F = (4, 256, 128, 16, 8, 512)
        DH = D // H

        def _ln(x, g, b):
            m = jnp.mean(x, axis=-1, keepdims=True)
            v = jnp.mean((x - m) ** 2, axis=-1, keepdims=True)
            return (x - m) * jax.lax.rsqrt(v + 1e-05) * g + b

        def _phi(t):
            return jax.nn.elu(t) + 1.0
        b, s, d = x.shape

        def layer(h, p):
            wq, bq_, wk, bk_, wv, bv_, wo, bo_, g1_, be1_, g2_, be2_, w1, c1_, w2, c2_ = p
            q = _phi((h @ wq + bq_).reshape(b, s, H, DH))
            k = _phi((h @ wk + bk_).reshape(b, s, H, DH))
            v = (h @ wv + bv_).reshape(b, s, H, DH)
            kv = jnp.einsum('bshd,bshm->bhdm', k, v)
            z = 1.0 / (jnp.einsum('bshd,bhd->bsh', q, k.sum(axis=1)) + 1e-06)
            att = jnp.einsum('bshd,bhdm,bsh->bshm', q, kv, z).reshape(b, s, d)
            h = h + att @ wo + bo_
            h = _ln(h, g1_, be1_)
            y = jax.nn.gelu(h @ w1 + c1_, approximate=False) @ w2 + c2_
            return (_ln(h + y, g2_, be2_), None)
        params = (Wq, bq, Wk, bk, Wv, bv, Wo, bo, g1, be1, g2, be2, W1, c1, W2, c2)
        h, _ = jax.lax.scan(layer, x, params)
        return _ln(h, gf, bef)

    def _L0_ffn_ref(x, gamma, beta, router_w, W1, W2):
        import jax, jax.numpy as jnp
        import numpy as np
        E = 8
        K = 2
        D = 128
        H = 4 * D
        EPS = 1e-05
        TEMP = 1.5
        res = x
        mu = jnp.mean(x, axis=-1, keepdims=True)
        var = jnp.mean(jnp.square(x - mu), axis=-1, keepdims=True)
        xn = (x - mu) * jax.lax.rsqrt(var + EPS) * gamma + beta
        logits = jnp.einsum('btd,ed->bte', xn, router_w)
        probs = jax.nn.softmax(logits / TEMP, axis=-1)
        w, idx = jax.lax.top_k(probs, K)
        wdense = jnp.sum(jax.nn.one_hot(idx, E, dtype=w.dtype) * w[..., None], axis=-2)
        h = jax.nn.silu(jnp.einsum('btd,edf->betf', xn, W1))
        y = jnp.einsum('betf,efd->betd', h, W2)
        out = jnp.einsum('bte,betd->btd', wdense, y)
        return out + res
    x = L0_attn_x
    x = x + _L0_attn_ref(_layernorm(x, axis=-1), L0_attn_Wq, L0_attn_bq, L0_attn_Wk, L0_attn_bk, L0_attn_Wv, L0_attn_bv, L0_attn_Wo, L0_attn_bo, L0_attn_g1, L0_attn_be1, L0_attn_g2, L0_attn_be2, L0_attn_W1, L0_attn_c1, L0_attn_W2, L0_attn_c2, L0_attn_gf, L0_attn_bef)
    x = x + _L0_ffn_ref(_layernorm(x, axis=-1), L0_ffn_gamma, L0_ffn_beta, L0_ffn_router_w, L0_ffn_W1, L0_ffn_W2)
    return x

_drawn_inputs = setup_inputs


def setup_inputs(seed=0):
    import zlib

    import numpy as np

    out = dict(_drawn_inputs(seed))
    spreads = {'L0_attn_bq': (0.0, 2.0),
     'L0_attn_bk': (0.0, 2.0),
     'L0_attn_bv': (0.0, 0.1),
     'L0_attn_bo': (0.0, 0.1),
     'L0_attn_g1': (1.0, 0.2),
     'L0_attn_be1': (0.0, 0.1),
     'L0_attn_g2': (1.0, 0.2),
     'L0_attn_be2': (0.0, 0.1),
     'L0_attn_c1': (0.0, 0.1),
     'L0_attn_c2': (0.0, 0.1),
     'L0_attn_gf': (1.0, 0.2),
     'L0_attn_bef': (0.0, 0.1),
     'L0_ffn_gamma': (1.0, 0.6),
     'L0_ffn_beta': (0.0, 0.8)}
    factors = {'L0_attn_Wq': 153.253,
     'L0_attn_Wk': 102.48,
     'L0_ffn_router_w': 8.0,
     'L0_ffn_W1': 8.0,
     'L0_ffn_W2': 8.0}
    for name, (base, spread) in spreads.items():
        noise = np.random.default_rng([zlib.crc32(name.encode()), seed]).standard_normal(out[name].shape)
        drawn = base * np.exp(spread * noise) if base else spread * noise
        out[name] = jnp.asarray(drawn.astype(out[name].dtype))
    for name, factor in factors.items():
        out[name] = (out[name] * factor).astype(out[name].dtype)
    return out
```

```python
from contextlib import ExitStack

import numpy as np

import concourse.bass as bass
from concourse import mybir

F32 = mybir.dt.float32
F32R = mybir.dt.float32r
ALU = mybir.AluOpType
ACT = mybir.ActivationFunctionType
AX = mybir.AxisListType

P = 128
LAYERS = 8
EXPERTS = 8
HEADS, HEAD = 16, 8
FF = 4
HALVES = 8
T = 4
N = T * P
SLOTS = HALVES // 2
QKV = 3 * P
EPS = 1e-5
DEN_EPS = 1e-6
INV_TEMP = 1.0 / 1.5
KVW = P + HEADS
VW = P + 2

C_GIN, C_BIN = 0, 8
C_G1, C_B1 = 16, 24
C_BQ = 32
C_C1 = 40
C_GAMMA, C_BETA = 72, 73
C_END = 74
R_G2, R_B2 = 0, 9
R_G1, R_B1 = 18, 26
R_BKV = 34
R_GF, R_BF = 50, 51
R_END = 52
R2_BO, R2_C2 = 0, 9


def wait(eng, sem, count):
    if not isinstance(count, int) or count > 0:
        eng.wait_ge(sem, count)


def wait_apart(eng, sem, count, passed):
    wait(eng, sem, count)
    if not isinstance(count, int):
        eng.sem_inc(passed, 1)


def upto(l, s, h, per=1, base=0):
    return l * (HALVES * per) + per * (2 * s + h + 1 + base)


def build(nc, x, rows, rows2, cols, wqkv, wo, w1, w2, router, out):
    ctx = ExitStack()
    with ctx:
        def sb(name, shape, dt=F32):
            return ctx.enter_context(nc.sbuf_tensor(name, shape, dt))

        def sem(name):
            return ctx.enter_context(nc.semaphore(name))

        bank = [ctx.enter_context(nc.psum_tensor("ps01", [P, 2, 512], F32)),
                ctx.enter_context(nc.psum_tensor("ps23", [P, 2, 512], F32)),
                ctx.enter_context(nc.psum_tensor("ps45", [P, 2, 512], F32)),
                ctx.enter_context(nc.psum_tensor("ps67", [P, 2, 512], F32))]

        def ps(b):
            return bank[b // 2][:, b % 2, :]

        x_all = sb("x_all", [P, HALVES, T, P])
        res_a = sb("res_a", [P, HALVES, T, P])
        xt_hi = sb("xt_hi", [P, HALVES, N], F32R)
        xt_lo = sb("xt_lo", [P, HALVES, N], F32R)
        ident = sb("ident", [P, P])
        mask = sb("mask", [P, KVW])
        neg_half = sb("neg_half", [P, T])
        ones = sb("ones", [P, P])
        tri = sb("tri", [P, EXPERTS, EXPERTS])
        row = sb("row", [P, R_END, P])
        col = sb("col", [P, C_END])
        bq_neg = sb("bq_neg", [P, LAYERS])
        bq_one = sb("bq_one", [P, LAYERS])
        raw_qkv = sb("raw_qkv", [P, QKV])
        raw_w1 = sb("raw_w1", [P, N])
        scaled_qkv = sb("scaled_qkv", [P, QKV])
        scaled_w1 = sb("scaled_w1", [P, N])
        next_qkv = sb("next_qkv", [P, 2, QKV], F32R)
        this_qkv = sb("this_qkv", [P, 2, QKV], F32R)
        next_w1 = sb("next_w1", [P, 2, N], F32R)
        this_w1 = sb("this_w1", [P, 2, N], F32R)
        this_wo = sb("this_wo", [P, P])
        this_w2 = sb("this_w2", [P, FF, P])
        other_w2 = sb("other_w2", [P, FF, P])
        gain = sb("gain", [P, 2])
        gain1 = sb("gain1", [P, 1])
        boff = sb("boff", [P, P])
        two = range(2)
        eq = [sb(f"eq{h}", [P, N]) for h in two]
        qt = [sb(f"qt{h}", [P, N]) for h in two]
        kt = [sb(f"kt{h}", [P, T, P]) for h in two]
        ek = [sb(f"ek{h}", [P, T, P]) for h in two]
        v = [sb(f"v{h}", [P, T, VW]) for h in two]
        kv = [sb(f"kv{h}", [P, 2, KVW]) for h in two]
        den = [sb(f"den{h}", [P, T, HEADS]) for h in two]
        rec = [sb(f"rec{h}", [P, T, HEADS]) for h in two]
        att = [sb(f"att{h}", [P, T, P]) for h in two]
        att_t = [sb(f"att_t{h}", [P, N]) for h in two]
        s1 = [sb(f"s1{h}", [P, T, P]) for h in two]
        s2 = [sb(f"s2{h}", [P, T, P]) for h in two]
        x1_hi = [sb(f"x1_hi{h}", [P, N], F32R) for h in two]
        x1_lo = [sb(f"x1_lo{h}", [P, N], F32R) for h in two]
        res_f = [sb(f"res_f{h}", [P, T, P]) for h in two]
        hid = [sb(f"hid{h}", [P, FF, N]) for h in two]
        stat = [sb(f"stat{i}", [P, T, 6]) for i in range(4)]
        mv = [sb(f"mv{i}", [P, T, 2]) for i in range(4)]
        var = [sb(f"var{i}", [P, T]) for i in range(4)]
        rstd = [sb(f"rstd{i}", [P, T]) for i in range(4)]
        row2 = hid[0][:, :, :].rearrange("p c n -> p (c n)")
        row2b = hid[1][:, :, :].rearrange("p c n -> p (c n)")
        r_raw = sb("r_raw", [P, EXPERTS])
        r_sc = sb("r_sc", [P, EXPERTS])
        r_hi = sb("r_hi", [P, EXPERTS], F32R)
        r_lo = sb("r_lo", [P, EXPERTS], F32R)
        r_bias = sb("r_bias", [P, EXPERTS])
        ex = sb("ex", [P, T, EXPERTS])
        mx = sb("mx", [P, T])
        gt = sb("gt", [P, T, EXPERTS, EXPERTS])
        ge = sb("ge", [P, T, EXPERTS, EXPERTS])
        rank = sb("rank", [P, T, EXPERTS])
        gate = sb("gate", [P, EXPERTS, HALVES * T])
        e_bias = sb("e_bias", [P, EXPERTS, FF])

        x_in = [sem(f"x_in{u}") for u in range(HALVES)]
        par_in = sem("par_in")
        raw_in = sem("raw_in")
        qkv_in, wo_in, w1_in, w2_in = sem("qkv_in"), sem("wo_in"), sem("w1_in"), sem("w2_in")
        out_done = sem("out_done")
        pool_passed, act_passed, dve_passed, sp_passed = (sem(n) for n in ("pool_passed", "act_passed", "dve_passed", "sp_passed"))
        const_step, const_done, row_done = sem("const_step"), sem("const_done"), sem("row_done")
        qkv_scaled, qkv_split = sem("qkv_scaled"), sem("qkv_split")
        w1_scaled, w1_split = sem("w1_scaled"), sem("w1_split")
        gain_done, gain1_done = sem("gain_done"), sem("gain1_done")
        boff_done, bias_mm, bias_done = sem("boff_done"), sem("bias_mm"), sem("bias_done")
        q_mm, kvp_mm, kvm_mm, att_mm, attt_mm = (sem(n) for n in ("q_mm", "kvp_mm", "kvm_mm", "att_mm", "attt_mm"))
        wo_mm, t1_mm, w1_mm, w2_mm, t2_mm = (sem(n) for n in ("wo_mm", "t1_mm", "w1_mm", "w2_mm", "t2_mm"))
        q_rel, q_exp, k_rel, k_exp, attt_sb = (sem(n) for n in ("q_rel", "q_exp", "k_rel", "k_exp", "attt_sb"))
        x1_hi_done, hid_done, xt_hi_done = sem("x1_hi_done"), sem("hid_done"), sem("xt_hi_done")
        kt_done, v_done, qt_done, k_done, kv_done = (sem(n) for n in ("kt_done", "v_done", "qt_done", "k_done", "kv_done"))
        den_done, rec_done, att_done = sem("den_done"), sem("rec_done"), sem("att_done")
        s1_done, stat1_done, mv1_done, x1_done, x1_lo_done = (sem(n) for n in ("s1_done", "stat1_done", "mv1_done", "x1_done", "x1_lo_done"))
        s2_done, stat2_done, mv2_done, x2_done, xt_lo_done = (sem(n) for n in ("s2_done", "stat2_done", "mv2_done", "x2_done", "xt_lo_done"))
        var1_done, rstd1_done, var2_done, rstd2_done = (sem(n) for n in ("var1_done", "rstd1_done", "var2_done", "rstd2_done"))
        resf_mul, resf_done, resa_mul, resa_done = (sem(n) for n in ("resf_mul", "resf_done", "resa_mul", "resa_done"))
        f_step, f_mv, f_var, f_rstd = sem("f_step"), sem("f_mv"), sem("f_var"), sem("f_rstd")
        xn_done, ft_mm, xn_hi, xn_lo = sem("xn_done"), sem("ft_mm"), sem("xn_hi"), sem("xn_lo")
        r_prep, rb_mm, rb_done, r_mm, r_sub, r_ex, gate_done = (sem(n) for n in ("r_prep", "rb_mm", "rb_done", "r_mm", "r_sub", "r_ex", "gate_done"))
        e_scaled, e_split, eb_mm, eb_done = sem("e_scaled"), sem("e_split"), sem("eb_mm"), sem("eb_done")
        up_mm, up_done, down_mm, comb = sem("up_mm"), sem("up_done"), sem("down_mm"), sem("comb")
        w2e_in = [sem(f"w2e_in{k}") for k in range(2)]

        LAST = LAYERS - 1
        w1_set = [next_w1, this_w1]
        w2_set = [other_w2, this_w2]

        block = ctx.enter_context(nc.Block())

        @block.sync
        def _(sp):
            def load_raw(l):
                if not isinstance(l, int) or l > 0:
                    wait_apart(sp, qkv_scaled, l * 8, sp_passed)
                    wait_apart(sp, w1_scaled, l * 8, sp_passed)
                    wait_apart(sp, bias_mm, l * 8, sp_passed)
                sp.dma_start(raw_qkv[:, :], wqkv[bass.ds(l, 1)].rearrange("l p n -> (l p) n")).then_inc(raw_in, 16)
                sp.dma_start(raw_w1[:, :], w1[bass.ds(l, 1)].rearrange("l p n -> (l p) n")).then_inc(raw_in, 16)

            def set_qkv(l):
                wait_apart(sp, qkv_split, l * 8 + 8, sp_passed)
                wait_apart(sp, kvp_mm, upto(l, -1, 1), sp_passed)
                sp.dma_start(this_qkv[:, :, :].bitcast(F32), next_qkv[:, :, :].bitcast(F32)).then_inc(qkv_in, 16)

            def set_wo(l):
                wait_apart(sp, wo_mm, upto(l, -1, 1), sp_passed)
                sp.dma_start(this_wo[:, :], wo[bass.ds(l, 1)].rearrange("l p n -> (l p) n")).then_inc(wo_in, 16)

            def set_w1(l):
                wait_apart(sp, w1_split, l * 8 + 8, sp_passed)
                wait_apart(sp, w1_mm, upto(l, -1, 1, per=FF), sp_passed)
                sp.dma_start(this_w1[:, :, :].bitcast(F32), next_w1[:, :, :].bitcast(F32)).then_inc(w1_in, 16)

            def set_w2(l):
                wait_apart(sp, w2_mm, upto(l, -1, 1), sp_passed)
                sp.dma_start(this_w2[:, :, :],
                             w2[bass.ds(l, 1)].rearrange("l (c p) n -> (l p) c n", p=P)).then_inc(w2_in, 16)

            sp.dma_start(x_all[:, 0], x[0]).then_inc(x_in[0], 16)
            load_raw(0)
            sp.dma_start(col[:, :], cols).then_inc(par_in, 16)
            sp.dma_start(x_all[:, 1], x[1]).then_inc(x_in[1], 16)
            sp.dma_start(row[:, :, :], rows.partition_broadcast(P)).then_inc(par_in, 16)
            sp.dma_start(row2[:, 0:9 * P], rows2[0:9 * P].partition_broadcast(P)).then_inc(par_in, 16)
            sp.dma_start(row2b[:, 0:8 * P], rows2[9 * P:17 * P].partition_broadcast(P)).then_inc(par_in, 16)
            sp.dma_start(r_raw[:, :], router).then_inc(par_in, 16)
            for u in range(2, HALVES):
                sp.dma_start(x_all[:, u], x[u]).then_inc(x_in[u], 16)
            set_qkv(0)
            set_wo(0)

            def layer(l, last=False):
                if not last:
                    load_raw(l + 1)
                set_w1(l)
                set_w2(l)
                if not last:
                    set_qkv(l + 1)
                    set_wo(l + 1)

            layer(0)
            with sp.Fori(1, LAST) as l:
                layer(l)
            layer(LAST, last=True)

            for e in range(EXPERTS):
                if e == 0:
                    wait_apart(sp, w1_scaled, LAYERS * 8, sp_passed)
                    wait_apart(sp, bias_mm, LAYERS * 8, sp_passed)
                else:
                    wait_apart(sp, e_scaled, e, sp_passed)
                    wait_apart(sp, eb_mm, e, sp_passed)
                sp.dma_start(raw_w1[:, :], w1[LAYERS + e]).then_inc(raw_in, 16)
                if e == 1:
                    wait_apart(sp, w2_mm, upto(LAST, SLOTS - 1, 1), sp_passed)
                if e >= 2:
                    wait_apart(sp, down_mm, HALVES * (e - 1), sp_passed)
                sp.dma_start(w2_set[e % 2][:, :, :],
                             w2[LAYERS + e].rearrange("(c p) n -> p c n", p=P)).then_inc(w2e_in[e % 2], 16)
            for u in range(HALVES):
                wait_apart(sp, comb, HALVES * (EXPERTS - 1) + u + 1, sp_passed)
                sp.dma_start(out[u], res_a[:, u]).then_inc(out_done, 16)
            sp.wait_ge(out_done, 16 * HALVES)

        @block.gpsimd
        def _(pool):
            g = nc.gpsimd
            g.memset(ident[:, :], 0.0).then_inc(const_step, 1)
            g.memset(mask[:, :], 1.0).then_inc(const_step, 1)
            g.memset(tri[:, :, :], 1.0).then_inc(const_step, 1)
            g.memset(ones[:, :], 1.0).then_inc(const_step, 1)
            g.memset(neg_half[:, :], -0.5).then_inc(const_step, 1)
            for h in two:
                g.memset(v[h][:, :, P:VW], 1.0).then_inc(const_step, 1)
            pool.wait_ge(const_step, 7)
            g.affine_select(out=ident[:, :], in_=ident[:, :], compare_op=ALU.not_equal, fill=1.0, base=0,
                            pattern=[[-1, P]], channel_multiplier=1).then_inc(const_step, 1)
            same = mask[:, 0:P].rearrange("p (a b) -> p a b", b=HEAD)
            g.affine_select(out=same, in_=same, compare_op=ALU.is_ge, fill=0.0, base=0,
                            pattern=[[-HEAD, HEADS], [0, HEAD]], channel_multiplier=1).then_inc(const_step, 1)
            memb = mask[:, P:KVW]
            g.affine_select(out=memb, in_=memb, compare_op=ALU.is_ge, fill=0.0, base=0,
                            pattern=[[-HEAD, HEADS]], channel_multiplier=1).then_inc(const_step, 1)
            g.affine_select(out=tri[:, :, :], in_=tri[:, :, :], compare_op=ALU.is_gt, fill=0.0, base=0,
                            pattern=[[1, EXPERTS], [-1, EXPERTS]], channel_multiplier=0).then_inc(const_step, 1)
            pool.wait_ge(const_step, 11)
            g.affine_select(out=same, in_=same, compare_op=ALU.is_ge, fill=0.0, base=HEAD - 1,
                            pattern=[[HEAD, HEADS], [0, HEAD]], channel_multiplier=-1).then_inc(const_step, 1)
            g.affine_select(out=memb, in_=memb, compare_op=ALU.is_ge, fill=0.0, base=HEAD - 1,
                            pattern=[[HEAD, HEADS]], channel_multiplier=-1).then_inc(const_step, 1)
            pool.wait_ge(const_step, 13)
            g.memset(var[0][:, :], 0.0).then_inc(const_done, 1)

            def prep_qkv(l):
                wait_apart(pool, raw_in, l * 32 + 32, pool_passed)
                wait_apart(pool, qkv_split, l * 8, pool_passed)
                wait_apart(pool, boff_done, l * 8, pool_passed)
                g.tensor_copy(gain[:, 0:1], col[:, bass.ds(l + C_GIN, 1)]).then_inc(gain_done, 4)
                g.tensor_copy(gain[:, 1:2], col[:, bass.ds(l + C_BIN, 1)]).then_inc(gain_done, 4)
                wait_apart(pool, gain_done, l * 8 + 8, pool_passed)
                g.tensor_scalar(scaled_qkv[:, :], raw_qkv[:, :], gain[:, 0:1], 0.0,
                                ALU.mult, ALU.add).then_inc(qkv_scaled, 8)
                wait_apart(pool, qkv_scaled, l * 8 + 8, pool_passed)
                wait_apart(pool, qkv_in, l * 16, pool_passed)
                g.tensor_scalar(next_qkv[:, 0, :], scaled_qkv[:, :], 1.0, 0.0, ALU.mult, ALU.add).then_inc(qkv_split, 4)
                wait_apart(pool, qkv_split, l * 8 + 4, pool_passed)
                g.tensor_tensor(next_qkv[:, 1, :], scaled_qkv[:, :], next_qkv[:, 0, :].bitcast(F32),
                                ALU.subtract).then_inc(qkv_split, 4)
                wait_apart(pool, bias_mm, l * 8, pool_passed)
                g.tensor_scalar(boff[:, :], ones[:, :], gain[:, 1:2], 0.0,
                                ALU.mult, ALU.add).then_inc(boff_done, 8)

            def prep_w1(l):
                wait_apart(pool, w1_split, l * 8, pool_passed)
                g.tensor_copy(gain1[:, :], col[:, bass.ds(l + C_G1, 1)]).then_inc(gain1_done, 8)
                wait_apart(pool, gain1_done, l * 8 + 8, pool_passed)
                g.tensor_scalar(scaled_w1[:, :], raw_w1[:, :], gain1[:, :], 0.0,
                                ALU.mult, ALU.add).then_inc(w1_scaled, 8)
                wait_apart(pool, w1_scaled, l * 8 + 8, pool_passed)
                wait_apart(pool, w1_in, l * 16, pool_passed)
                g.tensor_scalar(next_w1[:, 0, :], scaled_w1[:, :], 1.0, 0.0, ALU.mult, ALU.add).then_inc(w1_split, 4)
                wait_apart(pool, w1_split, l * 8 + 4, pool_passed)
                g.tensor_tensor(next_w1[:, 1, :], scaled_w1[:, :], next_w1[:, 0, :].bitcast(F32),
                                ALU.subtract).then_inc(w1_split, 4)

            def inv_std(i, mvs, var_sem, rstd_sem, count):
                wait_apart(pool, mvs, count, pool_passed)
                g.tensor_scalar(var[i][:, :], mv[i][:, :, 1], 1.0, EPS, ALU.mult, ALU.add).then_inc(var_sem, 1)
                wait_apart(pool, var_sem, count, pool_passed)
                g.tensor_tensor(rstd[i][:, :], var[i][:, :], neg_half[:, :], ALU.pow).then_inc(rstd_sem, 1)

            def inv_std1(l, s, h):
                inv_std(h, mv1_done, var1_done, rstd1_done, upto(l, s, h))

            def inv_std2(l, s, h):
                inv_std(2 + h, mv2_done, var2_done, rstd2_done, upto(l, s, h, base=8))

            def rows_of(first, l, n=1):
                return row[:, bass.ds(l + first, 1), :].to_broadcast([P, T, P])

            def resid_f(l, s, h, lw):
                wait_apart(pool, x1_done, upto(l, s, h), pool_passed)
                wait_apart(pool, s2_done, upto(l, s - 1, h), pool_passed)
                g.tensor_tensor(res_f[h][:, :, :], s1[h][:, :, :], rows_of(R_G1, lw), ALU.mult).then_inc(resf_mul, 1)
                wait_apart(pool, resf_mul, upto(l, s, h), pool_passed)
                g.tensor_tensor(res_f[h][:, :, :], res_f[h][:, :, :], rows_of(R_B1, lw), ALU.add).then_inc(resf_done, 1)

            def resid_a(l, s, h, lw):
                u = (2 * s + h) % HALVES
                wait_apart(pool, x2_done, upto(l, s, h, base=8), pool_passed)
                wait_apart(pool, s1_done, upto(l, s, h), pool_passed)
                g.tensor_tensor(res_a[:, u], s2[h][:, :, :], rows_of(R_G2, lw), ALU.mult).then_inc(resa_mul, 1)
                wait_apart(pool, resa_mul, upto(l, s, h, base=8), pool_passed)
                g.tensor_tensor(res_a[:, u], res_a[:, u], rows_of(R_B2, lw), ALU.add).then_inc(resa_done, 1)

            pool.wait_ge(par_in, 16 * 5)
            prep_qkv(0)
            wait_apart(pool, raw_in, 32, pool_passed)
            g.tensor_tensor(row[:, R_B2:R_B2 + 9, :], row[:, R_B2:R_B2 + 9, :],
                            row2[:, 0:9 * P].rearrange("p (a b) -> p a b", b=P), ALU.add).then_inc(row_done, 1)
            g.tensor_tensor(row[:, R_B1:R_B1 + 8, :], row[:, R_B1:R_B1 + 8, :],
                            row2b[:, 0:8 * P].rearrange("p (a b) -> p a b", b=P), ALU.add).then_inc(row_done, 1)
            prep_w1(0)
            pool.wait_ge(row_done, 2)
            for s in range(SLOTS):
                for h in two:
                    inv_std2(-1, s, h)
                for h in two:
                    resid_a(-1, s, h, 0)

            def slot(l, s, first, last):
                p1, p2 = not first or s >= 1, not first or s >= 2
                lw1 = l if s >= 1 else l - 1
                lw2 = l if s >= 2 else l - 1
                if p1:
                    inv_std1(l, s - 1, 0)
                    inv_std1(l, s - 1, 1)
                    resid_f(l, s - 1, 0, lw1)
                if p2:
                    inv_std2(l, s - 2, 0)
                if p1:
                    resid_f(l, s - 1, 1, lw1)
                if p2:
                    inv_std2(l, s - 2, 1)
                    resid_a(l, s - 2, 0, lw2 + 1)
                    resid_a(l, s - 2, 1, lw2 + 1)
                if s == 1 and not last:
                    prep_qkv(l + 1)
                    prep_w1(l + 1)

            for s in range(SLOTS):
                slot(0, s, True, False)
            with pool.Fori(1, LAST) as l:
                for s in range(SLOTS):
                    slot(l, s, False, False)
            for s in range(SLOTS):
                slot(LAST, s, False, True)
            inv_std1(LAST, 3, 0)
            inv_std1(LAST, 3, 1)
            resid_f(LAST, 3, 0, LAST)
            inv_std2(LAST, 2, 0)
            resid_f(LAST, 3, 1, LAST)
            inv_std2(LAST, 2, 1)
            resid_a(LAST, 2, 0, LAYERS)
            resid_a(LAST, 2, 1, LAYERS)
            for h in two:
                inv_std2(LAST, 3, h)
                resid_a(LAST, 3, h, LAYERS)

            g.tensor_scalar(r_sc[:, :], r_raw[:, :], col[:, C_GAMMA:C_GAMMA + 1], 0.0, ALU.mult, ALU.add).then_inc(r_prep, 1)
            pool.wait_ge(r_prep, 1)
            g.tensor_scalar(r_hi[:, :], r_sc[:, :], 1.0, 0.0, ALU.mult, ALU.add).then_inc(r_prep, 1)
            pool.wait_ge(r_prep, 2)
            g.tensor_tensor(r_lo[:, :], r_sc[:, :], r_hi[:, :].bitcast(F32), ALU.subtract).then_inc(r_prep, 1)
            wait_apart(pool, bias_mm, LAYERS * 8, pool_passed)
            g.tensor_scalar(boff[:, :], ones[:, :], col[:, C_BETA:C_BETA + 1], 0.0, ALU.mult, ALU.add).then_inc(r_prep, 1)

            def prep_expert(e):
                dst = w1_set[e % 2]
                wait_apart(pool, raw_in, 32 * LAYERS + 16 * (e + 1), pool_passed)
                wait_apart(pool, w1_split, LAYERS * 8, pool_passed)
                wait_apart(pool, e_split, 2 * e, pool_passed)
                g.tensor_scalar(scaled_w1[:, :], raw_w1[:, :], col[:, C_GAMMA:C_GAMMA + 1], 0.0,
                                ALU.mult, ALU.add).then_inc(e_scaled, 1)
                wait_apart(pool, e_scaled, e + 1, pool_passed)
                if e == 0:
                    wait_apart(pool, w1_in, LAYERS * 16, pool_passed)
                elif e == 1:
                    wait_apart(pool, w1_mm, upto(LAST, SLOTS - 1, 1, per=FF), pool_passed)
                else:
                    wait_apart(pool, up_mm, FF * HALVES * (e - 1), pool_passed)
                g.tensor_scalar(dst[:, 0, :], scaled_w1[:, :], 1.0, 0.0, ALU.mult, ALU.add).then_inc(e_split, 1)
                wait_apart(pool, e_split, 2 * e + 1, pool_passed)
                g.tensor_tensor(dst[:, 1, :], scaled_w1[:, :], dst[:, 0, :].bitcast(F32),
                                ALU.subtract).then_inc(e_split, 1)

            prep_expert(0)
            for k in range(3 * HALVES):
                i = k % 2
                pool.wait_ge(f_mv, k + 1)
                g.tensor_scalar(var[i][:, :], mv[i][:, :, 1], 1.0, EPS, ALU.mult, ALU.add).then_inc(f_var, 1)
                pool.wait_ge(f_var, k + 1)
                g.tensor_tensor(rstd[i][:, :], var[i][:, :], neg_half[:, :], ALU.pow).then_inc(f_rstd, 1)
            for e in range(1, EXPERTS):
                prep_expert(e)

        @block.scalar
        def _(act):
            a = nc.scalar

            def phi_q(l, s, h):
                if s == 0 and h == 0:
                    wait(act, bias_done, l * 8 + 8)
                wait(act, q_mm, upto(l, s, h))
                wait_apart(act, qt_done, upto(l, s - 1, h), act_passed)
                a.activation(eq[h][:, :], ps(3 * h), ACT.Relu, bias=bq_neg[:, bass.ds(l, 1)], scale=-1.0).then_inc(q_rel, 1)
                wait(act, q_rel, upto(l, s, h))
                a.activation(eq[h][:, :], eq[h][:, :], ACT.Exp, scale=-1.0).then_inc(q_exp, 1)

            def phi_k(l, s, h):
                wait(act, kt_done, upto(l, s, h))
                wait(act, k_done, upto(l, s - 1, h))
                a.activation(ek[h][:, :, :], kt[h][:, :, :], ACT.Relu, scale=-1.0).then_inc(k_rel, 1)
                wait(act, k_rel, upto(l, s, h))
                a.activation(ek[h][:, :, :], ek[h][:, :, :], ACT.Exp, scale=-1.0).then_inc(k_exp, 1)

            def split_x1(l, s, h):
                wait(act, t1_mm, upto(l, s, h))
                wait(act, w1_mm, upto(l, s - 1, h, per=FF))
                a.activation(x1_hi[h][:, :], ps(7 if h == 0 else 0), ACT.Copy).then_inc(x1_hi_done, 1)

            def gelu(l, s, h, lw):
                for c in range(FF):
                    if c == 0:
                        wait(act, w2_mm, upto(l, s - 1, h))
                    wait_apart(act, w1_mm, upto(l, s, h, per=FF) - (FF - 1 - c), act_passed)
                    a.activation(hid[h][:, c, :], ps(3 + h + c), ACT.Gelu,
                                 bias=col[:, bass.ds(lw * FF + (C_C1 + c), 1)]).then_inc(hid_done, 1)

            def copy_att(l, s, h):
                wait(act, attt_mm, upto(l, s, h))
                wait(act, wo_mm, upto(l, s - 1, h))
                a.activation(att_t[h][:, :], ps(2 * h), ACT.Copy).then_inc(attt_sb, 1)

            def split_xt(l, s, h):
                u = (2 * s + h) % HALVES
                wait(act, t2_mm, upto(l, s, h, base=8))
                wait(act, kvp_mm, upto(l, s, h))
                a.activation(xt_hi[:, u], ps(4 + h), ACT.Copy).then_inc(xt_hi_done, 1)

            for s in range(SLOTS):
                for h in two:
                    split_xt(-1, s, h)

            def slot(l, s, first, last):
                p1, p2 = not first or s >= 1, not first or s >= 2
                lw = l if s >= 1 else l - 1
                for h in two:
                    phi_q(l, s, h)
                    phi_k(l, s, h)
                if p1:
                    split_x1(l, s - 1, 0)
                    split_x1(l, s - 1, 1)
                    gelu(l, s - 1, 0, lw)
                    gelu(l, s - 1, 1, lw)
                copy_att(l, s, 0)
                copy_att(l, s, 1)
                if p2 and not (last and s >= 2):
                    split_xt(l, s - 2, 0)
                    split_xt(l, s - 2, 1)

            for s in range(SLOTS):
                slot(0, s, True, False)
            with act.Fori(1, LAST) as l:
                for s in range(SLOTS):
                    slot(l, s, False, False)
            for s in range(SLOTS):
                slot(LAST, s, False, True)
            split_x1(LAST, 3, 0)
            split_x1(LAST, 3, 1)
            gelu(LAST, 3, 0, LAST)
            gelu(LAST, 3, 1, LAST)

            for u in range(HALVES):
                act.wait_ge(ft_mm, u + 1)
                if u == 0:
                    wait(act, kvp_mm, upto(LAST, SLOTS - 1, 1))
                a.activation(xt_hi[:, u], ps(4 + u % 2), ACT.Copy).then_inc(xn_hi, 1)
                act.wait_ge(r_sub, u + 1)
                a.activation(ex[:, :, :], ex[:, :, :], ACT.Exp, scale=INV_TEMP).then_inc(r_ex, 1)

            def silu(e, first=False):
                wait(act, eb_done, e + 1)
                for u in range(HALVES):
                    for c in range(FF):
                        if c == 0:
                            wait(act, down_mm, e * HALVES + (u - 1))
                            if first and u < 2:
                                wait(act, w2_mm, upto(LAST, 3, 1))
                        wait_apart(act, up_mm, e * (FF * HALVES) + (FF * u + c + 1), act_passed)
                        a.activation(hid[u % 2][:, c, :], ps(c), ACT.Silu,
                                     bias=e_bias[:, bass.ds(e, 1), c]).then_inc(up_done, 1)

            silu(0, first=True)
            with act.Fori(1, EXPERTS) as e:
                silu(e)

        @block.vector
        def _(dve):
            d = nc.vector

            def norm(i, src, dst, stats, mvs, rstds, done, count, war=(), summed=None):
                def moments():
                    if summed is not None:
                        wait(dve, *summed)
                    for t in range(T):
                        ins = d.bn_stats(stat[i][:, t, :], src[:, t, :])
                    ins.then_inc(stats, 1)
                    wait_apart(dve, stats, count, dve_passed)
                    for t in range(T):
                        ins = d.bn_aggr(mv[i][:, t, :], stat[i][:, t, :])
                    ins.then_inc(mvs, 1)

                def scale():
                    wait(dve, rstds, count)
                    for sm, value in war:
                        wait(dve, sm, value)
                    for t in range(T):
                        ins = d.tensor_scalar(dst[:, t, :], src[:, t, :], mv[i][:, t, 0:1], rstd[i][:, t:t + 1],
                                              ALU.subtract, ALU.mult)
                    ins.then_inc(done, 1)
                return moments, scale

            def keys_values(l, s, h):
                wait(dve, kvp_mm, upto(l, s, h))
                wait(dve, kvm_mm, upto(l, s - 1, h))
                for half in two:
                    b = (1, 4)[h] + half
                    src = ps(b).rearrange("p (t n) -> p t n", t=2)
                    bias = row[:, bass.ds(l * 2 + R_BKV, 2), :]
                    ins = d.tensor_tensor(kt[h][:, 2 * half:2 * half + 2, :], src[:, :, 0:P],
                                          bias[:, 0:1, :].to_broadcast([P, 2, P]), ALU.add)
                ins.then_inc(kt_done, 1)
                for half in two:
                    b = (1, 4)[h] + half
                    src = ps(b).rearrange("p (t n) -> p t n", t=2)
                    bias = row[:, bass.ds(l * 2 + R_BKV, 2), :]
                    ins = d.tensor_tensor(v[h][:, 2 * half:2 * half + 2, 0:P], src[:, :, P:2 * P],
                                          bias[:, 1:2, :].to_broadcast([P, 2, P]), ALU.add)
                ins.then_inc(v_done, 1)

            def queries(l, s, h):
                wait(dve, q_exp, upto(l, s, h))
                wait(dve, att_mm, upto(l, s - 1, h))
                d.scalar_tensor_tensor(out=qt[h][:, :], in0=ps(3 * h), scalar=bq_one[:, bass.ds(l, 1)],
                                       in1=eq[h][:, :], op0=ALU.add, op1=ALU.max).then_inc(qt_done, 1)

            def keys(l, s, h):
                wait(dve, k_exp, upto(l, s, h))
                d.scalar_tensor_tensor(out=kt[h][:, :, :], in0=kt[h][:, :, :], scalar=1.0,
                                       in1=ek[h][:, :, :], op0=ALU.add, op1=ALU.max).then_inc(k_done, 1)

            def mask_kv(l, s, h):
                wait(dve, kvm_mm, upto(l, s, h))
                wait(dve, att_mm, upto(l, s - 1, h))
                src = ps(1 + h).rearrange("p (q n) -> p q n", q=2)
                d.tensor_tensor(kv[h][:, :, 0:P], src[:, :, 0:P],
                                mask[:, 0:P].unsqueeze(1).to_broadcast([P, 2, P]), ALU.mult)
                for q in two:
                    ins = d.tensor_scalar(kv[h][:, q, P:KVW], mask[:, P:KVW], src[:, q, P:P + 1], None, ALU.mult)
                ins.then_inc(kv_done, 1)

            def attend(l, s, h):
                wait(dve, att_mm, upto(l, s, h))
                wait(dve, attt_mm, upto(l, s - 1, h))
                src = bank[h][:, :, 0:2 * KVW].rearrange("p b (t n) -> p b t n", t=2)
                d.tensor_scalar(den[h][:, :, :].rearrange("p (b t) c -> p b t c", b=2), src[:, :, :, P:KVW], DEN_EPS, None,
                                ALU.add).then_inc(den_done, 1)
                wait(dve, den_done, upto(l, s, h))
                d.reciprocal(rec[h][:, :, :], den[h][:, :, :]).then_inc(rec_done, 1)
                wait(dve, rec_done, upto(l, s, h))
                for b in two:
                    ins = d.tensor_tensor(
                        att[h][:, 2 * b:2 * b + 2, :].rearrange("p t (a c) -> p t a c", c=HEAD),
                        src[:, b, :, 0:P].rearrange("p t (a c) -> p t a c", c=HEAD),
                        rec[h][:, 2 * b:2 * b + 2, :].unsqueeze(3).to_broadcast([P, 2, HEADS, HEAD]), ALU.mult)
                ins.then_inc(att_done, 1)

            def add_res1(l, s, h):
                u = (2 * s + h) % HALVES
                wait(dve, wo_mm, upto(l, s, h))
                wait(dve, resa_done, upto(l, s, h))
                wait(dve, t1_mm, upto(l, s - 1, h))
                wait(dve, resf_done, upto(l, s - 1, h))
                d.tensor_tensor(s1[h][:, :, :], ps(7 - h).rearrange("p (t n) -> p t n", t=T), res_a[:, u],
                                ALU.add).then_inc(s1_done, 1)

            def norm1(l, s, h):
                return norm(h, s1[h], s1[h], stat1_done, mv1_done, rstd1_done, x1_done, upto(l, s, h),
                            summed=(s1_done, upto(l, s, h)))

            def lo_x1(l, s, h):
                wait(dve, x1_hi_done, upto(l, s, h))
                wait(dve, w1_mm, upto(l, s - 1, h, per=FF))
                d.tensor_tensor(x1_lo[h][:, :], ps(7 if h == 0 else 0), x1_hi[h][:, :].bitcast(F32),
                                ALU.subtract).then_inc(x1_lo_done, 1)

            def add_res2(l, s, h, lastl=False):
                wait(dve, w2_mm, upto(l, s, h))
                wait(dve, resf_done, upto(l, s, h))
                if not (lastl and s >= 1):
                    wait(dve, t2_mm, upto(l, s - 1, h, base=8))
                wait(dve, resa_done, upto(l, s - 1, h, base=8))
                d.tensor_tensor(s2[h][:, :, :], ps(3 if h == 0 else 6).rearrange("p (t n) -> p t n", t=T),
                                res_f[h][:, :, :], ALU.add).then_inc(s2_done, 1)

            def norm2(l, s, h):
                return norm(2 + h, s2[h], s2[h], stat2_done, mv2_done, rstd2_done, x2_done, upto(l, s, h, base=8),
                            summed=(s2_done, upto(l, s, h)))

            def lo_xt(l, s, h):
                u = (2 * s + h) % HALVES
                wait(dve, xt_hi_done, upto(l, s, h, base=8))
                d.tensor_tensor(xt_lo[:, u], ps(4 + h), xt_hi[:, u].bitcast(F32), ALU.subtract).then_inc(xt_lo_done, 1)

            def biases(l):
                wait(dve, bias_mm, l * 8 + 8)
                b = ps(1)
                kvb = row[:, bass.ds(l * 2 + R_BKV, 2), :]
                bq = col[:, bass.ds(l + C_BQ, 1)]
                c1 = col[:, bass.ds(l * FF + C_C1, FF)]
                d.tensor_tensor(kvb, b[:, 0:2 * P].rearrange("p (a b) -> p a b", a=2), kvb, ALU.add)
                d.scalar_tensor_tensor(out=bq_neg[:, bass.ds(l, 1)], in0=b[:, 256:257], scalar=-1.0, in1=bq,
                                       op0=ALU.mult, op1=ALU.subtract)
                d.scalar_tensor_tensor(out=bq_one[:, bass.ds(l, 1)], in0=b[:, 256:257], scalar=1.0, in1=bq,
                                       op0=ALU.add, op1=ALU.add)
                d.tensor_tensor(c1, b[:, 260:260 + FF], c1, ALU.add).then_inc(bias_done, 8)

            for s in range(SLOTS):
                both = []
                for h in two:
                    dve.wait_ge(x_in[2 * s + h], 16)
                    c = 2 * s + h + 1
                    both.append(norm(2 + h, x_all[:, 2 * s + h], s2[h], stat2_done, mv2_done, rstd2_done, x2_done, c,
                                     war=((t2_mm, c - 2), (resa_done, c - 2))))
                    both[h][0]()
                for h in two:
                    both[h][1]()
                if s == 0:
                    biases(0)
                for h in two:
                    lo_xt(-1, s, h)

            def slot(l, s, first, last):
                p1, p2 = not first or s >= 1, not first or s >= 2
                if s == 0:
                    wait(dve, bias_done, l * 8 + 8)
                n1 = [norm1(l, s - 1, h) for h in two]
                n2 = [norm2(l, s - 2, h) for h in two]
                if p1:
                    n1[0][0]()
                keys_values(l, s, 0)
                if p1:
                    n1[1][0]()
                queries(l, s, 0)
                if p1:
                    n1[0][1]()
                keys_values(l, s, 1)
                if p1:
                    n1[1][1]()
                keys(l, s, 0)
                queries(l, s, 1)
                keys(l, s, 1)
                if p2:
                    add_res2(l, s - 2, 1, last)
                if p1:
                    lo_x1(l, s - 1, 0)
                    lo_x1(l, s - 1, 1)
                if p2:
                    n2[0][0]()
                mask_kv(l, s, 0)
                mask_kv(l, s, 1)
                if p2:
                    n2[0][1]()
                    n2[1][0]()
                    n2[1][1]()
                attend(l, s, 0)
                attend(l, s, 1)
                if p2 and not (last and s >= 2):
                    lo_xt(l, s - 2, 0)
                    lo_xt(l, s - 2, 1)
                if s == 2 and not last:
                    biases(l + 1)
                if p1:
                    add_res2(l, s - 1, 0, last)
                add_res1(l, s, 0)
                add_res1(l, s, 1)

            for s in range(SLOTS):
                slot(0, s, True, False)
            with dve.Fori(1, LAST) as l:
                for s in range(SLOTS):
                    slot(l, s, False, False)
            for s in range(SLOTS):
                slot(LAST, s, False, True)
            n1 = [norm1(LAST, 3, h) for h in two]
            n2 = [norm2(LAST, 2, h) for h in two]
            n3 = [norm2(LAST, 3, h) for h in two]
            n1[0][0]()
            n1[1][0]()
            n1[0][1]()
            n1[1][1]()
            add_res2(LAST, 2, 1, True)
            lo_x1(LAST, 3, 0)
            lo_x1(LAST, 3, 1)
            n2[0][0]()
            n2[0][1]()
            n2[1][0]()
            n2[1][1]()
            for h in two:
                add_res2(LAST, 3, h, True)
                n3[h][0]()
                n3[h][1]()

            steps = [0]

            def link(ins):
                steps[0] += 1
                ins.then_inc(f_step, 1)
                dve.wait_ge(f_step, steps[0])

            norms = [0]

            def final_norm(src, dst):
                i = norms[0] % 2
                norms[0] += 1
                for t in range(T):
                    ins = d.bn_stats(stat[i][:, t, :], src[:, t, :])
                link(ins)
                for t in range(T):
                    ins = d.bn_aggr(mv[i][:, t, :], stat[i][:, t, :])
                ins.then_inc(f_mv, 1)
                dve.wait_ge(f_rstd, norms[0])
                for t in range(T):
                    ins = d.tensor_scalar(dst[:, t, :], src[:, t, :], mv[i][:, t, 0:1], rstd[i][:, t:t + 1],
                                          ALU.subtract, ALU.mult)
                return ins

            dve.wait_ge(rb_mm, 1)
            d.tensor_copy(r_bias[:, :], ps(7)[:, 0:EXPERTS]).then_inc(rb_done, 1)
            dve.wait_ge(rb_done, 1)
            for u in range(HALVES):
                b = u % 2
                wait(dve, resa_done, upto(LAST, 0, u, base=8))
                link(final_norm(res_a[:, u], s1[b]))
                link(d.tensor_tensor(s1[b][:, :, :], s1[b][:, :, :], row[:, R_GF:R_GF + 1, :].to_broadcast([P, T, P]), ALU.mult))
                link(d.tensor_tensor(s1[b][:, :, :], s1[b][:, :, :], row[:, R_BF:R_BF + 1, :].to_broadcast([P, T, P]), ALU.add))
                link(d.tensor_tensor(x_all[:, u], s1[b][:, :, :], x_all[:, u], ALU.add))
                link(final_norm(x_all[:, u], s1[b]))
                link(d.tensor_tensor(res_a[:, u], x_all[:, u], s1[b][:, :, :], ALU.add))
                if u >= 2:
                    dve.wait_ge(ft_mm, u - 1)
                final_norm(s1[b], s2[b]).then_inc(xn_done, 1)
                dve.wait_ge(xn_hi, u + 1)
                d.tensor_tensor(xt_lo[:, u], ps(4 + b), xt_hi[:, u].bitcast(F32), ALU.subtract).then_inc(xn_lo, 1)
                dve.wait_ge(r_mm, u + 1)
                link(d.tensor_tensor(ex[:, :, :], ps(7)[:, 0:T * EXPERTS].rearrange("p (t e) -> p t e", t=T),
                                     r_bias[:, :].unsqueeze(1).to_broadcast([P, T, EXPERTS]), ALU.add))
                link(d.tensor_reduce(mx[:, :], ex[:, :, :], AX.X, ALU.max))
                d.tensor_tensor(ex[:, :, :], ex[:, :, :], mx[:, :].unsqueeze(2).to_broadcast([P, T, EXPERTS]),
                                ALU.subtract).then_inc(r_sub, 1)
                dve.wait_ge(r_ex, u + 1)
                e_j = ex[:, :, :].unsqueeze(2).to_broadcast([P, T, EXPERTS, EXPERTS])
                e_e = ex[:, :, :].unsqueeze(3).to_broadcast([P, T, EXPERTS, EXPERTS])
                d.tensor_tensor(gt[:, :, :, :], e_j, e_e, ALU.is_gt)
                link(d.tensor_tensor(ge[:, :, :, :], e_j, e_e, ALU.is_equal))
                link(d.tensor_tensor(ge[:, :, :, :].rearrange("p t a b -> p t (a b)"),
                                     ge[:, :, :, :].rearrange("p t a b -> p t (a b)"),
                                     tri[:, :, :].rearrange("p a b -> p (a b)").unsqueeze(1).to_broadcast([P, T, EXPERTS * EXPERTS]),
                                     ALU.mult))
                link(d.tensor_tensor(gt[:, :, :, :], gt[:, :, :, :], ge[:, :, :, :], ALU.add))
                d.tensor_reduce(rank[:, :, :], gt[:, :, :, :], AX.X, ALU.add)
                link(d.tensor_reduce(mx[:, :], ex[:, :, :], AX.X, ALU.add))
                link(d.reciprocal(mx[:, :], mx[:, :]))
                link(d.scalar_tensor_tensor(out=rank[:, :, :], in0=rank[:, :, :], scalar=2.0, in1=ex[:, :, :],
                                            op0=ALU.is_lt, op1=ALU.mult))
                d.tensor_tensor(gate[:, :, T * u:T * u + T].rearrange("p e t -> p t e"), rank[:, :, :],
                                mx[:, :].unsqueeze(2).to_broadcast([P, T, EXPERTS]), ALU.mult).then_inc(gate_done, 1)

            dve.wait_ge(gate_done, HALVES)
            with dve.Fori(0, EXPERTS) as e:
                wait(dve, eb_mm, e + 1)
                d.tensor_copy(e_bias[:, bass.ds(e, 1), :], ps(6)[:, 0:FF].unsqueeze(1)).then_inc(eb_done, 1)
                for u in range(HALVES):
                    wait(dve, down_mm, e * HALVES + (u + 1))
                    for t in range(T):
                        ins = d.scalar_tensor_tensor(
                            out=res_a[:, u, t, :], in0=ps(4 + u % 2)[:, t * P:(t + 1) * P],
                            scalar=gate[:, bass.ds(e, 1), T * u + t], in1=res_a[:, u, t, :],
                            op0=ALU.mult, op1=ALU.add)
                    ins.then_inc(comb, 1)
                wait(dve, comb, e * HALVES + HALVES)

        @block.tensor
        def _(pe):
            t_ = nc.tensor

            def three(out_, a_hi, a_lo, b_hi, b_lo):
                t_.matmul(out_, a_hi, b_hi, start=True, stop=False)
                t_.matmul(out_, a_hi, b_lo, start=False, stop=False)
                return t_.matmul(out_, a_lo, b_hi, start=False, stop=True)

            def project(l, s, h, first, last):
                u = (2 * s + h) % HALVES
                if s == 0 and h == 0:
                    wait(pe, qkv_in, l * 16 + 16)
                wait(pe, xt_lo_done, upto(l, s, h))
                if h == 1:
                    wait(pe, s2_done, upto(l, s - 2, 0))
                three(ps(3 * h), this_qkv[:, 0, 0:P], this_qkv[:, 1, 0:P], xt_hi[:, u], xt_lo[:, u]).then_inc(q_mm, 1)
                if h == 1 and not (last and s == 3):
                    wait(pe, xt_lo_done, HALVES if first and s < 3 else upto(l, s - 3, 1, base=8))
                elif h == 0 and ((s == 3 and not last) or (first and s == 0)):
                    wait(pe, bias_done, l * 8 + (16 if s == 3 else 8))
                for t in range(T):
                    b = ps((1, 4)[h] + t // 2)[:, (t % 2) * 256:(t % 2) * 256 + 256]
                    tile = slice(t * P, (t + 1) * P)
                    ins = three(b, xt_hi[:, u, tile], xt_lo[:, u, tile], this_qkv[:, 0, P:QKV], this_qkv[:, 1, P:QKV])
                ins.then_inc(kvp_mm, 1)

            def key_value(l, s, h):
                wait(pe, k_done, upto(l, s, h))
                wait(pe, v_done, upto(l, s, h))
                for q in two:
                    for t in two:
                        ins = t_.matmul(ps(1 + h)[:, q * 256:q * 256 + P + 1], kt[h][:, 2 * q + t, :],
                                        v[h][:, 2 * q + t, 0:P + 1], start=t == 0, stop=t == 1)
                ins.then_inc(kvm_mm, 1)

            def attention(l, s, h, first):
                wait(pe, kv_done, upto(l, s, h))
                wait(pe, qt_done, upto(l, s, h))
                if h == 0:
                    wait(pe, x1_lo_done, upto(l, s - 1, 1))
                else:
                    wait(pe, hid_done, upto(l, s - 1, 0, per=FF) - 3)
                for t in range(T):
                    ins = t_.matmul(bank[h][:, t // 2, (t % 2) * KVW:(t % 2 + 1) * KVW], qt[h][:, t * P:(t + 1) * P],
                                    kv[h][:, t // 2, :], start=True, stop=True)
                ins.then_inc(att_mm, 1)

            def flip(b, src):
                for t in range(T):
                    ins = t_.transpose(ps(b)[:, t * P:(t + 1) * P], src[:, t, :], ident[:, :])
                return ins

            def flip_att(l, s, h):
                wait(pe, att_done, upto(l, s, h))
                flip(2 * h, att[h]).then_inc(attt_mm, 1)

            def out_proj(l, s, h):
                if s == 0 and h == 0:
                    wait(pe, wo_in, l * 16 + 16)
                wait(pe, attt_sb, upto(l, s, h))
                wait(pe, hid_done, upto(l, s - 1, 1, per=FF) - h)
                for t in range(T):
                    ins = t_.matmul(ps(7 - h)[:, t * P:(t + 1) * P], att_t[h][:, t * P:(t + 1) * P], this_wo[:, :],
                                    start=True, stop=True)
                ins.then_inc(wo_mm, 1)

            def flip_x1(l, s, h, tail=False):
                wait(pe, x1_done, upto(l, s, h))
                if h == 1 and not tail:
                    wait(pe, qt_done, upto(l, s + 1, 0))
                flip(7 if h == 0 else 0, s1[h]).then_inc(t1_mm, 1)

            def ff_up(l, s, h, lw, tail=False):
                if s % SLOTS == 0 and h == 0:
                    wait(pe, w1_in, lw * 16 + 16)
                wait(pe, x1_lo_done, upto(l, s, h))
                if h == 0:
                    wait(pe, s2_done, upto(l, s - 1, 1))
                for c in range(FF):
                    chunk = slice(c * P, (c + 1) * P)
                    if h == 1 and c < 3:
                        wait(pe, hid_done, upto(l, s, 0, per=FF) - 2 + c)
                    three(ps(3 + h + c), this_w1[:, 0, chunk], this_w1[:, 1, chunk], x1_hi[h][:, :], x1_lo[h][:, :]
                          ).then_inc(w1_mm, 1)

            def ff_down(l, s, h, lw):
                if s % SLOTS == 0 and h == 0:
                    wait(pe, w2_in, lw * 16 + 16)
                wait(pe, hid_done, upto(l, s, h, per=FF))
                if h == 1:
                    wait(pe, s1_done, upto(l, s + 1, 1) if not (isinstance(l, int) and l == LAST and s == 3)
                         else upto(l, s, 1))
                for t in range(T):
                    for c in range(FF):
                        ins = t_.matmul(ps(3 if h == 0 else 6)[:, t * P:(t + 1) * P], hid[h][:, c, t * P:(t + 1) * P],
                                        this_w2[:, c, :], start=c == 0, stop=c == FF - 1)
                ins.then_inc(w2_mm, 1)

            def flip_x2(l, s, h):
                wait(pe, x2_done, upto(l, s, h, base=8))
                if isinstance(l, int) and l == -1:
                    wait(pe, xt_lo_done, upto(l, s - 1, h, base=8))
                else:
                    wait(pe, hid_done, upto(l, s + 1, 1, per=FF) - 3 + h)
                flip(4 + h, s2[h]).then_inc(t2_mm, 1)

            def bias_products(l):
                wait(pe, raw_in, l * 32 + 32)
                wait(pe, boff_done, l * 8 + 8)
                b = ps(1)
                t_.matmul(b[:, 0:2 * P], boff[:, :], raw_qkv[:, P:QKV], start=True, stop=True)
                t_.matmul(b[:, 256:257], raw_qkv[:, 0:P], col[:, bass.ds(l + C_BIN, 1)], start=True, stop=True)
                for c in range(FF):
                    ins = t_.matmul(b[:, 260 + c:261 + c], raw_w1[:, c * P:(c + 1) * P], col[:, bass.ds(l + C_B1, 1)],
                                    start=True, stop=True)
                ins.then_inc(bias_mm, 8)

            pe.wait_ge(const_done, 1)
            for s in range(SLOTS):
                for h in two:
                    flip_x2(-1, s, h)
                if s == 0:
                    bias_products(0)

            def slot(l, s, first, last):
                p1, p2 = not first or s >= 1, not first or s >= 2
                lw1 = l if s >= 1 else l - 1
                lw2 = l if s >= 2 else l - 1
                project(l, s, 0, first, last)
                project(l, s, 1, first, last)
                if p2:
                    ff_down(l, s - 2, 1, lw2)
                if p1:
                    flip_x1(l, s - 1, 0)
                    flip_x1(l, s - 1, 1)
                key_value(l, s, 0)
                key_value(l, s, 1)
                if p1:
                    ff_up(l, s - 1, 0, lw1)
                attention(l, s, 0, first)
                attention(l, s, 1, first)
                if p1:
                    ff_up(l, s - 1, 1, lw1)
                flip_att(l, s, 0)
                flip_att(l, s, 1)
                if p2 and not (last and s >= 2):
                    flip_x2(l, s - 2, 0)
                    flip_x2(l, s - 2, 1)
                if s == 2 and not last:
                    bias_products(l + 1)
                if p1:
                    ff_down(l, s - 1, 0, lw1)
                out_proj(l, s, 0)
                out_proj(l, s, 1)

            for s in range(SLOTS):
                slot(0, s, True, False)
            with pe.Fori(1, LAST) as l:
                for s in range(SLOTS):
                    slot(l, s, False, False)
            for s in range(SLOTS):
                slot(LAST, s, False, True)
            ff_down(LAST, 2, 1, LAST)
            flip_x1(LAST, 3, 0, tail=True)
            flip_x1(LAST, 3, 1, tail=True)
            ff_up(LAST, 3, 0, LAST)
            ff_up(LAST, 3, 1, LAST)
            ff_down(LAST, 3, 0, LAST)
            ff_down(LAST, 3, 1, LAST)

            pe.wait_ge(r_prep, 4)
            t_.matmul(ps(7)[:, 0:EXPERTS], boff[:, :], r_raw[:, :], start=True, stop=True).then_inc(rb_mm, 1)
            for u in range(HALVES):
                pe.wait_ge(xn_done, u + 1)
                if u >= 2:
                    pe.wait_ge(xn_lo, u - 1)
                flip(4 + u % 2, s2[u % 2]).then_inc(ft_mm, 1)
                pe.wait_ge(xn_lo, u + 1)
                pe.wait_ge(rb_done, 1)
                if u >= 1:
                    pe.wait_ge(r_sub, u)
                for t in range(T):
                    tile = slice(t * P, (t + 1) * P)
                    ins = three(ps(7)[:, t * EXPERTS:(t + 1) * EXPERTS], xt_hi[:, u, tile], xt_lo[:, u, tile],
                                r_hi[:, :], r_lo[:, :])
                ins.then_inc(r_mm, 1)

            def expert_bias(e, k):
                wait(pe, raw_in, 32 * LAYERS + (e * 16 + 16))
                wait(pe, eb_done, e)
                for c in range(FF):
                    ins = t_.matmul(ps(6)[:, c:c + 1], raw_w1[:, c * P:(c + 1) * P], col[:, C_BETA:C_BETA + 1],
                                    start=True, stop=True)
                ins.then_inc(eb_mm, 1)

            def up(e, k, u):
                w = w1_set[k]
                if u == 0:
                    wait(pe, e_split, e * 2 + 2)
                for c in range(FF):
                    chunk = slice(c * P, (c + 1) * P)
                    wait(pe, up_done, e * (FF * HALVES) + (FF * (u - 1) + c + 1))
                    three(ps(c), w[:, 0, chunk], w[:, 1, chunk], xt_hi[:, u], xt_lo[:, u]).then_inc(up_mm, 1)

            def down(e, k, u):
                if u == 0:
                    wait(pe, w2e_in[k], e * 8 + (16 if k == 0 else 8))
                wait(pe, up_done, e * (FF * HALVES) + FF * (u + 1))
                wait(pe, comb, e * HALVES + (u - 1))
                for t in range(T):
                    for c in range(FF):
                        ins = t_.matmul(ps(4 + u % 2)[:, t * P:(t + 1) * P], hid[u % 2][:, c, t * P:(t + 1) * P],
                                        w2_set[k][:, c, :], start=c == 0, stop=c == FF - 1)
                ins.then_inc(down_mm, 1)

            def expert(e, k, first=False):
                expert_bias(e, k)
                for u in range(HALVES):
                    up(e, k, u)
                    if u >= 1:
                        down(e, k, u - 1)
                    elif not first:
                        down(e - 1, 1 - k, HALVES - 1)

            pe.wait_ge(gate_done, HALVES)
            expert(0, 0, first=True)
            expert(1, 1)
            with pe.Fori(2, EXPERTS, 2) as e:
                expert(e, 0)
                expert(e + 1, 1)
            down(EXPERTS - 1, 1, HALVES - 1)


def kernel(**inputs):
    import concourse.bacc as _bacc
    from concourse.bass_utils import run_bass_kernel_spmd as _run

    a = {k: np.ascontiguousarray(np.asarray(v)) for k, v in inputs.items()}
    ones, zeros = np.ones((1, P), np.float32), np.zeros((1, P), np.float32)
    A = "L0_attn_"

    def halves(y):
        return np.ascontiguousarray(y.reshape(HALVES, T, P, P).transpose(0, 2, 1, 3))

    gin, bin_ = np.concatenate([ones, a[A + "g2"]]), np.concatenate([zeros, a[A + "be2"]])
    rows = np.concatenate([gin, bin_, a[A + "g1"], a[A + "be1"],
                           np.stack([a[A + "bk"], a[A + "bv"]], 1).reshape(2 * LAYERS, P),
                           a[A + "gf"][None], a[A + "bef"][None]]).reshape(-1)
    rows2 = np.concatenate([a[A + "bo"], zeros, a[A + "c2"]]).reshape(-1)
    cols = np.concatenate([gin[:LAYERS], bin_[:LAYERS], a[A + "g1"], a[A + "be1"], a[A + "bq"],
                           a[A + "c1"].reshape(LAYERS * FF, P), a["L0_ffn_gamma"][None], a["L0_ffn_beta"][None]]).T
    arrays = {
        "x": halves(a[A + "x"].reshape(-1, P)),
        "rows": rows,
        "rows2": rows2,
        "cols": cols,
        "wqkv": np.concatenate([a[A + "Wq"], a[A + "Wk"], a[A + "Wv"]], axis=2),
        "wo": a[A + "Wo"],
        "w1": np.concatenate([a[A + "W1"], a["L0_ffn_W1"]]),
        "w2": np.concatenate([a[A + "W2"], a["L0_ffn_W2"]]),
        "router": a["L0_ffn_router_w"].T,
    }
    arrays = {k: np.ascontiguousarray(v) for k, v in arrays.items()}
    nc = _bacc.Bacc("TRN2", target_bir_lowering=False, num_devices=1)
    args = [nc.dram_tensor(k, v.shape, mybir.dt.from_np(v.dtype), kind="ExternalInput").ap() for k, v in arrays.items()]
    out = nc.dram_tensor("out", (HALVES, P, T, P), F32, kind="ExternalOutput").ap()
    build(nc, *args, out)
    r = _run(nc, [arrays], core_ids=[0])
    got = r.results[0]["out"]
    return np.ascontiguousarray(got.transpose(0, 2, 1, 3)).reshape(16, 256, P)
```

```python
from contextlib import ExitStack

import numpy as np

import concourse.bass as bass
from concourse import mybir

F32 = mybir.dt.float32
F32R = mybir.dt.float32r
ALU = mybir.AluOpType
ACT = mybir.ActivationFunctionType
AX = mybir.AxisListType

P = 128
LAYERS = 8
EXPERTS = 8
HEADS, HEAD = 16, 8
FF = 4
HALVES = 8
T = 4
N = T * P
SLOTS = HALVES // 2
QKV = 3 * P
NORMS = 10
EPS = 1e-5
DEN_EPS = 1e-6
INV_TEMP = 1.0 / 1.5
KVW = P + HEADS
VW = P + 2

C_GIN, C_BIN = 0, 8
C_G1, C_B1 = 16, 24
C_BQ = 32
C_C1 = 40
C_GAMMA, C_BETA = 72, 73
C_END = 74
ROWS = 8
R_GIN, R_BIN, R_BO = 0, 1, 2
R_G1, R_B1, R_C2 = 3, 4, 5
R_BK = 6


def wait(eng, sem, count):
    if not isinstance(count, int) or count > 0:
        eng.wait_ge(sem, count)


def wait_apart(eng, sem, count, passed):
    wait(eng, sem, count)
    if not isinstance(count, int):
        eng.sem_inc(passed, 1)


def upto(l, s, h, per=1, base=0):
    return l * (HALVES * per) + per * (2 * s + h + 1 + base)


def build(nc, x, rows, cols, wqkv, wo, w1, w2, router, out):
    ctx = ExitStack()
    with ctx:
        def sb(name, shape, dt=F32):
            return ctx.enter_context(nc.sbuf_tensor(name, shape, dt))

        def sem(name):
            return ctx.enter_context(nc.semaphore(name))

        bank = [ctx.enter_context(nc.psum_tensor("ps01", [P, 2, 512], F32)),
                ctx.enter_context(nc.psum_tensor("ps23", [P, 2, 512], F32)),
                ctx.enter_context(nc.psum_tensor("ps45", [P, 2, 512], F32)),
                ctx.enter_context(nc.psum_tensor("ps67", [P, 2, 512], F32))]

        def ps(b):
            return bank[b // 2][:, b % 2, :]

        x_all = sb("x_all", [P, HALVES, T, P])
        res_a = sb("res_a", [P, HALVES, T, P])
        xt_hi = sb("xt_hi", [P, HALVES, N], F32R)
        xt_lo = sb("xt_lo", [P, HALVES, N], F32R)
        ident = sb("ident", [P, P])
        mask = sb("mask", [P, KVW])
        neg_half = sb("neg_half", [P, T])
        ones = sb("ones", [P, P])
        warm = sb("warm", [P, 2])
        tri = sb("tri", [P, EXPERTS, EXPERTS])
        row = sb("row", [P, LAYERS + 1, ROWS, P])
        col = sb("col", [P, C_END])
        bq_neg = sb("bq_neg", [P, LAYERS])
        bq_one = sb("bq_one", [P, LAYERS])
        raw_qkv = sb("raw_qkv", [P, QKV])
        raw_w1 = sb("raw_w1", [P, N])
        scaled_qkv = sb("scaled_qkv", [P, QKV])
        scaled_w1 = sb("scaled_w1", [P, N])
        next_qkv = sb("next_qkv", [P, 2, QKV], F32R)
        this_qkv = sb("this_qkv", [P, 2, QKV], F32R)
        next_w1 = sb("next_w1", [P, 2, N], F32R)
        this_w1 = sb("this_w1", [P, 2, N], F32R)
        this_wo = sb("this_wo", [P, P])
        this_w2 = sb("this_w2", [P, FF, P])
        other_w2 = sb("other_w2", [P, FF, P])
        gain = sb("gain", [P, 2])
        gain1 = sb("gain1", [P, 1])
        boff = sb("boff", [P, P])
        two = range(2)
        eq = [sb(f"eq{h}", [P, N]) for h in two]
        qt = [sb(f"qt{h}", [P, N]) for h in two]
        kt = [sb(f"kt{h}", [P, T, P]) for h in two]
        ek = [sb(f"ek{h}", [P, T, P]) for h in two]
        v = [sb(f"v{h}", [P, T, VW]) for h in two]
        kv = [sb(f"kv{h}", [P, 2, KVW]) for h in two]
        den = [sb(f"den{h}", [P, T, HEADS]) for h in two]
        rec = [sb(f"rec{h}", [P, T, HEADS]) for h in two]
        att = [sb(f"att{h}", [P, T, P]) for h in two]
        att_t = [sb(f"att_t{h}", [P, N]) for h in two]
        s1 = [sb(f"s1{h}", [P, T, P]) for h in two]
        s2 = [sb(f"s2{h}", [P, T, P]) for h in two]
        x1_hi = [sb(f"x1_hi{h}", [P, N], F32R) for h in two]
        x1_lo = [sb(f"x1_lo{h}", [P, N], F32R) for h in two]
        res_f = [sb(f"res_f{h}", [P, T, P]) for h in two]
        hid = [sb(f"hid{h}", [P, FF, N]) for h in two]
        stat = [sb(f"stat{i}", [P, T, 6]) for i in range(NORMS)]
        mv = [sb(f"mv{i}", [P, T, 2]) for i in range(NORMS)]
        var = [sb(f"var{i}", [P, T]) for i in range(NORMS)]
        rstd = [sb(f"rstd{i}", [P, T]) for i in range(NORMS)]
        shift = [sb(f"shift{i}", [P, T]) for i in range(NORMS)]
        r_raw = sb("r_raw", [P, EXPERTS])
        r_sc = sb("r_sc", [P, EXPERTS])
        r_hi = sb("r_hi", [P, EXPERTS], F32R)
        r_lo = sb("r_lo", [P, EXPERTS], F32R)
        r_bias = sb("r_bias", [P, EXPERTS])
        ex = sb("ex", [P, T, EXPERTS])
        mx = sb("mx", [P, T])
        gt = sb("gt", [P, T, EXPERTS, EXPERTS])
        ge = sb("ge", [P, T, EXPERTS, EXPERTS])
        rank = sb("rank", [P, T, EXPERTS])
        gate = sb("gate", [P, EXPERTS, HALVES * T])
        e_bias = sb("e_bias", [P, EXPERTS, FF])

        x_in = [sem(f"x_in{u}") for u in range(HALVES)]
        col_in, row_in, router_in = sem("col_in"), sem("row_in"), sem("router_in")
        raw_in = sem("raw_in")
        qkv_in, wo_in, w1_in, w2_in = sem("qkv_in"), sem("wo_in"), sem("w1_in"), sem("w2_in")
        out_done = sem("out_done")
        pool_passed, act_passed, dve_passed, sp_passed = (sem(n) for n in ("pool_passed", "act_passed", "dve_passed", "sp_passed"))
        const_step, const_done, rows_summed = sem("const_step"), sem("const_done"), sem("rows_summed")
        qkv_scaled, qkv_split = sem("qkv_scaled"), sem("qkv_split")
        w1_scaled, w1_split = sem("w1_scaled"), sem("w1_split")
        gain_done, gain1_done = sem("gain_done"), sem("gain1_done")
        boff_done, bias_mm, bias_done = sem("boff_done"), sem("bias_mm"), sem("bias_done")
        q_mm, kvp_mm, kvm_mm, att_mm, attt_mm = (sem(n) for n in ("q_mm", "kvp_mm", "kvm_mm", "att_mm", "attt_mm"))
        wo_mm, t1_mm, w1_mm, w2_mm, t2_mm = (sem(n) for n in ("wo_mm", "t1_mm", "w1_mm", "w2_mm", "t2_mm"))
        q_rel, q_exp, k_rel, k_exp, attt_sb = (sem(n) for n in ("q_rel", "q_exp", "k_rel", "k_exp", "attt_sb"))
        exp_table, gelu_table = sem("exp_table"), sem("gelu_table")
        x1_hi_done, hid_done, xt_hi_done = sem("x1_hi_done"), sem("hid_done"), sem("xt_hi_done")
        kt_done, v_done, qt_done, k_done, kv_done = (sem(n) for n in ("kt_done", "v_done", "qt_done", "k_done", "kv_done"))
        den_done, rec_done, att_done = sem("den_done"), sem("rec_done"), sem("att_done")
        s1_done, stat1_done, mv1_done, x1_done, x1_lo_done = (sem(n) for n in ("s1_done", "stat1_done", "mv1_done", "x1_done", "x1_lo_done"))
        s2_done, stat2_done, mv2_done, x2_done, xt_lo_done = (sem(n) for n in ("s2_done", "stat2_done", "mv2_done", "x2_done", "xt_lo_done"))
        var1_done, pow1_done, rstd1_done = sem("var1_done"), sem("pow1_done"), sem("rstd1_done")
        var2_done, pow2_done, rstd2_done = sem("var2_done"), sem("pow2_done"), sem("rstd2_done")
        resf_mul, resf_done, resa_mul, resa_done = (sem(n) for n in ("resf_mul", "resf_done", "resa_mul", "resa_done"))
        three_ = range(3)
        f_mv = [sem(f"f_mv{k}") for k in three_]
        f_var = [sem(f"f_var{k}") for k in three_]
        f_pow = [sem(f"f_pow{k}") for k in three_]
        f_rstd = [sem(f"f_rstd{k}") for k in three_]
        f_norm = [sem(f"f_norm{k}") for k in three_]
        f_stat, f_gain, f_offset, f_sum, acc_done = (sem(n) for n in ("f_stat", "f_gain", "f_offset", "f_sum", "acc_done"))
        ft_mm, xn_hi, xn_lo = sem("ft_mm"), sem("xn_hi"), sem("xn_lo")
        r_prep, rb_mm, rb_done, r_mm, r_sub, r_ex, r_step, gate_done = (
            sem(n) for n in ("r_prep", "rb_mm", "rb_done", "r_mm", "r_sub", "r_ex", "r_step", "gate_done"))
        e_scaled, e_split, eb_mm, eb_done = sem("e_scaled"), sem("e_split"), sem("eb_mm"), sem("eb_done")
        w2e_in = [sem(f"w2e_in{k}") for k in two]
        up_mm = [sem(f"up_mm{k}") for k in two]
        up_done = [sem(f"up_done{k}") for k in two]
        down_mm = [sem(f"down_mm{k}") for k in two]
        comb = [sem(f"comb{k}") for k in two]

        def first_norm(u):
            return hid[u % 2][:, u // 2, :].rearrange("p (t n) -> p t n", t=T)

        LAST = LAYERS - 1
        w1_set = [next_w1, this_w1]
        w2_set = [other_w2, this_w2]

        START_BANK = (4, 5, 6, 7, 6, 7, 4, 5)

        block = ctx.enter_context(nc.Block())

        @block.sync
        def _(sp):
            def load_raw(l):
                if not isinstance(l, int) or l > 0:
                    wait_apart(sp, qkv_scaled, l * 8, sp_passed)
                    wait_apart(sp, w1_scaled, l * 8, sp_passed)
                    wait_apart(sp, bias_mm, l * 8, sp_passed)
                sp.dma_start(raw_qkv[:, :], wqkv[bass.ds(l, 1)].rearrange("l p n -> (l p) n")).then_inc(raw_in, 16)
                sp.dma_start(raw_w1[:, :], w1[bass.ds(l, 1)].rearrange("l p n -> (l p) n")).then_inc(raw_in, 16)

            def set_qkv(l):
                wait_apart(sp, qkv_split, l * 8 + 8, sp_passed)
                wait_apart(sp, kvp_mm, upto(l, -1, 1), sp_passed)
                sp.dma_start(this_qkv[:, :, :].bitcast(F32), next_qkv[:, :, :].bitcast(F32)).then_inc(qkv_in, 16)

            def set_wo(l):
                wait_apart(sp, wo_mm, upto(l, -1, 1), sp_passed)
                sp.dma_start(this_wo[:, :], wo[bass.ds(l, 1)].rearrange("l p n -> (l p) n")).then_inc(wo_in, 16)

            def set_w1(l):
                wait_apart(sp, w1_split, l * 8 + 8, sp_passed)
                wait_apart(sp, w1_mm, upto(l, -1, 1, per=FF), sp_passed)
                sp.dma_start(this_w1[:, :, :].bitcast(F32), next_w1[:, :, :].bitcast(F32)).then_inc(w1_in, 16)

            def set_w2(l):
                wait_apart(sp, w2_mm, upto(l, -1, 1), sp_passed)
                sp.dma_start(this_w2[:, :, :],
                             w2[bass.ds(l, 1)].rearrange("l (c p) n -> (l p) c n", p=P)).then_inc(w2_in, 16)

            def load_rows(l):
                wait_apart(sp, rows_summed, l * 8, sp_passed)
                sp.dma_start(row[:, bass.ds(l, 1)].rearrange("p l r n -> p (l r n)"),
                             rows[bass.ds(l, 1)].rearrange("l n -> (l n)").partition_broadcast(P)).then_inc(row_in, 16)

            sp.dma_start(x_all[:, 0], x[0]).then_inc(x_in[0], 16)
            sp.dma_start(col[:, :], cols).then_inc(col_in, 16)
            load_raw(0)
            sp.dma_start(x_all[:, 1], x[1]).then_inc(x_in[1], 16)
            load_rows(0)
            for u in range(2, HALVES):
                sp.dma_start(x_all[:, u], x[u]).then_inc(x_in[u], 16)
            sp.dma_start(r_raw[:, :], router).then_inc(router_in, 16)
            set_qkv(0)
            set_wo(0)

            def layer(l, last=False):
                if not last:
                    load_raw(l + 1)
                load_rows(l + 1)
                set_w1(l)
                set_w2(l)
                if not last:
                    set_qkv(l + 1)
                    set_wo(l + 1)

            layer(0)
            with sp.Fori(1, LAST) as l:
                layer(l)
            layer(LAST, last=True)

            for e in range(EXPERTS):
                if e == 0:
                    wait(sp, w1_scaled, LAYERS * 8)
                    wait(sp, bias_mm, LAYERS * 8)
                else:
                    wait(sp, e_scaled, e)
                    wait(sp, eb_mm, e)
                sp.dma_start(raw_w1[:, :], w1[LAYERS + e]).then_inc(raw_in, 16)
                if e == 1:
                    wait(sp, w2_mm, upto(LAST, SLOTS - 1, 1))
                if e >= 2:
                    wait(sp, down_mm[e % 2], HALVES * (e // 2))
                sp.dma_start(w2_set[e % 2][:, :, :],
                             w2[LAYERS + e].rearrange("(c p) n -> p c n", p=P)).then_inc(w2e_in[e % 2], 16)
            for u in range(HALVES):
                wait(sp, comb[1], HALVES * (EXPERTS // 2 - 1) + u + 1)
                sp.dma_start(out[u], res_a[:, u]).then_inc(out_done, 16)
            sp.wait_ge(out_done, 16 * HALVES)

        @block.gpsimd
        def _(pool):
            g = nc.gpsimd
            g.memset(ident[:, :], 0.0).then_inc(const_step, 1)
            g.memset(mask[:, :], 1.0).then_inc(const_step, 1)
            g.memset(tri[:, :, :], 1.0).then_inc(const_step, 1)
            g.memset(ones[:, :], 1.0).then_inc(const_step, 1)
            g.memset(neg_half[:, :], -0.5).then_inc(const_step, 1)
            for h in two:
                g.memset(v[h][:, :, P:VW], 1.0).then_inc(const_step, 1)
            pool.wait_ge(const_step, 7)
            g.affine_select(out=ident[:, :], in_=ident[:, :], compare_op=ALU.not_equal, fill=1.0, base=0,
                            pattern=[[-1, P]], channel_multiplier=1).then_inc(const_step, 1)
            same = mask[:, 0:P].rearrange("p (a b) -> p a b", b=HEAD)
            g.affine_select(out=same, in_=same, compare_op=ALU.is_ge, fill=0.0, base=0,
                            pattern=[[-HEAD, HEADS], [0, HEAD]], channel_multiplier=1).then_inc(const_step, 1)
            memb = mask[:, P:KVW]
            g.affine_select(out=memb, in_=memb, compare_op=ALU.is_ge, fill=0.0, base=0,
                            pattern=[[-HEAD, HEADS]], channel_multiplier=1).then_inc(const_step, 1)
            g.affine_select(out=tri[:, :, :], in_=tri[:, :, :], compare_op=ALU.is_gt, fill=0.0, base=0,
                            pattern=[[1, EXPERTS], [-1, EXPERTS]], channel_multiplier=0).then_inc(const_step, 1)
            pool.wait_ge(const_step, 11)
            g.affine_select(out=same, in_=same, compare_op=ALU.is_ge, fill=0.0, base=HEAD - 1,
                            pattern=[[HEAD, HEADS], [0, HEAD]], channel_multiplier=-1).then_inc(const_step, 1)
            g.affine_select(out=memb, in_=memb, compare_op=ALU.is_ge, fill=0.0, base=HEAD - 1,
                            pattern=[[HEAD, HEADS]], channel_multiplier=-1).then_inc(const_step, 1)
            pool.wait_ge(const_step, 13)
            g.memset(var[0][:, :], 0.0).then_inc(const_done, 1)

            def scale_qkv(l):
                wait_apart(pool, raw_in, l * 32 + 32, pool_passed)
                wait_apart(pool, qkv_split, l * 8, pool_passed)
                wait_apart(pool, boff_done, l * 8, pool_passed)
                g.tensor_copy(gain[:, 0:1], col[:, bass.ds(l + C_GIN, 1)]).then_inc(gain_done, 4)
                g.tensor_copy(gain[:, 1:2], col[:, bass.ds(l + C_BIN, 1)]).then_inc(gain_done, 4)
                wait_apart(pool, gain_done, l * 8 + 8, pool_passed)
                g.tensor_scalar(scaled_qkv[:, :], raw_qkv[:, :], gain[:, 0:1], 0.0,
                                ALU.mult, ALU.add).then_inc(qkv_scaled, 8)
                wait_apart(pool, bias_mm, l * 8, pool_passed)
                g.tensor_scalar(boff[:, :], ones[:, :], gain[:, 1:2], 0.0,
                                ALU.mult, ALU.add).then_inc(boff_done, 8)

            def split_qkv(l):
                wait_apart(pool, qkv_scaled, l * 8 + 8, pool_passed)
                wait_apart(pool, qkv_in, l * 16, pool_passed)
                g.tensor_scalar(next_qkv[:, 0, :], scaled_qkv[:, :], 1.0, 0.0, ALU.mult, ALU.add).then_inc(qkv_split, 4)
                wait_apart(pool, qkv_split, l * 8 + 4, pool_passed)
                g.tensor_tensor(next_qkv[:, 1, :], scaled_qkv[:, :], next_qkv[:, 0, :].bitcast(F32),
                                ALU.subtract).then_inc(qkv_split, 4)

            def scale_w1(l):
                wait_apart(pool, raw_in, l * 32 + 32, pool_passed)
                wait_apart(pool, w1_split, l * 8, pool_passed)
                g.tensor_copy(gain1[:, :], col[:, bass.ds(l + C_G1, 1)]).then_inc(gain1_done, 8)
                wait_apart(pool, gain1_done, l * 8 + 8, pool_passed)
                g.tensor_scalar(scaled_w1[:, :], raw_w1[:, :], gain1[:, :], 0.0,
                                ALU.mult, ALU.add).then_inc(w1_scaled, 8)

            def hi_w1(l):
                wait_apart(pool, w1_scaled, l * 8 + 8, pool_passed)
                wait_apart(pool, w1_in, l * 16, pool_passed)
                g.tensor_scalar(next_w1[:, 0, :], scaled_w1[:, :], 1.0, 0.0, ALU.mult, ALU.add).then_inc(w1_split, 4)

            def lo_w1(l):
                wait_apart(pool, w1_split, l * 8 + 4, pool_passed)
                g.tensor_tensor(next_w1[:, 1, :], scaled_w1[:, :], next_w1[:, 0, :].bitcast(F32),
                                ALU.subtract).then_inc(w1_split, 4)

            def inv_std(i, mvs, var_sem, pow_sem, rstd_sem, count, used=None, previous=0):
                wait_apart(pool, used, previous, pool_passed)
                wait_apart(pool, mvs, count, pool_passed)
                g.tensor_scalar(shift[i][:, :], mv[i][:, :, 0], -1.0, 0.0, ALU.mult, ALU.add)
                g.tensor_scalar(var[i][:, :], mv[i][:, :, 1], 1.0, EPS, ALU.mult, ALU.add).then_inc(var_sem, 1)
                wait_apart(pool, var_sem, count, pool_passed)
                g.tensor_tensor(rstd[i][:, :], var[i][:, :], neg_half[:, :], ALU.pow).then_inc(pow_sem, 1)
                wait_apart(pool, pow_sem, count, pool_passed)
                g.tensor_tensor(shift[i][:, :], shift[i][:, :], rstd[i][:, :], ALU.mult).then_inc(rstd_sem, 1)

            def inv_std1(l, s, h):
                inv_std(h, mv1_done, var1_done, pow1_done, rstd1_done, upto(l, s, h), x1_done, upto(l, s - 1, h))

            def inv_std2(l, s, h):
                inv_std(2 + h, mv2_done, var2_done, pow2_done, rstd2_done, upto(l, s, h, base=8),
                        x2_done, upto(l, s - 1, h, base=8))

            def rows_of(kind, l):
                return row[:, bass.ds(l, 1), kind, :].to_broadcast([P, T, P])

            def sum_rows(l):
                wait(pool, row_in, l * 16 + 16)
                for kind, other in ((R_BIN, R_BO), (R_B1, R_C2)):
                    r = row[:, bass.ds(l, 1), kind, :]
                    if not isinstance(l, int):
                        pool.sem_inc(pool_passed, 1)
                    g.tensor_tensor(r, r, row[:, bass.ds(l, 1), other, :], ALU.add).then_inc(rows_summed, 4)

            def resid_f(l, s, h, lw):
                wait_apart(pool, x1_done, upto(l, s, h), pool_passed)
                wait_apart(pool, s2_done, upto(l, s - 1, h), pool_passed)
                g.tensor_tensor(res_f[h][:, :, :], s1[h][:, :, :], rows_of(R_G1, lw), ALU.mult).then_inc(resf_mul, 1)
                wait_apart(pool, resf_mul, upto(l, s, h), pool_passed)
                g.tensor_tensor(res_f[h][:, :, :], res_f[h][:, :, :], rows_of(R_B1, lw), ALU.add).then_inc(resf_done, 1)

            def resid_a(l, s, h, lw):
                scale_resid(l, s, h, lw)
                offset_resid(l, s, h, lw)

            def scale_resid(l, s, h, lw):
                u = (2 * s + h) % HALVES
                wait_apart(pool, x2_done, upto(l, s, h, base=8), pool_passed)
                wait_apart(pool, s1_done, upto(l, s, h), pool_passed)
                g.tensor_tensor(res_a[:, u], s2[h][:, :, :], rows_of(R_GIN, lw), ALU.mult).then_inc(resa_mul, 1)

            def offset_resid(l, s, h, lw):
                u = (2 * s + h) % HALVES
                wait_apart(pool, resa_mul, upto(l, s, h), pool_passed)
                g.tensor_tensor(res_a[:, u], res_a[:, u], rows_of(R_BIN, lw), ALU.add).then_inc(resa_done, 1)

            def prep_router():
                pool.wait_ge(router_in, 16)
                g.tensor_scalar(r_sc[:, :], r_raw[:, :], col[:, C_GAMMA:C_GAMMA + 1], 0.0, ALU.mult, ALU.add).then_inc(r_prep, 1)
                pool.wait_ge(r_prep, 1)
                g.tensor_scalar(r_hi[:, :], r_sc[:, :], 1.0, 0.0, ALU.mult, ALU.add).then_inc(r_prep, 1)
                pool.wait_ge(r_prep, 2)
                g.tensor_tensor(r_lo[:, :], r_sc[:, :], r_hi[:, :].bitcast(F32), ALU.subtract).then_inc(r_prep, 1)
                wait(pool, bias_mm, LAYERS * 8)
                wait(pool, boff_done, LAYERS * 8)
                g.tensor_scalar(boff[:, :], ones[:, :], col[:, C_BETA:C_BETA + 1], 0.0, ALU.mult, ALU.add).then_inc(r_prep, 1)

            def prep_expert(e, until_scaled=None):
                dst = w1_set[e % 2]
                if until_scaled is not False:
                    wait(pool, raw_in, 32 * LAYERS + 16 * (e + 1))
                    wait(pool, w1_split, LAYERS * 8)
                    wait(pool, e_split, 2 * e)
                    g.tensor_scalar(scaled_w1[:, :], raw_w1[:, :], col[:, C_GAMMA:C_GAMMA + 1], 0.0,
                                    ALU.mult, ALU.add).then_inc(e_scaled, 1)
                if until_scaled:
                    return
                wait(pool, e_scaled, e + 1)
                if e == 0:
                    wait(pool, w1_in, LAYERS * 16)
                elif e == 1:
                    wait(pool, w1_mm, upto(LAST, SLOTS - 1, 1, per=FF))
                else:
                    wait(pool, up_mm[e % 2], FF * HALVES * (e // 2))
                g.tensor_scalar(dst[:, 0, :], scaled_w1[:, :], 1.0, 0.0, ALU.mult, ALU.add).then_inc(e_split, 1)
                wait(pool, e_split, 2 * e + 1)
                g.tensor_tensor(dst[:, 1, :], scaled_w1[:, :], dst[:, 0, :].bitcast(F32),
                                ALU.subtract).then_inc(e_split, 1)

            def start(u):
                inv_std(2 + u, mv2_done, var2_done, pow2_done, rstd2_done, u + 1)

            def start_resid(u):
                pool.wait_ge(x2_done, u + 1)
                g.tensor_tensor(res_a[:, u], first_norm(u), rows_of(R_BIN, 0), ALU.add).then_inc(resa_done, 1)

            start(0)
            start(1)
            pool.wait_ge(col_in, 16)
            scale_qkv(0)
            split_qkv(0)
            start(2)
            start(3)
            scale_w1(0)
            for u in range(4, HALVES):
                start(u)
            hi_w1(0)
            lo_w1(0)
            sum_rows(0)
            wait(pool, rows_summed, 8)
            for u in range(HALVES):
                start_resid(u)

            def slot(l, s, first, last):
                p1, p2 = not first or s >= 1, not first or s >= 2
                lw1 = l if s >= 1 else l - 1
                lw2 = l if s >= 2 else l - 1
                if p1:
                    inv_std1(l, s - 1, 0)
                    inv_std1(l, s - 1, 1)
                    resid_f(l, s - 1, 0, lw1)
                    resid_f(l, s - 1, 1, lw1)
                if s == 1:
                    if not last:
                        scale_qkv(l + 1)
                    else:
                        prep_router()
                elif s == 2:
                    if not last:
                        scale_w1(l + 1)
                    else:
                        prep_expert(0, until_scaled=True)
                elif s == 3 and not last:
                    lo_w1(l + 1)
                if p2:
                    inv_std2(l, s - 2, 0)
                    scale_resid(l, s - 2, 0, lw2 + 1)
                    inv_std2(l, s - 2, 1)
                    offset_resid(l, s - 2, 0, lw2 + 1)
                    resid_a(l, s - 2, 1, lw2 + 1)
                if s == 0:
                    sum_rows(l + 1)
                elif s == 1:
                    wait_apart(pool, rows_summed, l * 8 + 16, pool_passed)
                    if not last:
                        split_qkv(l + 1)
                elif s == 2:
                    if not last:
                        hi_w1(l + 1)
                    else:
                        prep_expert(0, until_scaled=False)

            for s in range(SLOTS):
                slot(0, s, True, False)
            with pool.Fori(1, LAST) as l:
                for s in range(SLOTS):
                    slot(l, s, False, False)
            for s in range(SLOTS):
                slot(LAST, s, False, True)
            def final_inv(k, u):
                i = 4 + 2 * k + u % 2
                pool.wait_ge(f_mv[k], u + 1)
                wait(pool, f_norm[k], u - 1)
                g.tensor_scalar(shift[i][:, :], mv[i][:, :, 0], -1.0, 0.0, ALU.mult, ALU.add)
                g.tensor_scalar(var[i][:, :], mv[i][:, :, 1], 1.0, EPS, ALU.mult, ALU.add).then_inc(f_var[k], 1)
                pool.wait_ge(f_var[k], u + 1)
                g.tensor_tensor(rstd[i][:, :], var[i][:, :], neg_half[:, :], ALU.pow).then_inc(f_pow[k], 1)
                pool.wait_ge(f_pow[k], u + 1)
                g.tensor_tensor(shift[i][:, :], shift[i][:, :], rstd[i][:, :], ALU.mult).then_inc(f_rstd[k], 1)

            def stack_norm(u):
                final_inv(0, u)
                i = 4 + u % 2
                pool.wait_ge(f_rstd[0], u + 1)
                wait(pool, f_sum, u - 1)
                for t in range(T):
                    ins = g.tensor_scalar(kt[u % 2][:, t, :], res_a[:, u, t, :], rstd[i][:, t:t + 1],
                                          shift[i][:, t:t + 1], ALU.mult, ALU.add)
                ins.then_inc(f_norm[0], 1)

            def start_output(u):
                pool.wait_ge(f_norm[1], u + 1)
                g.tensor_tensor(res_a[:, u], x_all[:, u], ek[u % 2][:, :, :], ALU.add).then_inc(acc_done, 1)

            inv_std1(LAST, 3, 0)
            inv_std1(LAST, 3, 1)
            stack_norm(0)
            resid_f(LAST, 3, 0, LAST)
            inv_std2(LAST, 2, 0)
            inv_std2(LAST, 2, 1)
            resid_f(LAST, 3, 1, LAST)
            resid_a(LAST, 2, 0, LAYERS)
            resid_a(LAST, 2, 1, LAYERS)
            final_inv(1, 0)
            stack_norm(1)
            inv_std2(LAST, 3, 0)
            resid_a(LAST, 3, 0, LAYERS)
            start_output(0)
            final_inv(2, 0)
            final_inv(1, 1)
            stack_norm(2)
            prep_expert(1)
            inv_std2(LAST, 3, 1)
            resid_a(LAST, 3, 1, LAYERS)
            start_output(1)
            for u in range(HALVES):
                if u + 3 < HALVES:
                    stack_norm(u + 3)
                if u + 2 < HALVES:
                    final_inv(1, u + 2)
                    start_output(u + 2)
                if u + 1 < HALVES:
                    final_inv(2, u + 1)
                if u == 3:
                    prep_expert(2, until_scaled=True)
            prep_expert(2, until_scaled=False)
            for e in range(3, EXPERTS):
                prep_expert(e)

        @block.scalar
        def _(act):
            a = nc.scalar

            def load_table(func, column, loaded, count):
                wait(act, loaded, count)
                a.activation(warm[:, column:column + 1], ones[:, 0:1], func).then_inc(loaded, 1)

            def phi_q(l, s, h):
                if s == 0 and h == 0:
                    wait(act, bias_done, l * 8 + 8)
                wait(act, q_mm, upto(l, s, h))
                wait_apart(act, qt_done, upto(l, s - 1, h), act_passed)
                a.activation(eq[h][:, :], ps(3 * h), ACT.Relu, bias=bq_neg[:, bass.ds(l, 1)], scale=-1.0).then_inc(q_rel, 1)
                wait(act, q_rel, upto(l, s, h))
                a.activation(eq[h][:, :], eq[h][:, :], ACT.Exp, scale=-1.0).then_inc(q_exp, 1)

            def phi_k(l, s, h):
                wait(act, kt_done, upto(l, s, h))
                wait(act, k_done, upto(l, s - 1, h))
                a.activation(ek[h][:, :, :], kt[h][:, :, :], ACT.Relu, scale=-1.0).then_inc(k_rel, 1)
                wait(act, k_rel, upto(l, s, h))
                a.activation(ek[h][:, :, :], ek[h][:, :, :], ACT.Exp, scale=-1.0).then_inc(k_exp, 1)

            def split_x1(l, s, h):
                wait(act, t1_mm, upto(l, s, h))
                wait(act, w1_mm, upto(l, s - 1, h, per=FF))
                a.activation(x1_hi[h][:, :], ps(7 if h == 0 else 0), ACT.Copy).then_inc(x1_hi_done, 1)

            def gelu(l, s, h, lw):
                if isinstance(l, int) and l == 0:
                    wait(act, resa_done, HALVES)
                for c in range(FF):
                    if c == 0:
                        wait(act, w2_mm, upto(l, s - 1, h))
                    wait_apart(act, w1_mm, upto(l, s, h, per=FF) - (FF - 1 - c), act_passed)
                    a.activation(hid[h][:, c, :], ps(3 + h + c), ACT.Gelu,
                                 bias=col[:, bass.ds(lw * FF + (C_C1 + c), 1)]).then_inc(hid_done, 1)

            def copy_att(l, s, h):
                wait(act, attt_mm, upto(l, s, h))
                wait(act, wo_mm, upto(l, s - 1, h))
                a.activation(att_t[h][:, :], ps(2 * h), ACT.Copy).then_inc(attt_sb, 1)

            def split_xt(l, s, h, b=None):
                u = (2 * s + h) % HALVES
                wait(act, t2_mm, upto(l, s, h, base=8))
                wait(act, kvp_mm, upto(l, s, h))
                a.activation(xt_hi[:, u], ps(4 + h if b is None else b), ACT.Copy).then_inc(xt_hi_done, 1)

            def scale_rows(i, src, dst, tile_sem):
                for t in range(T):
                    ins = a.activation(dst[:, t, :], src[:, t, :], ACT.Identity, bias=shift[i][:, t:t + 1],
                                       scale=rstd[i][:, t:t + 1])
                ins.then_inc(tile_sem, 1)

            def norm1(l, s, h):
                wait(act, rstd1_done, upto(l, s, h))
                scale_rows(h, s1[h], s1[h], x1_done)

            def norm2(l, s, h):
                wait(act, rstd2_done, upto(l, s, h, base=8))
                scale_rows(2 + h, s2[h], s2[h], x2_done)

            def start(u):
                act.wait_ge(rstd2_done, u + 1)
                scale_rows(2 + u, x_all[:, u], first_norm(u), x2_done)

            def start_split(u):
                split_xt(-1, u // 2, u % 2, b=START_BANK[u])

            start(0)
            start(1)
            start_split(0)
            start_split(1)
            start(2)
            start(3)

            def slot(l, s, first, last):
                p1, p2 = not first or s >= 1, not first or s >= 2
                lw = l if s >= 1 else l - 1
                phi_q(l, s, 0)
                phi_k(l, s, 0)
                if p1:
                    norm1(l, s - 1, 0)
                phi_q(l, s, 1)
                if p1:
                    split_x1(l, s - 1, 0)
                    norm1(l, s - 1, 1)
                phi_k(l, s, 1)
                if first and s == 0:
                    start_split(2)
                    start_split(3)
                    for u in range(4, HALVES):
                        start(u)
                    start_split(4)
                    start_split(5)
                if p1:
                    split_x1(l, s - 1, 1)
                    load_table(ACT.Gelu, 0, gelu_table, l * SLOTS + (s - 1))
                    gelu(l, s - 1, 0, lw)
                if p2:
                    norm2(l, s - 2, 0)
                if p1:
                    gelu(l, s - 1, 1, lw)
                copy_att(l, s, 0)
                copy_att(l, s, 1)
                if p2:
                    if not (last and s >= 2):
                        split_xt(l, s - 2, 0)
                    norm2(l, s - 2, 1)
                    if not (last and s >= 2):
                        split_xt(l, s - 2, 1)
                if first and s == 0:
                    start_split(6)
                    start_split(7)
                load_table(ACT.Exp, 1, exp_table, l * SLOTS + s)

            act.wait_ge(const_done, 1)
            for s in range(SLOTS):
                slot(0, s, True, False)
            with act.Fori(1, LAST) as l:
                for s in range(SLOTS):
                    slot(l, s, False, False)
            for s in range(SLOTS):
                slot(LAST, s, False, True)
            def sum_norm(u):
                act.wait_ge(f_rstd[1], u + 1)
                wait(act, f_mv[2], u - 1)
                wait(act, acc_done, u - 1)
                scale_rows(6 + u % 2, x_all[:, u], ek[u % 2], f_norm[1])

            def expert_norm(u):
                act.wait_ge(f_rstd[2], u + 1)
                act.wait_ge(f_norm[1], u + 1)
                wait(act, ft_mm, u - 1)
                scale_rows(8 + u % 2, ek[u % 2], att[u % 2], f_norm[2])

            def silu(r, k, u, buf):
                for c in range(FF):
                    wait_apart(act, up_mm[k], r * (FF * HALVES) + (FF * u + c + 1), act_passed)
                    a.activation(hid[buf][:, c, :], ps(c), ACT.Silu,
                                 bias=e_bias[:, bass.ds(r * 2 + k, 1), c]).then_inc(up_done[k], 1)

            norm1(LAST, 3, 0)
            norm1(LAST, 3, 1)
            split_x1(LAST, 3, 0)
            split_x1(LAST, 3, 1)
            gelu(LAST, 3, 0, LAST)
            norm2(LAST, 2, 0)
            norm2(LAST, 2, 1)
            gelu(LAST, 3, 1, LAST)
            sum_norm(0)
            norm2(LAST, 3, 0)
            expert_norm(0)
            sum_norm(1)
            norm2(LAST, 3, 1)

            act.wait_ge(eb_done, 1)
            for u in range(HALVES):
                act.wait_ge(ft_mm, u + 1)
                if u == 0:
                    wait(act, kvp_mm, upto(LAST, SLOTS - 1, 1))
                a.activation(xt_hi[:, u], ps(6), ACT.Copy).then_inc(xn_hi, 1)
                if u == 0:
                    wait(act, w2_mm, upto(LAST, 3, 1))
                else:
                    act.wait_ge(down_mm[0], u)
                silu(0, 0, u, 0)
                if u + 2 < HALVES:
                    sum_norm(u + 2)
                act.wait_ge(r_sub, u + 1)
                a.activation(ex[:, :, :], ex[:, :, :], ACT.Exp, scale=INV_TEMP).then_inc(r_ex, 1)
                if u + 1 < HALVES:
                    expert_norm(u + 1)
                if u == 0:
                    act.wait_ge(eb_done, 2)
                wait(act, down_mm[1], u)
                silu(0, 1, u, 1)

            def silu_sweep(r, k):
                wait(act, eb_done, r * 2 + (k + 1))
                before = (lambda n: r * HALVES + (n - HALVES)) if k == 0 else (lambda n: r * HALVES + n)
                for u in range(HALVES):
                    if u == 0 and k == 0:
                        wait(act, down_mm[0], r * HALVES)
                    if u < 2:
                        wait(act, down_mm[1 - k], before(HALVES - 1 + u))
                    else:
                        wait(act, down_mm[k], r * HALVES + (u - 1))
                    silu(r, k, u, u % 2)

            with act.Fori(1, EXPERTS // 2) as r:
                silu_sweep(r, 0)
                silu_sweep(r, 1)

        @block.vector
        def _(dve):
            d = nc.vector

            def moments(i, src, stats, mvs, count):
                for t in range(T):
                    ins = d.bn_stats(stat[i][:, t, :], src[:, t, :])
                ins.then_inc(stats, 1)
                wait_apart(dve, stats, count, dve_passed)
                for t in range(T):
                    ins = d.bn_aggr(mv[i][:, t, :], stat[i][:, t, :])
                ins.then_inc(mvs, 1)

            def keys_values(l, s, h):
                wait(dve, kvp_mm, upto(l, s, h))
                wait(dve, kvm_mm, upto(l, s - 1, h))
                for half in two:
                    b = (1, 4)[h] + half
                    src = ps(b).rearrange("p (t n) -> p t n", t=2)
                    bias = row[:, bass.ds(l, 1), R_BK:R_BK + 2, :]
                    ins = d.tensor_tensor(kt[h][:, 2 * half:2 * half + 2, :], src[:, :, 0:P],
                                          bias[:, 0, 0:1, :].to_broadcast([P, 2, P]), ALU.add)
                ins.then_inc(kt_done, 1)
                for half in two:
                    b = (1, 4)[h] + half
                    src = ps(b).rearrange("p (t n) -> p t n", t=2)
                    bias = row[:, bass.ds(l, 1), R_BK:R_BK + 2, :]
                    ins = d.tensor_tensor(v[h][:, 2 * half:2 * half + 2, 0:P], src[:, :, P:2 * P],
                                          bias[:, 0, 1:2, :].to_broadcast([P, 2, P]), ALU.add)
                ins.then_inc(v_done, 1)

            def queries(l, s, h):
                wait(dve, q_exp, upto(l, s, h))
                wait(dve, att_mm, upto(l, s - 1, h))
                d.scalar_tensor_tensor(out=qt[h][:, :], in0=ps(3 * h), scalar=bq_one[:, bass.ds(l, 1)],
                                       in1=eq[h][:, :], op0=ALU.add, op1=ALU.max).then_inc(qt_done, 1)

            def keys(l, s, h):
                wait(dve, k_exp, upto(l, s, h))
                d.scalar_tensor_tensor(out=kt[h][:, :, :], in0=kt[h][:, :, :], scalar=1.0,
                                       in1=ek[h][:, :, :], op0=ALU.add, op1=ALU.max).then_inc(k_done, 1)

            def mask_kv(l, s, h):
                wait(dve, kvm_mm, upto(l, s, h))
                wait(dve, att_mm, upto(l, s - 1, h))
                src = ps(1 + h).rearrange("p (q n) -> p q n", q=2)
                d.tensor_tensor(kv[h][:, :, 0:P], src[:, :, 0:P],
                                mask[:, 0:P].unsqueeze(1).to_broadcast([P, 2, P]), ALU.mult)
                for q in two:
                    ins = d.tensor_scalar(kv[h][:, q, P:KVW], mask[:, P:KVW], src[:, q, P:P + 1], None, ALU.mult)
                ins.then_inc(kv_done, 1)

            def attend(l, s, h):
                wait(dve, att_mm, upto(l, s, h))
                wait(dve, attt_mm, upto(l, s - 1, h))
                src = bank[h][:, :, 0:2 * KVW].rearrange("p b (t n) -> p b t n", t=2)
                d.tensor_scalar(den[h][:, :, :].rearrange("p (b t) c -> p b t c", b=2), src[:, :, :, P:KVW], DEN_EPS, None,
                                ALU.add).then_inc(den_done, 1)
                wait(dve, den_done, upto(l, s, h))
                d.reciprocal(rec[h][:, :, :], den[h][:, :, :]).then_inc(rec_done, 1)
                wait(dve, rec_done, upto(l, s, h))
                for b in two:
                    ins = d.tensor_tensor(
                        att[h][:, 2 * b:2 * b + 2, :].rearrange("p t (a c) -> p t a c", c=HEAD),
                        src[:, b, :, 0:P].rearrange("p t (a c) -> p t a c", c=HEAD),
                        rec[h][:, 2 * b:2 * b + 2, :].unsqueeze(3).to_broadcast([P, 2, HEADS, HEAD]), ALU.mult)
                ins.then_inc(att_done, 1)

            def add_res1(l, s, h):
                u = (2 * s + h) % HALVES
                wait(dve, wo_mm, upto(l, s, h))
                wait(dve, resa_done, upto(l, s, h))
                wait(dve, t1_mm, upto(l, s - 1, h))
                wait(dve, resf_mul, upto(l, s - 1, h))
                d.tensor_tensor(s1[h][:, :, :], ps(7 - h).rearrange("p (t n) -> p t n", t=T), res_a[:, u],
                                ALU.add).then_inc(s1_done, 1)

            def moments1(l, s, h):
                wait(dve, s1_done, upto(l, s, h))
                wait(dve, rstd1_done, upto(l, s - 1, h))
                moments(h, s1[h], stat1_done, mv1_done, upto(l, s, h))

            def lo_x1(l, s, h):
                wait(dve, x1_hi_done, upto(l, s, h))
                wait(dve, w1_mm, upto(l, s - 1, h, per=FF))
                d.tensor_tensor(x1_lo[h][:, :], ps(7 if h == 0 else 0), x1_hi[h][:, :].bitcast(F32),
                                ALU.subtract).then_inc(x1_lo_done, 1)

            def add_res2(l, s, h, lastl=False):
                wait(dve, w2_mm, upto(l, s, h))
                wait(dve, resf_done, upto(l, s, h))
                if not (lastl and s >= 1):
                    wait(dve, t2_mm, upto(l, s - 1, h, base=8))
                wait(dve, resa_mul, upto(l, s - 1, h))
                d.tensor_tensor(s2[h][:, :, :], ps(3 if h == 0 else 6).rearrange("p (t n) -> p t n", t=T),
                                res_f[h][:, :, :], ALU.add).then_inc(s2_done, 1)

            def moments2(l, s, h):
                wait(dve, s2_done, upto(l, s, h))
                wait(dve, rstd2_done, upto(l, s - 1, h, base=8))
                moments(2 + h, s2[h], stat2_done, mv2_done, upto(l, s, h, base=8))

            def lo_xt(l, s, h, b=None):
                u = (2 * s + h) % HALVES
                wait(dve, xt_hi_done, upto(l, s, h, base=8))
                d.tensor_tensor(xt_lo[:, u], ps(4 + h if b is None else b), xt_hi[:, u].bitcast(F32), ALU.subtract).then_inc(xt_lo_done, 1)

            def biases(l):
                wait(dve, bias_mm, l * 8 + 8)
                wait(dve, row_in, l * 16 + 16)
                b = ps(1)
                kvb = row[:, bass.ds(l, 1), R_BK:R_BK + 2, :].rearrange("p l a n -> p (l a) n")
                bq = col[:, bass.ds(l + C_BQ, 1)]
                c1 = col[:, bass.ds(l * FF + C_C1, FF)]
                d.tensor_tensor(kvb, b[:, 0:2 * P].rearrange("p (a b) -> p a b", a=2), kvb, ALU.add)
                d.scalar_tensor_tensor(out=bq_neg[:, bass.ds(l, 1)], in0=b[:, 256:257], scalar=-1.0, in1=bq,
                                       op0=ALU.mult, op1=ALU.subtract)
                d.scalar_tensor_tensor(out=bq_one[:, bass.ds(l, 1)], in0=b[:, 256:257], scalar=1.0, in1=bq,
                                       op0=ALU.add, op1=ALU.add)
                d.tensor_tensor(c1, b[:, 260:260 + FF], c1, ALU.add).then_inc(bias_done, 8)

            def start(u):
                dve.wait_ge(x_in[u], 16)
                moments(2 + u, x_all[:, u], stat2_done, mv2_done, u + 1)

            def start_lo(u):
                lo_xt(-1, u // 2, u % 2, b=START_BANK[u])

            for u in range(4):
                start(u)
            start_lo(0)
            start_lo(1)
            biases(0)
            for u in range(4, HALVES):
                start(u)

            def slot(l, s, first, last):
                p1, p2 = not first or s >= 1, not first or s >= 2
                if s == 0:
                    wait(dve, bias_done, l * 8 + 8)
                if p1:
                    moments1(l, s - 1, 0)
                keys_values(l, s, 0)
                if p1:
                    moments1(l, s - 1, 1)
                queries(l, s, 0)
                keys(l, s, 0)
                keys_values(l, s, 1)
                queries(l, s, 1)
                if p1:
                    lo_x1(l, s - 1, 0)
                if p2:
                    add_res2(l, s - 2, 1, last)
                mask_kv(l, s, 0)
                keys(l, s, 1)
                if p2:
                    moments2(l, s - 2, 0)
                if p1:
                    lo_x1(l, s - 1, 1)
                if first and s == 0:
                    start_lo(2)
                    start_lo(3)
                mask_kv(l, s, 1)
                attend(l, s, 0)
                attend(l, s, 1)
                if first and s == 0:
                    start_lo(4)
                    start_lo(5)
                if p2:
                    moments2(l, s - 2, 1)
                if p2 and not (last and s >= 2):
                    lo_xt(l, s - 2, 0)
                if p1:
                    add_res2(l, s - 1, 0, last)
                add_res1(l, s, 0)
                add_res1(l, s, 1)
                if first and s == 0:
                    start_lo(6)
                    start_lo(7)
                if p2 and not (last and s >= 2):
                    lo_xt(l, s - 2, 1)
                if s == 2 and not last:
                    biases(l + 1)
                if s == 2 and last:
                    dve.wait_ge(eb_mm, 1)
                    d.tensor_copy(r_bias[:, :], ps(1)[:, 0:EXPERTS]).then_inc(rb_done, 1)
                    d.tensor_copy(e_bias[:, 0, :], ps(1)[:, 260:260 + FF]).then_inc(eb_done, 1)

            for s in range(SLOTS):
                slot(0, s, True, False)
            with dve.Fori(1, LAST) as l:
                for s in range(SLOTS):
                    slot(l, s, False, False)
            for s in range(SLOTS):
                slot(LAST, s, False, True)

            stats = [0]

            def final_moments(k, u, src):
                i = 4 + 2 * k + u % 2
                wait(dve, f_rstd[k], u - 1)
                for t in range(T):
                    ins = d.bn_stats(stat[i][:, t, :], src[:, t, :])
                stats[0] += 1
                ins.then_inc(f_stat, 1)
                dve.wait_ge(f_stat, stats[0])
                for t in range(T):
                    ins = d.bn_aggr(mv[i][:, t, :], stat[i][:, t, :])
                ins.then_inc(f_mv[k], 1)

            def stack_moments(u):
                wait(dve, resa_done, upto(LAST, 0, u, base=8))
                final_moments(0, u, res_a[:, u])

            def outer_residual(u):
                y = kt[u % 2]
                dve.wait_ge(f_norm[0], u + 1)
                d.tensor_tensor(y[:, :, :], y[:, :, :], row[:, LAYERS, R_G1:R_G1 + 1, :].to_broadcast([P, T, P]),
                                ALU.mult).then_inc(f_gain, 1)
                dve.wait_ge(f_gain, u + 1)
                d.tensor_tensor(y[:, :, :], y[:, :, :], row[:, LAYERS, R_B1:R_B1 + 1, :].to_broadcast([P, T, P]),
                                ALU.add).then_inc(f_offset, 1)
                dve.wait_ge(f_offset, u + 1)
                d.tensor_tensor(x_all[:, u], y[:, :, :], x_all[:, u], ALU.add).then_inc(f_sum, 1)
                dve.wait_ge(f_sum, u + 1)
                final_moments(1, u, x_all[:, u])

            def expert_moments(u):
                dve.wait_ge(f_norm[1], u + 1)
                final_moments(2, u, ek[u % 2])

            steps = [0]

            def link(ins):
                steps[0] += 1
                ins.then_inc(r_step, 1)
                dve.wait_ge(r_step, steps[0])

            def logits(u):
                dve.wait_ge(r_mm, u + 1)
                link(d.tensor_tensor(ex[:, :, :], ps(7)[:, 0:T * EXPERTS].rearrange("p (t e) -> p t e", t=T),
                                     r_bias[:, :].unsqueeze(1).to_broadcast([P, T, EXPERTS]), ALU.add))
                link(d.tensor_reduce(mx[:, :], ex[:, :, :], AX.X, ALU.max))
                d.tensor_tensor(ex[:, :, :], ex[:, :, :], mx[:, :].unsqueeze(2).to_broadcast([P, T, EXPERTS]),
                                ALU.subtract).then_inc(r_sub, 1)

            def routing(u):
                dve.wait_ge(r_ex, u + 1)
                e_j = ex[:, :, :].unsqueeze(2).to_broadcast([P, T, EXPERTS, EXPERTS])
                e_e = ex[:, :, :].unsqueeze(3).to_broadcast([P, T, EXPERTS, EXPERTS])
                d.tensor_tensor(gt[:, :, :, :], e_j, e_e, ALU.is_gt)
                link(d.tensor_tensor(ge[:, :, :, :], e_j, e_e, ALU.is_equal))
                flat = ge[:, :, :, :].rearrange("p t a b -> p t (a b)")
                link(d.tensor_tensor(flat, flat, tri[:, :, :].rearrange("p a b -> p (a b)").unsqueeze(1)
                                     .to_broadcast([P, T, EXPERTS * EXPERTS]), ALU.mult))
                link(d.tensor_tensor(gt[:, :, :, :], gt[:, :, :, :], ge[:, :, :, :], ALU.add))
                d.tensor_reduce(rank[:, :, :], gt[:, :, :, :], AX.X, ALU.add)
                link(d.tensor_reduce(mx[:, :], ex[:, :, :], AX.X, ALU.add))
                link(d.reciprocal(mx[:, :], mx[:, :]))
                link(d.scalar_tensor_tensor(out=rank[:, :, :], in0=rank[:, :, :], scalar=2.0, in1=ex[:, :, :],
                                            op0=ALU.is_lt, op1=ALU.mult))
                d.tensor_tensor(gate[:, :, T * u:T * u + T].rearrange("p e t -> p t e"), rank[:, :, :],
                                mx[:, :].unsqueeze(2).to_broadcast([P, T, EXPERTS]), ALU.mult).then_inc(gate_done, 1)

            def combine(r, k, u, b):
                wait(dve, down_mm[k], r * HALVES + (u + 1))
                for t in range(T):
                    ins = d.scalar_tensor_tensor(
                        out=res_a[:, u, t, :], in0=ps(b)[:, t * P:(t + 1) * P],
                        scalar=gate[:, bass.ds(r * 2 + k, 1), T * u + t], in1=res_a[:, u, t, :],
                        op0=ALU.mult, op1=ALU.add)
                ins.then_inc(comb[k], 1)

            moments1(LAST, 3, 0)
            moments1(LAST, 3, 1)
            stack_moments(0)
            add_res2(LAST, 2, 1, True)
            lo_x1(LAST, 3, 0)
            lo_x1(LAST, 3, 1)
            moments2(LAST, 2, 0)
            moments2(LAST, 2, 1)
            outer_residual(0)
            stack_moments(1)
            add_res2(LAST, 3, 0, True)
            moments2(LAST, 3, 0)
            expert_moments(0)
            outer_residual(1)
            stack_moments(2)
            add_res2(LAST, 3, 1, True)
            moments2(LAST, 3, 1)

            for u in range(HALVES):
                dve.wait_ge(xn_hi, u + 1)
                d.tensor_tensor(xt_lo[:, u], ps(6), xt_hi[:, u].bitcast(F32), ALU.subtract).then_inc(xn_lo, 1)
                if u == 0:
                    dve.wait_ge(eb_mm, 2)
                    d.tensor_copy(e_bias[:, 1, :], ps(5)[:, 0:FF]).then_inc(eb_done, 1)
                if u + 3 < HALVES:
                    stack_moments(u + 3)
                if u + 2 < HALVES:
                    outer_residual(u + 2)
                if u >= 1:
                    dve.wait_ge(comb[0], u)
                    combine(0, 1, u - 1, 5)
                logits(u)
                if u + 1 < HALVES:
                    expert_moments(u + 1)
                if u == HALVES - 1:
                    dve.wait_ge(eb_mm, 3)
                    d.tensor_copy(e_bias[:, 2, :], ps(6)[:, 0:FF]).then_inc(eb_done, 1)
                routing(u)
                dve.wait_ge(gate_done, u + 1)
                dve.wait_ge(acc_done, u + 1)
                combine(0, 0, u, 4)
            dve.wait_ge(comb[0], HALVES)
            combine(0, 1, HALVES - 1, 5)

            def combine_sweep(r, k, last=False):
                for u in range(HALVES):
                    if u == 0:
                        wait(dve, comb[1 - k], r * HALVES + (HALVES if k == 1 else 0))
                    combine(r, k, u, 4 + u % 2)
                    if u == 3 and not last:
                        wait(dve, eb_mm, r * 2 + (k + 2))
                        d.tensor_copy(e_bias[:, bass.ds(r * 2 + (k + 1), 1), :],
                                      ps(6)[:, 0:FF].unsqueeze(1)).then_inc(eb_done, 1)

            with dve.Fori(1, EXPERTS // 2 - 1) as r:
                combine_sweep(r, 0)
                combine_sweep(r, 1)
            combine_sweep(EXPERTS // 2 - 1, 0)
            combine_sweep(EXPERTS // 2 - 1, 1, last=True)

        @block.tensor
        def _(pe):
            t_ = nc.tensor

            def three(out_, a_hi, a_lo, b_hi, b_lo):
                t_.matmul(out_, a_hi, b_hi, start=True, stop=False)
                t_.matmul(out_, a_hi, b_lo, start=False, stop=False)
                return t_.matmul(out_, a_lo, b_hi, start=False, stop=True)

            def project(l, s, h, first, last):
                u = (2 * s + h) % HALVES
                if s == 0 and h == 0:
                    wait(pe, qkv_in, l * 16 + 16)
                wait(pe, xt_lo_done, upto(l, s, h))
                if h == 1:
                    wait(pe, s2_done, upto(l, s - 2, 0))
                three(ps(3 * h), this_qkv[:, 0, 0:P], this_qkv[:, 1, 0:P], xt_hi[:, u], xt_lo[:, u]).then_inc(q_mm, 1)
                if h == 1 and not (last and s == 3):
                    wait(pe, xt_lo_done, (2 if s == 0 else HALVES) if first and s < 3 else upto(l, s - 3, 1, base=8))
                elif h == 0 and ((s == 3 and not last) or (first and s == 0)):
                    wait(pe, bias_done, l * 8 + (16 if s == 3 else 8))
                elif h == 0 and s == 3:
                    wait(pe, eb_done, 1)
                for t in range(T):
                    b = ps((1, 4)[h] + t // 2)[:, (t % 2) * 256:(t % 2) * 256 + 256]
                    tile = slice(t * P, (t + 1) * P)
                    ins = three(b, xt_hi[:, u, tile], xt_lo[:, u, tile], this_qkv[:, 0, P:QKV], this_qkv[:, 1, P:QKV])
                ins.then_inc(kvp_mm, 1)

            def key_value(l, s, h):
                wait(pe, k_done, upto(l, s, h))
                wait(pe, v_done, upto(l, s, h))
                for q in two:
                    for t in two:
                        ins = t_.matmul(ps(1 + h)[:, q * 256:q * 256 + P + 1], kt[h][:, 2 * q + t, :],
                                        v[h][:, 2 * q + t, 0:P + 1], start=t == 0, stop=t == 1)
                ins.then_inc(kvm_mm, 1)

            def attention(l, s, h, first):
                wait(pe, kv_done, upto(l, s, h))
                wait(pe, qt_done, upto(l, s, h))
                if h == 0:
                    wait(pe, x1_lo_done, upto(l, s - 1, 1))
                else:
                    wait(pe, hid_done, upto(l, s - 1, 0, per=FF) - 3)
                for t in range(T):
                    ins = t_.matmul(bank[h][:, t // 2, (t % 2) * KVW:(t % 2 + 1) * KVW], qt[h][:, t * P:(t + 1) * P],
                                    kv[h][:, t // 2, :], start=True, stop=True)
                ins.then_inc(att_mm, 1)

            def flip(b, src):
                for t in range(T):
                    ins = t_.transpose(ps(b)[:, t * P:(t + 1) * P], src[:, t, :], ident[:, :])
                return ins

            def flip_att(l, s, h):
                wait(pe, att_done, upto(l, s, h))
                flip(2 * h, att[h]).then_inc(attt_mm, 1)

            def out_proj(l, s, h):
                if s == 0 and h == 0:
                    wait(pe, wo_in, l * 16 + 16)
                wait(pe, attt_sb, upto(l, s, h))
                wait(pe, hid_done, upto(l, s - 1, 1, per=FF) - h)
                for t in range(T):
                    ins = t_.matmul(ps(7 - h)[:, t * P:(t + 1) * P], att_t[h][:, t * P:(t + 1) * P], this_wo[:, :],
                                    start=True, stop=True)
                ins.then_inc(wo_mm, 1)

            def flip_x1(l, s, h, tail=False):
                wait(pe, x1_done, upto(l, s, h))
                if h == 1 and not tail:
                    wait(pe, qt_done, upto(l, s + 1, 0))
                flip(7 if h == 0 else 0, s1[h]).then_inc(t1_mm, 1)

            def ff_up(l, s, h, lw, between=None):
                if s % SLOTS == 0 and h == 0:
                    wait(pe, w1_in, lw * 16 + 16)
                wait(pe, x1_lo_done, upto(l, s, h))
                for c in range(FF):
                    chunk = slice(c * P, (c + 1) * P)
                    if h == 0 and c == 3:
                        wait(pe, s2_done, upto(l, s - 1, 1))
                    if h == 1 and c < 3:
                        wait(pe, hid_done, upto(l, s, 0, per=FF) - 2 + c)
                    three(ps(3 + h + c), this_w1[:, 0, chunk], this_w1[:, 1, chunk], x1_hi[h][:, :], x1_lo[h][:, :]
                          ).then_inc(w1_mm, 1)
                    if c == 1 and between is not None:
                        between()

            def ff_down(l, s, h, lw, between=None):
                if s % SLOTS == 0 and h == 0:
                    wait(pe, w2_in, lw * 16 + 16)
                wait(pe, hid_done, upto(l, s, h, per=FF))
                if h == 1:
                    wait(pe, s1_done, upto(l, s + 1, 1) if not (isinstance(l, int) and l == LAST and s == 3)
                         else upto(l, s, 1))
                for t in range(T):
                    for c in range(FF):
                        ins = t_.matmul(ps(3 if h == 0 else 6)[:, t * P:(t + 1) * P], hid[h][:, c, t * P:(t + 1) * P],
                                        this_w2[:, c, :], start=c == 0, stop=c == FF - 1)
                    if t == 1 and between is not None:
                        between()
                ins.then_inc(w2_mm, 1)

            def flip_x2(l, s, h):
                wait(pe, x2_done, upto(l, s, h, base=8))
                wait(pe, hid_done, upto(l, s + 1, 1, per=FF) - 3 + h)
                flip(4 + h, s2[h]).then_inc(t2_mm, 1)

            def bias_products(l):
                if isinstance(l, int) and l == 0:
                    pe.wait_ge(col_in, 16)
                wait(pe, raw_in, l * 32 + 32)
                wait(pe, boff_done, l * 8 + 8)
                b = ps(1)
                t_.matmul(b[:, 0:2 * P], boff[:, :], raw_qkv[:, P:QKV], start=True, stop=True)
                t_.matmul(b[:, 256:257], raw_qkv[:, 0:P], col[:, bass.ds(l + C_BIN, 1)], start=True, stop=True)
                for c in range(FF):
                    ins = t_.matmul(b[:, 260 + c:261 + c], raw_w1[:, c * P:(c + 1) * P], col[:, bass.ds(l + C_B1, 1)],
                                    start=True, stop=True)
                ins.then_inc(bias_mm, 8)

            def router_bias():
                pe.wait_ge(r_prep, 4)
                t_.matmul(ps(1)[:, 0:EXPERTS], boff[:, :], r_raw[:, :], start=True, stop=True).then_inc(rb_mm, 1)

            def expert_bias(e, b, at):
                wait(pe, raw_in, 32 * LAYERS + (e * 16 + 16))
                for c in range(FF):
                    ins = t_.matmul(ps(b)[:, at + c:at + c + 1], raw_w1[:, c * P:(c + 1) * P],
                                    col[:, C_BETA:C_BETA + 1], start=True, stop=True)
                ins.then_inc(eb_mm, 1)

            pe.wait_ge(const_done, 1)
            def start(u):
                pe.wait_ge(x2_done, u + 1)
                if 4 <= u < 6:
                    pe.wait_ge(xt_lo_done, u - 1)
                elif u >= 6:
                    pe.wait_ge(v_done, 2)
                flip(START_BANK[u], first_norm(u)).then_inc(t2_mm, 1)

            start(0)
            start(1)
            bias_products(0)

            def slot(l, s, first, last):
                p1, p2 = not first or s >= 1, not first or s >= 2
                lw1 = l if s >= 1 else l - 1
                lw2 = l if s >= 2 else l - 1
                project(l, s, 0, first, last)
                project(l, s, 1, first, last)
                if first and s == 0:
                    start(2)
                    start(3)
                if p2:
                    ff_down(l, s - 2, 1, lw2, between=lambda: flip_x1(l, s - 1, 0))
                elif p1:
                    flip_x1(l, s - 1, 0)
                key_value(l, s, 0)
                if p1:
                    ff_up(l, s - 1, 0, lw1, between=lambda: flip_x1(l, s - 1, 1))
                key_value(l, s, 1)
                attention(l, s, 0, first)
                attention(l, s, 1, first)
                if p1:
                    ff_up(l, s - 1, 1, lw1)
                if first and s == 0:
                    start(4)
                    start(5)
                flip_att(l, s, 0)
                if p2 and not (last and s >= 2):
                    flip_x2(l, s - 2, 0)
                flip_att(l, s, 1)
                if p1:
                    ff_down(l, s - 1, 0, lw1)
                if first and s == 0:
                    pe.wait_ge(xt_lo_done, 6)
                out_proj(l, s, 0)
                out_proj(l, s, 1)
                if first and s == 0:
                    start(6)
                    start(7)
                if p2 and not (last and s >= 2):
                    flip_x2(l, s - 2, 1)
                if s == 2 and not last:
                    bias_products(l + 1)
                if s == 2 and last:
                    router_bias()
                    expert_bias(0, 1, 260)

            for s in range(SLOTS):
                slot(0, s, True, False)
            with pe.Fori(1, LAST) as l:
                for s in range(SLOTS):
                    slot(l, s, False, False)
            for s in range(SLOTS):
                slot(LAST, s, False, True)
            ff_down(LAST, 2, 1, LAST)
            flip_x1(LAST, 3, 0, tail=True)
            flip_x1(LAST, 3, 1, tail=True)
            ff_up(LAST, 3, 0, LAST)
            ff_up(LAST, 3, 1, LAST)
            ff_down(LAST, 3, 0, LAST)
            ff_down(LAST, 3, 1, LAST)

            def norm_and_route(u):
                pe.wait_ge(xn_lo, u + 1)
                pe.wait_ge(rb_done, 1)
                wait(pe, r_sub, u)
                for t in range(T):
                    tile = slice(t * P, (t + 1) * P)
                    ins = three(ps(7)[:, t * EXPERTS:(t + 1) * EXPERTS], xt_hi[:, u, tile], xt_lo[:, u, tile],
                                r_hi[:, :], r_lo[:, :])
                ins.then_inc(r_mm, 1)

            def up(r, k, u):
                w = w1_set[k]
                for c in range(FF):
                    chunk = slice(c * P, (c + 1) * P)
                    if isinstance(r, int) and r == 0:
                        wait(pe, up_done[1 - k], FF * (u - 1 + k) + c + 1)
                    elif u > 0:
                        wait(pe, up_done[k], r * (FF * HALVES) + (FF * (u - 1) + c + 1))
                    else:
                        wait(pe, up_done[1 - k], r * (FF * HALVES) + (FF * HALVES * k - FF + c + 1))
                    three(ps(c), w[:, 0, chunk], w[:, 1, chunk], xt_hi[:, u], xt_lo[:, u]).then_inc(up_mm[k], 1)

            def down(r, k, u, buf, b):
                if u == 0:
                    wait(pe, w2e_in[k], r * 16 + 16)
                wait(pe, up_done[k], r * (FF * HALVES) + FF * (u + 1))
                for t in range(T):
                    for c in range(FF):
                        ins = t_.matmul(ps(b)[:, t * P:(t + 1) * P], hid[buf][:, c, t * P:(t + 1) * P],
                                        w2_set[k][:, c, :], start=c == 0, stop=c == FF - 1)
                ins.then_inc(down_mm[k], 1)

            for u in range(HALVES):
                pe.wait_ge(f_norm[2], u + 1)
                if u == 0:
                    pe.wait_ge(s2_done, upto(LAST, 3, 1))
                wait(pe, xn_lo, u)
                flip(6, att[u % 2]).then_inc(ft_mm, 1)
                if u >= 1:
                    wait(pe, comb[1], u - 1)
                    down(0, 1, u - 1, 1, 5)
                if u == 0:
                    expert_bias(1, 5, 0)
                pe.wait_ge(xn_lo, u + 1)
                if u == 0:
                    pe.wait_ge(e_split, 2)
                up(0, 0, u)
                norm_and_route(u)
                if u == HALVES - 1:
                    expert_bias(2, 6, 0)
                if u == 0:
                    pe.wait_ge(e_split, 4)
                up(0, 1, u)
                wait(pe, comb[0], u)
                if u == 0:
                    pe.wait_ge(eb_done, 2)
                down(0, 0, u, 0, 4)

            def sweep(r, k, last=False):
                for u in range(HALVES):
                    if u == 0:
                        wait(pe, e_split, r * 4 + (2 * k + 2))
                    up(r, k, u)
                    if u == 0:
                        prev = (r - 1, 1) if k == 0 else (r, 0)
                        wait(pe, comb[prev[1]], prev[0] * HALVES + (HALVES - 2))
                        down(prev[0], prev[1], HALVES - 1, 1, 5)
                    else:
                        if u <= 2:
                            if k == 0 and u == 1:
                                wait(pe, comb[0], r * HALVES)
                            wait(pe, comb[1 - k], r * HALVES + (HALVES * k - HALVES + HALVES - 2 + u))
                        else:
                            wait(pe, comb[k], r * HALVES + (u - 2))
                        down(r, k, u - 1, (u - 1) % 2, 4 + (u - 1) % 2)
                    if u == 3 and not last:
                        wait(pe, eb_done, r * 2 + (k + 1))
                        expert_bias(r * 2 + (k + 1), 6, 0)

            with pe.Fori(1, EXPERTS // 2 - 1) as r:
                sweep(r, 0)
                sweep(r, 1)
            sweep(EXPERTS // 2 - 1, 0)
            sweep(EXPERTS // 2 - 1, 1, last=True)
            wait(pe, comb[1], (EXPERTS // 2 - 1) * HALVES + HALVES - 2)
            down(EXPERTS // 2 - 1, 1, HALVES - 1, 1, 5)


def kernel(**inputs):
    import concourse.bacc as _bacc
    from concourse.bass_utils import run_bass_kernel_spmd as _run

    a = {k: np.ascontiguousarray(np.asarray(v)) for k, v in inputs.items()}
    ones, zeros = np.ones((1, P), np.float32), np.zeros((1, P), np.float32)
    A = "L0_attn_"

    def halves(y):
        return np.ascontiguousarray(y.reshape(HALVES, T, P, P).transpose(0, 2, 1, 3))

    gin, bin_ = np.concatenate([ones, a[A + "g2"]]), np.concatenate([zeros, a[A + "be2"]])
    rows = np.stack([gin, bin_, np.concatenate([a[A + "bo"], zeros]),
                     np.concatenate([a[A + "g1"], a[A + "gf"][None]]), np.concatenate([a[A + "be1"], a[A + "bef"][None]]),
                     np.concatenate([a[A + "c2"], zeros]), np.concatenate([a[A + "bk"], zeros]),
                     np.concatenate([a[A + "bv"], zeros])], axis=1).reshape(LAYERS + 1, ROWS * P)
    cols = np.concatenate([gin[:LAYERS], bin_[:LAYERS], a[A + "g1"], a[A + "be1"], a[A + "bq"],
                           a[A + "c1"].reshape(LAYERS * FF, P), a["L0_ffn_gamma"][None], a["L0_ffn_beta"][None]]).T
    arrays = {
        "x": halves(a[A + "x"].reshape(-1, P)),
        "rows": rows,
        "cols": cols,
        "wqkv": np.concatenate([a[A + "Wq"], a[A + "Wk"], a[A + "Wv"]], axis=2),
        "wo": a[A + "Wo"],
        "w1": np.concatenate([a[A + "W1"], a["L0_ffn_W1"]]),
        "w2": np.concatenate([a[A + "W2"], a["L0_ffn_W2"]]),
        "router": a["L0_ffn_router_w"].T,
    }
    arrays = {k: np.ascontiguousarray(v) for k, v in arrays.items()}
    nc = _bacc.Bacc("TRN2", target_bir_lowering=False, num_devices=1)
    args = [nc.dram_tensor(k, v.shape, mybir.dt.from_np(v.dtype), kind="ExternalInput").ap() for k, v in arrays.items()]
    out = nc.dram_tensor("out", (HALVES, P, T, P), F32, kind="ExternalOutput").ap()
    build(nc, *args, out)
    r = _run(nc, [arrays], core_ids=[0])
    got = r.results[0]["out"]
    return np.ascontiguousarray(got.transpose(0, 2, 1, 3)).reshape(16, 256, P)
```

```python
from contextlib import ExitStack

import numpy as np

import concourse.bass as bass
from concourse import mybir

F32 = mybir.dt.float32
F32R = mybir.dt.float32r
ALU = mybir.AluOpType
ACT = mybir.ActivationFunctionType
AX = mybir.AxisListType

P = 128
LAYERS = 8
EXPERTS = 8
HEADS, HEAD = 16, 8
FF = 4
HALVES = 8
T = 4
N = T * P
SLOTS = HALVES // 2
QKV = 3 * P
NORMS = 4 + 3 * HALVES
EPS = 1e-5
DEN_EPS = 1e-6
INV_TEMP = 1.0 / 1.5
KVW = P + HEADS
VW = P + 2

C_GIN, C_BIN = 0, 8
C_G1, C_B1 = 16, 24
C_BQ = 32
C_C1 = 40
C_GAMMA, C_BETA = 72, 73
C_END = 74
ROWS = 8
R_GIN, R_BIN, R_BO = 0, 1, 2
R_G1, R_B1, R_C2 = 3, 4, 5
R_BK = 6


def wait(eng, sem, count):
    if not isinstance(count, int) or count > 0:
        eng.wait_ge(sem, count)


def wait_apart(eng, sem, count, passed):
    wait(eng, sem, count)
    if not isinstance(count, int):
        eng.sem_inc(passed, 1)


def upto(l, s, h, per=1, base=0):
    return l * (HALVES * per) + per * (2 * s + h + 1 + base)


def build(nc, x, rows, cols, wqkv, wo, w1, w2, router, out):
    ctx = ExitStack()
    with ctx:
        def sb(name, shape, dt=F32):
            return ctx.enter_context(nc.sbuf_tensor(name, shape, dt))

        def sem(name):
            return ctx.enter_context(nc.semaphore(name))

        bank = [ctx.enter_context(nc.psum_tensor("ps01", [P, 2, 512], F32)),
                ctx.enter_context(nc.psum_tensor("ps23", [P, 2, 512], F32)),
                ctx.enter_context(nc.psum_tensor("ps45", [P, 2, 512], F32)),
                ctx.enter_context(nc.psum_tensor("ps67", [P, 2, 512], F32))]

        def ps(b):
            return bank[b // 2][:, b % 2, :]

        x_all = sb("x_all", [P, HALVES, T, P])
        res_a = sb("res_a", [P, HALVES, T, P])
        xt_hi = sb("xt_hi", [P, HALVES, N], F32R)
        xt_lo = sb("xt_lo", [P, HALVES, N], F32R)
        ident = sb("ident", [P, P])
        mask = sb("mask", [P, KVW])
        neg_half = sb("neg_half", [P, T])
        ones = sb("ones", [P, P])
        warm = sb("warm", [P, 2])
        order = sb("order", [P, EXPERTS])
        row = sb("row", [P, LAYERS + 1, ROWS, P])
        col = sb("col", [P, C_END])
        bq_neg = sb("bq_neg", [P, LAYERS])
        bq_one = sb("bq_one", [P, LAYERS])
        raw_qkv = sb("raw_qkv", [P, QKV])
        raw_w1 = sb("raw_w1", [P, N])
        scaled_qkv = sb("scaled_qkv", [P, QKV])
        scaled_w1 = sb("scaled_w1", [P, N])
        next_qkv = sb("next_qkv", [P, 2, QKV], F32R)
        this_qkv = sb("this_qkv", [P, 2, QKV], F32R)
        next_w1 = sb("next_w1", [P, 2, N], F32R)
        this_w1 = sb("this_w1", [P, 2, N], F32R)
        this_wo = sb("this_wo", [P, P])
        this_w2 = sb("this_w2", [P, FF, P])
        other_w2 = sb("other_w2", [P, FF, P])
        gain = sb("gain", [P, 2])
        gain1 = sb("gain1", [P, 1])
        boff = sb("boff", [P, P])
        two = range(2)
        eq = [sb(f"eq{h}", [P, N]) for h in two]
        qt = [sb(f"qt{h}", [P, N]) for h in two]
        kt = [sb(f"kt{h}", [P, T, P]) for h in two]
        ek = [sb(f"ek{h}", [P, T, P]) for h in two]
        v = [sb(f"v{h}", [P, T, VW]) for h in two]
        kv = [sb(f"kv{h}", [P, 2, KVW]) for h in two]
        den = [sb(f"den{h}", [P, T, HEADS]) for h in two]
        rec = [sb(f"rec{h}", [P, T, HEADS]) for h in two]
        att = [sb(f"att{h}", [P, T, P]) for h in two]
        att_t = [sb(f"att_t{h}", [P, N]) for h in two]
        s1 = [sb(f"s1{h}", [P, T, P]) for h in two]
        s2 = [sb(f"s2{h}", [P, T, P]) for h in two]
        x1_hi = [sb(f"x1_hi{h}", [P, N], F32R) for h in two]
        x1_lo = [sb(f"x1_lo{h}", [P, N], F32R) for h in two]
        res_f = [sb(f"res_f{h}", [P, T, P]) for h in two]
        hid = [sb(f"hid{h}", [P, FF, N]) for h in two]
        stat = [sb(f"stat{i}", [P, T, 6]) for i in range(NORMS)]
        mv = [sb(f"mv{i}", [P, T, 2]) for i in range(NORMS)]
        var = [sb(f"var{i}", [P, T]) for i in range(NORMS)]
        rstd = [sb(f"rstd{i}", [P, T]) for i in range(NORMS)]
        shift = [sb(f"shift{i}", [P, T]) for i in range(NORMS)]
        r_raw = sb("r_raw", [P, EXPERTS])
        r_sc = sb("r_sc", [P, EXPERTS])
        r_hi = sb("r_hi", [P, EXPERTS], F32R)
        r_lo = sb("r_lo", [P, EXPERTS], F32R)
        r_bias = sb("r_bias", [P, EXPERTS])
        ex = sb("ex", [P, 2 * T, EXPERTS])
        rest = sb("rest", [P, 2 * T, EXPERTS])
        mx, total = sb("mx", [P, 2 * T]), sb("total", [P, 2 * T])
        key = sb("key", [P, 2 * T, EXPERTS])
        best = [sb(f"best{k}", [P, 2 * T, EXPERTS]) for k in range(2)]
        gate = sb("gate", [P, EXPERTS, HALVES * T])
        e_bias = sb("e_bias", [P, EXPERTS, FF])

        x_in = [sem(f"x_in{u}") for u in range(HALVES)]
        col_in, row_in, router_in = sem("col_in"), sem("row_in"), sem("router_in")
        raw_in = sem("raw_in")
        qkv_in, wo_in, w1_in, w2_in = sem("qkv_in"), sem("wo_in"), sem("w1_in"), sem("w2_in")
        out_done = sem("out_done")
        pool_passed, act_passed, dve_passed, sp_passed = (
            sem(n) for n in ("pool_passed", "act_passed", "dve_passed", "sp_passed"))
        const_step, const_done, rows_summed = sem("const_step"), sem("const_done"), sem("rows_summed")
        qkv_scaled, qkv_split = sem("qkv_scaled"), sem("qkv_split")
        w1_scaled, w1_split = sem("w1_scaled"), sem("w1_split")
        gain_done, gain1_done = sem("gain_done"), sem("gain1_done")
        boff_done, bias_mm, bias_done = sem("boff_done"), sem("bias_mm"), sem("bias_done")
        q_mm, kvp_mm, kvm_mm, att_mm, attt_mm = (sem(n) for n in ("q_mm", "kvp_mm", "kvm_mm", "att_mm", "attt_mm"))
        wo_mm, t1_mm, w1_mm, w2_mm, t2_mm = (sem(n) for n in ("wo_mm", "t1_mm", "w1_mm", "w2_mm", "t2_mm"))
        q_rel, q_exp, k_rel, k_exp, attt_sb = (sem(n) for n in ("q_rel", "q_exp", "k_rel", "k_exp", "attt_sb"))
        exp_table, gelu_table = sem("exp_table"), sem("gelu_table")
        x1_hi_done, hid_done, xt_hi_done = sem("x1_hi_done"), sem("hid_done"), sem("xt_hi_done")
        kt_done, v_done, qt_done, k_done, kv_done = (sem(n) for n in ("kt_done", "v_done", "qt_done", "k_done", "kv_done"))
        den_done, rec_done, att_done = sem("den_done"), sem("rec_done"), sem("att_done")
        s1_done, stat1_done, mv1_done, x1_done, x1_lo_done = (sem(n) for n in ("s1_done", "stat1_done", "mv1_done", "x1_done", "x1_lo_done"))
        s2_done, stat2_done, mv2_done, x2_done, xt_lo_done = (sem(n) for n in ("s2_done", "stat2_done", "mv2_done", "x2_done", "xt_lo_done"))
        var1_done, pow1_done, rstd1_done = sem("var1_done"), sem("pow1_done"), sem("rstd1_done")
        var2_done, pow2_done, rstd2_done = sem("var2_done"), sem("pow2_done"), sem("rstd2_done")
        resf_mul, resf_done, resa_mul, resa_done = (sem(n) for n in ("resf_mul", "resf_done", "resa_mul", "resa_done"))
        three_ = range(3)
        f_mv = [sem(f"f_mv{k}") for k in three_]
        f_var = [sem(f"f_var{k}") for k in three_]
        f_pow = [sem(f"f_pow{k}") for k in three_]
        f_rstd = [sem(f"f_rstd{k}") for k in three_]
        f_norm = [sem(f"f_norm{k}") for k in three_]
        f_stat, f_gain, f_offset, f_sum, acc_done = (sem(n) for n in ("f_stat", "f_gain", "f_offset", "f_sum", "acc_done"))
        ft_mm, xn_hi, xn_lo = sem("ft_mm"), sem("xn_hi"), sem("xn_lo")
        r_prep, rb_mm, rb_done, r_mm, r_sub, r_ex, r_step, gate_done = (
            sem(n) for n in ("r_prep", "rb_mm", "rb_done", "r_mm", "r_sub", "r_ex", "r_step", "gate_done"))
        e_scaled, e_split, eb_mm, eb_done = sem("e_scaled"), sem("e_split"), sem("eb_mm"), sem("eb_done")
        w2e_in = [sem(f"w2e_in{k}") for k in two]
        up_mm = [sem(f"up_mm{k}") for k in two]
        up_done = [sem(f"up_done{k}") for k in two]
        down_mm = [sem(f"down_mm{k}") for k in two]
        comb = [sem(f"comb{k}") for k in two]

        def first_norm(u):
            return hid[u % 2][:, u // 2, :].rearrange("p (t n) -> p t n", t=T)

        LAST = LAYERS - 1
        w1_set = [next_w1, this_w1]
        w2_set = [other_w2, this_w2]

        def final_set(k, u):
            return 4 + k * HALVES + u

        def token_major(x):
            return x[:, :].rearrange("p (t n) -> p t n", t=T)

        def outer_rows(u):
            return (ek[0][:, :, :], ek[1][:, :, :], token_major(eq[0]), token_major(eq[1]))[u % 4]

        def expert_rows(u):
            return (att[0][:, :, :], att[1][:, :, :], token_major(qt[0]), token_major(qt[1]))[u % 4]

        START_BANK = (4, 5, 6, 7, 6, 7, 4, 5)

        block = ctx.enter_context(nc.Block())

        @block.sync
        def _(sp):
            def load_raw(l):
                if not isinstance(l, int) or l > 0:
                    wait_apart(sp, qkv_split, l * 8, sp_passed)
                    wait_apart(sp, w1_scaled, l * 8, sp_passed)
                    wait_apart(sp, bias_mm, l * 8, sp_passed)
                sp.dma_start(raw_qkv[:, :], wqkv[bass.ds(l, 1)].rearrange("l p n -> (l p) n")).then_inc(raw_in, 16)
                sp.dma_start(raw_w1[:, :], w1[bass.ds(l, 1)].rearrange("l p n -> (l p) n")).then_inc(raw_in, 16)

            def set_qkv(l):
                wait_apart(sp, qkv_split, l * 8 + 8, sp_passed)
                wait_apart(sp, kvp_mm, upto(l, -1, 1), sp_passed)
                sp.dma_start(this_qkv[:, :, :].bitcast(F32), next_qkv[:, :, :].bitcast(F32)).then_inc(qkv_in, 16)

            def set_wo(l):
                wait_apart(sp, wo_mm, upto(l, -1, 1), sp_passed)
                sp.dma_start(this_wo[:, :], wo[bass.ds(l, 1)].rearrange("l p n -> (l p) n")).then_inc(wo_in, 16)

            def set_w1(l):
                wait_apart(sp, w1_split, l * 8 + 8, sp_passed)
                wait_apart(sp, w1_mm, upto(l, -1, 1, per=FF), sp_passed)
                sp.dma_start(this_w1[:, :, :].bitcast(F32), next_w1[:, :, :].bitcast(F32)).then_inc(w1_in, 16)

            def set_w2(l):
                wait_apart(sp, w2_mm, upto(l, -1, 1), sp_passed)
                sp.dma_start(this_w2[:, :, :],
                             w2[bass.ds(l, 1)].rearrange("l (c p) n -> (l p) c n", p=P)).then_inc(w2_in, 16)

            def load_rows(l):
                wait_apart(sp, rows_summed, l * 8, sp_passed)
                sp.dma_start(row[:, bass.ds(l, 1)].rearrange("p l r n -> p (l r n)"),
                             rows[bass.ds(l, 1)].rearrange("l n -> (l n)").partition_broadcast(P)).then_inc(row_in, 16)

            sp.dma_start(x_all[:, 0], x[0]).then_inc(x_in[0], 16)
            sp.dma_start(col[:, :], cols).then_inc(col_in, 16)
            load_raw(0)
            sp.dma_start(x_all[:, 1], x[1]).then_inc(x_in[1], 16)
            load_rows(0)
            for u in range(2, HALVES):
                sp.dma_start(x_all[:, u], x[u]).then_inc(x_in[u], 16)
            sp.dma_start(r_raw[:, :], router).then_inc(router_in, 16)
            set_wo(0)

            def layer(l, last=False):
                if not last:
                    load_raw(l + 1)
                load_rows(l + 1)
                set_w1(l)
                set_w2(l)
                if not last:
                    set_qkv(l + 1)
                    set_wo(l + 1)

            layer(0)
            with sp.Fori(1, LAST) as l:
                layer(l)
            layer(LAST, last=True)

            for e in range(EXPERTS):
                if e == 0:
                    wait(sp, w1_scaled, LAYERS * 8)
                    wait(sp, bias_mm, LAYERS * 8)
                else:
                    wait(sp, e_scaled, e)
                    wait(sp, eb_mm, e)
                sp.dma_start(raw_w1[:, :], w1[LAYERS + e]).then_inc(raw_in, 16)
                if e == 1:
                    wait(sp, w2_mm, upto(LAST, SLOTS - 1, 1))
                if e >= 2:
                    wait(sp, down_mm[e % 2], HALVES * (e // 2))
                sp.dma_start(w2_set[e % 2][:, :, :],
                             w2[LAYERS + e].rearrange("(c p) n -> p c n", p=P)).then_inc(w2e_in[e % 2], 16)
            for u in range(HALVES):
                wait(sp, comb[1], HALVES * (EXPERTS // 2 - 1) + u + 1)
                sp.dma_start(out[u], res_a[:, u]).then_inc(out_done, 16)
            sp.wait_ge(out_done, 16 * HALVES)

        @block.gpsimd
        def _(pool):
            g = nc.gpsimd
            g.memset(ident[:, :], 0.0).then_inc(const_step, 1)
            g.memset(mask[:, :], 1.0).then_inc(const_step, 1)
            g.memset(order[:, :], 1.0).then_inc(const_step, 1)
            g.memset(ones[:, :], 1.0).then_inc(const_step, 1)
            g.memset(neg_half[:, :], -0.5).then_inc(const_step, 1)
            for h in two:
                g.memset(v[h][:, :, P:VW], 1.0).then_inc(const_step, 1)
            pool.wait_ge(const_step, 7)
            g.affine_select(out=ident[:, :], in_=ident[:, :], compare_op=ALU.not_equal, fill=1.0, base=0,
                            pattern=[[-1, P]], channel_multiplier=1).then_inc(const_step, 1)
            same = mask[:, 0:P].rearrange("p (a b) -> p a b", b=HEAD)
            g.affine_select(out=same, in_=same, compare_op=ALU.is_ge, fill=0.0, base=0,
                            pattern=[[-HEAD, HEADS], [0, HEAD]], channel_multiplier=1).then_inc(const_step, 1)
            memb = mask[:, P:KVW]
            g.affine_select(out=memb, in_=memb, compare_op=ALU.is_ge, fill=0.0, base=0,
                            pattern=[[-HEAD, HEADS]], channel_multiplier=1).then_inc(const_step, 1)
            pool.wait_ge(const_step, 10)
            g.affine_select(out=same, in_=same, compare_op=ALU.is_ge, fill=0.0, base=HEAD - 1,
                            pattern=[[HEAD, HEADS], [0, HEAD]], channel_multiplier=-1).then_inc(const_step, 1)
            g.affine_select(out=memb, in_=memb, compare_op=ALU.is_ge, fill=0.0, base=HEAD - 1,
                            pattern=[[HEAD, HEADS]], channel_multiplier=-1).then_inc(const_step, 1)
            for e in range(EXPERTS):
                ins = g.memset(order[:, e:e + 1], float(EXPERTS - e))
            ins.then_inc(const_step, 1)
            pool.wait_ge(const_step, 13)
            g.memset(var[0][:, :], 0.0).then_inc(const_done, 1)

            def scale_qkv(l):
                wait_apart(pool, raw_in, l * 32 + 32, pool_passed)
                if not isinstance(l, int) or l > 1:
                    wait_apart(pool, qkv_split, l * 8, pool_passed)
                wait_apart(pool, boff_done, l * 8, pool_passed)
                g.tensor_copy(gain[:, 0:1], col[:, bass.ds(l + C_GIN, 1)]).then_inc(gain_done, 4)
                g.tensor_copy(gain[:, 1:2], col[:, bass.ds(l + C_BIN, 1)]).then_inc(gain_done, 4)
                wait_apart(pool, gain_done, l * 8 + 8, pool_passed)
                if not isinstance(l, int) or l > 0:
                    g.tensor_scalar(scaled_qkv[:, :], raw_qkv[:, :], gain[:, 0:1], 0.0,
                                    ALU.mult, ALU.add).then_inc(qkv_scaled, 8)
                wait_apart(pool, bias_mm, l * 8, pool_passed)
                g.tensor_scalar(boff[:, :], ones[:, :], gain[:, 1:2], 0.0,
                                ALU.mult, ALU.add).then_inc(boff_done, 8)

            def split_qkv(l):
                wait_apart(pool, qkv_scaled, l * 8, pool_passed)
                wait_apart(pool, qkv_in, l * 16 - 16, pool_passed)
                g.tensor_scalar(next_qkv[:, 0, :], scaled_qkv[:, :], 1.0, 0.0, ALU.mult, ALU.add).then_inc(qkv_split, 4)
                wait_apart(pool, qkv_split, l * 8 + 4, pool_passed)
                g.tensor_tensor(next_qkv[:, 1, :], scaled_qkv[:, :], next_qkv[:, 0, :].bitcast(F32),
                                ALU.subtract).then_inc(qkv_split, 4)

            def scale_w1(l):
                wait_apart(pool, raw_in, l * 32 + 32, pool_passed)
                wait_apart(pool, w1_split, l * 8, pool_passed)
                g.tensor_copy(gain1[:, :], col[:, bass.ds(l + C_G1, 1)]).then_inc(gain1_done, 8)
                wait_apart(pool, gain1_done, l * 8 + 8, pool_passed)
                g.tensor_scalar(scaled_w1[:, :], raw_w1[:, :], gain1[:, :], 0.0,
                                ALU.mult, ALU.add).then_inc(w1_scaled, 8)

            def hi_w1(l):
                wait_apart(pool, w1_scaled, l * 8 + 8, pool_passed)
                wait_apart(pool, w1_in, l * 16, pool_passed)
                g.tensor_scalar(next_w1[:, 0, :], scaled_w1[:, :], 1.0, 0.0, ALU.mult, ALU.add).then_inc(w1_split, 4)

            def lo_w1(l):
                wait_apart(pool, w1_split, l * 8 + 4, pool_passed)
                g.tensor_tensor(next_w1[:, 1, :], scaled_w1[:, :], next_w1[:, 0, :].bitcast(F32),
                                ALU.subtract).then_inc(w1_split, 4)

            def inv_std(i, mvs, var_sem, pow_sem, rstd_sem, count, used=None, previous=0):
                wait_apart(pool, used, previous, pool_passed)
                wait_apart(pool, mvs, count, pool_passed)
                g.tensor_scalar(shift[i][:, :], mv[i][:, :, 0], -1.0, 0.0, ALU.mult, ALU.add)
                g.tensor_scalar(var[i][:, :], mv[i][:, :, 1], 1.0, EPS, ALU.mult, ALU.add).then_inc(var_sem, 1)
                wait_apart(pool, var_sem, count, pool_passed)
                g.tensor_tensor(rstd[i][:, :], var[i][:, :], neg_half[:, :], ALU.pow).then_inc(pow_sem, 1)
                wait_apart(pool, pow_sem, count, pool_passed)
                g.tensor_tensor(shift[i][:, :], shift[i][:, :], rstd[i][:, :], ALU.mult).then_inc(rstd_sem, 1)

            def inv_std1(l, s, h):
                inv_std(h, mv1_done, var1_done, pow1_done, rstd1_done, upto(l, s, h), x1_done, upto(l, s - 1, h))

            def inv_std2(l, s, h):
                inv_std(2 + h, mv2_done, var2_done, pow2_done, rstd2_done, upto(l, s, h, base=8),
                        x2_done, upto(l, s - 1, h, base=8))

            def rows_of(kind, l):
                return row[:, bass.ds(l, 1), kind, :].to_broadcast([P, T, P])

            def sum_rows(l):
                wait(pool, row_in, l * 16 + 16)
                for kind, other in ((R_BIN, R_BO), (R_B1, R_C2)):
                    r = row[:, bass.ds(l, 1), kind, :]
                    if not isinstance(l, int):
                        pool.sem_inc(pool_passed, 1)
                    g.tensor_tensor(r, r, row[:, bass.ds(l, 1), other, :], ALU.add).then_inc(rows_summed, 4)

            def resid_f(l, s, h, lw):
                wait_apart(pool, x1_done, upto(l, s, h), pool_passed)
                wait_apart(pool, s2_done, upto(l, s - 1, h), pool_passed)
                g.tensor_tensor(res_f[h][:, :, :], s1[h][:, :, :], rows_of(R_G1, lw), ALU.mult).then_inc(resf_mul, 1)
                wait_apart(pool, resf_mul, upto(l, s, h), pool_passed)
                g.tensor_tensor(res_f[h][:, :, :], res_f[h][:, :, :], rows_of(R_B1, lw), ALU.add).then_inc(resf_done, 1)

            def resid_a(l, s, h, lw):
                scale_resid(l, s, h, lw)
                offset_resid(l, s, h, lw)

            def scale_resid(l, s, h, lw):
                u = (2 * s + h) % HALVES
                wait_apart(pool, x2_done, upto(l, s, h, base=8), pool_passed)
                wait_apart(pool, s1_done, upto(l, s, h), pool_passed)
                g.tensor_tensor(res_a[:, u], s2[h][:, :, :], rows_of(R_GIN, lw), ALU.mult).then_inc(resa_mul, 1)

            def offset_resid(l, s, h, lw):
                u = (2 * s + h) % HALVES
                wait_apart(pool, resa_mul, upto(l, s, h), pool_passed)
                g.tensor_tensor(res_a[:, u], res_a[:, u], rows_of(R_BIN, lw), ALU.add).then_inc(resa_done, 1)

            def prep_router():
                pool.wait_ge(router_in, 16)
                g.tensor_scalar(r_sc[:, :], r_raw[:, :], col[:, C_GAMMA:C_GAMMA + 1], 0.0, ALU.mult, ALU.add).then_inc(r_prep, 1)
                pool.wait_ge(r_prep, 1)
                g.tensor_scalar(r_hi[:, :], r_sc[:, :], 1.0, 0.0, ALU.mult, ALU.add).then_inc(r_prep, 1)
                pool.wait_ge(r_prep, 2)
                g.tensor_tensor(r_lo[:, :], r_sc[:, :], r_hi[:, :].bitcast(F32), ALU.subtract).then_inc(r_prep, 1)
                wait(pool, bias_mm, LAYERS * 8)
                wait(pool, boff_done, LAYERS * 8)
                g.tensor_scalar(boff[:, :], ones[:, :], col[:, C_BETA:C_BETA + 1], 0.0, ALU.mult, ALU.add).then_inc(r_prep, 1)

            def scale_expert(e):
                wait(pool, raw_in, 32 * LAYERS + 16 * (e + 1))
                wait(pool, w1_split, LAYERS * 8)
                wait(pool, e_split, 2 * e)
                g.tensor_scalar(scaled_w1[:, :], raw_w1[:, :], col[:, C_GAMMA:C_GAMMA + 1], 0.0,
                                ALU.mult, ALU.add).then_inc(e_scaled, 1)

            def split_expert(e):
                dst = w1_set[e % 2]
                wait(pool, e_scaled, e + 1)
                if e == 0:
                    wait(pool, w1_in, LAYERS * 16)
                elif e == 1:
                    wait(pool, w1_mm, upto(LAST, SLOTS - 1, 1, per=FF))
                else:
                    wait(pool, up_mm[e % 2], FF * HALVES * (e // 2))
                g.tensor_scalar(dst[:, 0, :], scaled_w1[:, :], 1.0, 0.0, ALU.mult, ALU.add).then_inc(e_split, 1)
                wait(pool, e_split, 2 * e + 1)
                g.tensor_tensor(dst[:, 1, :], scaled_w1[:, :], dst[:, 0, :].bitcast(F32),
                                ALU.subtract).then_inc(e_split, 1)

            def start(u):
                inv_std(2 + u, mv2_done, var2_done, pow2_done, rstd2_done, u + 1)

            def start_resid(u):
                pool.wait_ge(x2_done, u + 1)
                g.tensor_tensor(res_a[:, u], first_norm(u), rows_of(R_BIN, 0), ALU.add).then_inc(resa_done, 1)

            start(0)
            pool.wait_ge(col_in, 16)
            scale_qkv(0)
            start(1)
            start(2)
            start(3)
            scale_w1(0)
            for u in range(4, HALVES):
                start(u)
            hi_w1(0)
            lo_w1(0)
            sum_rows(0)
            wait(pool, rows_summed, 8)
            for u in range(HALVES // 2):
                start_resid(u)

            def final_inv(k, u):
                i = final_set(k, u)
                pool.wait_ge(f_mv[k], u + 1)
                if k > 0:
                    g.tensor_scalar(shift[i][:, :], mv[i][:, :, 0], -1.0, 0.0, ALU.mult, ALU.add)
                g.tensor_scalar(var[i][:, :], mv[i][:, :, 1], 1.0, EPS, ALU.mult, ALU.add).then_inc(f_var[k], 1)
                pool.wait_ge(f_var[k], u + 1)
                g.tensor_tensor(rstd[i][:, :], var[i][:, :], neg_half[:, :],
                                ALU.pow).then_inc(f_pow[k] if k > 0 else f_rstd[k], 1)
                if k > 0:
                    pool.wait_ge(f_pow[k], u + 1)
                    g.tensor_tensor(shift[i][:, :], shift[i][:, :], rstd[i][:, :], ALU.mult).then_inc(f_rstd[k], 1)

            def offset_input(u):
                g.tensor_tensor(x_all[:, u], x_all[:, u], row[:, LAYERS, R_B1:R_B1 + 1, :].to_broadcast([P, T, P]),
                                ALU.add).then_inc(f_offset, 1)

            def slot(l, s, first, last):
                p1, p2 = not first or s >= 1, not first or s >= 2
                lw1 = l if s >= 1 else l - 1
                lw2 = l if s >= 2 else l - 1
                if p1:
                    inv_std1(l, s - 1, 0)
                    inv_std1(l, s - 1, 1)
                    if first and s == 1:
                        for u in range(HALVES // 2, HALVES):
                            start_resid(u)
                    resid_f(l, s - 1, 0, lw1)
                    resid_f(l, s - 1, 1, lw1)
                if s == 1:
                    if not last:
                        scale_qkv(l + 1)
                    else:
                        prep_router()
                elif s == 2:
                    if not last:
                        scale_w1(l + 1)
                    else:
                        scale_expert(0)
                elif s == 3 and not last:
                    lo_w1(l + 1)
                if p2:
                    inv_std2(l, s - 2, 0)
                    scale_resid(l, s - 2, 0, lw2 + 1)
                    inv_std2(l, s - 2, 1)
                    offset_resid(l, s - 2, 0, lw2 + 1)
                    resid_a(l, s - 2, 1, lw2 + 1)
                if s == 0:
                    sum_rows(l + 1)
                elif s == 1:
                    wait_apart(pool, rows_summed, l * 8 + 16, pool_passed)
                    if not last:
                        split_qkv(l + 1)
                elif s == 2:
                    if not last:
                        hi_w1(l + 1)
                    else:
                        split_expert(0)
                if last and s >= 1:
                    offset_input(s - 1)
                if last and s == 3:
                    final_inv(0, 0)
                    final_inv(0, 1)

            for s in range(SLOTS):
                slot(0, s, True, False)
            with pool.Fori(1, LAST) as l:
                for s in range(SLOTS):
                    slot(l, s, False, False)
            for s in range(SLOTS):
                slot(LAST, s, False, True)

            def start_output(u):
                pool.wait_ge(f_norm[1], u + 1)
                g.tensor_tensor(res_a[:, u], x_all[:, u], outer_rows(u), ALU.add).then_inc(acc_done, 1)

            inv_std1(LAST, 3, 0)
            inv_std1(LAST, 3, 1)
            final_inv(1, 0)
            resid_f(LAST, 3, 0, LAST)
            scale_expert(1)
            inv_std2(LAST, 2, 0)
            final_inv(2, 0)
            final_inv(1, 1)
            scale_resid(LAST, 2, 0, LAYERS)
            resid_f(LAST, 3, 1, LAST)
            split_expert(1)
            final_inv(2, 1)
            final_inv(0, 2)
            final_inv(0, 3)
            inv_std2(LAST, 2, 1)
            offset_input(3)
            offset_resid(LAST, 2, 0, LAYERS)
            final_inv(1, 2)
            resid_a(LAST, 2, 1, LAYERS)
            final_inv(1, 3)
            final_inv(2, 2)
            inv_std2(LAST, 3, 0)
            inv_std2(LAST, 3, 1)
            offset_input(4)
            final_inv(0, 4)
            start_output(0)
            final_inv(2, 3)
            start_output(1)
            offset_input(5)
            final_inv(0, 5)
            resid_a(LAST, 3, 0, LAYERS)
            final_inv(1, 4)
            resid_a(LAST, 3, 1, LAYERS)
            final_inv(2, 4)
            start_output(2)
            start_output(3)
            start_output(4)
            for u in range(2, HALVES):
                if u >= 2 and u + 4 < HALVES:
                    offset_input(u + 4)
                    final_inv(0, u + 4)
                if u + 3 < HALVES:
                    final_inv(1, u + 3)
                    final_inv(2, u + 3)
                    start_output(u + 3)
                if u == 3:
                    scale_expert(2)
            split_expert(2)
            for e in range(3, EXPERTS):
                scale_expert(e)
                split_expert(e)

        @block.scalar
        def _(act):
            a = nc.scalar

            def load_table(func, column, loaded, count):
                wait(act, loaded, count)
                a.activation(warm[:, column:column + 1], ones[:, 0:1], func).then_inc(loaded, 1)

            def phi_q(l, s, h):
                if s == 0 and h == 0:
                    wait(act, bias_done, l * 8 + 8)
                wait(act, q_mm, upto(l, s, h))
                wait_apart(act, qt_done, upto(l, s - 1, h), act_passed)
                a.activation(eq[h][:, :], ps(3 * h), ACT.Relu, bias=bq_neg[:, bass.ds(l, 1)], scale=-1.0).then_inc(q_rel, 1)
                wait(act, q_rel, upto(l, s, h))
                a.activation(eq[h][:, :], eq[h][:, :], ACT.Exp, scale=-1.0).then_inc(q_exp, 1)

            def phi_k(l, s, h):
                wait(act, kt_done, upto(l, s, h))
                wait(act, k_done, upto(l, s - 1, h))
                a.activation(ek[h][:, :, :], kt[h][:, :, :], ACT.Relu, scale=-1.0).then_inc(k_rel, 1)
                wait(act, k_rel, upto(l, s, h))
                a.activation(ek[h][:, :, :], ek[h][:, :, :], ACT.Exp, scale=-1.0).then_inc(k_exp, 1)

            def split_x1(l, s, h):
                wait(act, t1_mm, upto(l, s, h))
                wait(act, w1_mm, upto(l, s - 1, h, per=FF))
                a.activation(x1_hi[h][:, :], ps(7 if h == 0 else 0), ACT.Copy).then_inc(x1_hi_done, 1)

            def gelu(l, s, h, lw):
                if isinstance(l, int) and l == 0:
                    wait(act, resa_done, HALVES)
                for c in range(FF):
                    if c == 0:
                        wait(act, w2_mm, upto(l, s - 1, h))
                    wait_apart(act, w1_mm, upto(l, s, h, per=FF) - (FF - 1 - c), act_passed)
                    a.activation(hid[h][:, c, :], ps(3 + h + c), ACT.Gelu,
                                 bias=col[:, bass.ds(lw * FF + (C_C1 + c), 1)]).then_inc(hid_done, 1)

            def copy_att(l, s, h):
                wait(act, attt_mm, upto(l, s, h))
                wait(act, wo_mm, upto(l, s - 1, h))
                a.activation(att_t[h][:, :], ps(2 * h), ACT.Copy).then_inc(attt_sb, 1)

            def split_xt(l, s, h, b=None):
                u = (2 * s + h) % HALVES
                wait(act, t2_mm, upto(l, s, h, base=8))
                wait(act, kvp_mm, upto(l, s, h))
                a.activation(xt_hi[:, u], ps(4 + h if b is None else b), ACT.Copy).then_inc(xt_hi_done, 1)

            def scale_rows(i, src, dst, tile_sem):
                for t in range(T):
                    ins = a.activation(dst[:, t, :], src[:, t, :], ACT.Identity, bias=shift[i][:, t:t + 1],
                                       scale=rstd[i][:, t:t + 1])
                ins.then_inc(tile_sem, 1)

            def norm1(l, s, h):
                wait(act, rstd1_done, upto(l, s, h))
                scale_rows(h, s1[h], s1[h], x1_done)

            def norm2(l, s, h):
                wait(act, rstd2_done, upto(l, s, h, base=8))
                scale_rows(2 + h, s2[h], s2[h], x2_done)

            def start(u):
                act.wait_ge(rstd2_done, u + 1)
                scale_rows(2 + u, x_all[:, u], first_norm(u), x2_done)

            def start_split(u):
                split_xt(-1, u // 2, u % 2, b=START_BANK[u])

            act.wait_ge(raw_in, 32)
            a.activation(this_qkv[:, 0, :], raw_qkv[:, :], ACT.Copy).then_inc(qkv_split, 4)
            start(0)
            start(1)
            start_split(0)
            start_split(1)
            start(2)
            start(3)

            def slot(l, s, first, last):
                p1, p2 = not first or s >= 1, not first or s >= 2
                lw = l if s >= 1 else l - 1
                phi_q(l, s, 0)
                phi_k(l, s, 0)
                if p1:
                    norm1(l, s - 1, 0)
                phi_q(l, s, 1)
                if p1:
                    split_x1(l, s - 1, 0)
                    norm1(l, s - 1, 1)
                phi_k(l, s, 1)
                if first and s == 0:
                    start_split(2)
                    start_split(3)
                    for u in range(4, HALVES):
                        start(u)
                    start_split(4)
                    start_split(5)
                if p1:
                    load_table(ACT.Gelu, 0, gelu_table, l * SLOTS + (s - 1))
                    split_x1(l, s - 1, 1)
                    gelu(l, s - 1, 0, lw)
                if p2:
                    norm2(l, s - 2, 0)
                if p1:
                    gelu(l, s - 1, 1, lw)
                copy_att(l, s, 0)
                copy_att(l, s, 1)
                if p2:
                    if not (last and s >= 2):
                        split_xt(l, s - 2, 0)
                    norm2(l, s - 2, 1)
                load_table(ACT.Exp, 1, exp_table, l * SLOTS + s)
                if p2 and not (last and s >= 2):
                    split_xt(l, s - 2, 1)
                if first and s == 0:
                    start_split(6)
                    start_split(7)

            act.wait_ge(const_done, 1)
            for s in range(SLOTS):
                slot(0, s, True, False)
            with act.Fori(1, LAST) as l:
                for s in range(SLOTS):
                    slot(l, s, False, False)
            for s in range(SLOTS):
                slot(LAST, s, False, True)

            def sum_norm(u):
                act.wait_ge(f_rstd[1], u + 1)
                wait(act, acc_done, u - 3)
                wait(act, f_mv[2], u - 3)
                scale_rows(final_set(1, u), x_all[:, u], outer_rows(u), f_norm[1])

            def expert_norm(u):
                act.wait_ge(f_rstd[2], u + 1)
                act.wait_ge(f_norm[1], u + 1)
                wait(act, ft_mm, u - 3)
                scale_rows(final_set(2, u), outer_rows(u), expert_rows(u), f_norm[2])

            def split_rows(u):
                act.wait_ge(ft_mm, u + 1)
                a.activation(xt_hi[:, u], ps(7), ACT.Copy).then_inc(xn_hi, 1)

            def silu(r, k, u, buf):
                for c in range(FF):
                    wait_apart(act, up_mm[k], r * (FF * HALVES) + (FF * u + c + 1), act_passed)
                    a.activation(hid[buf][:, c, :], ps(c), ACT.Silu,
                                 bias=e_bias[:, bass.ds(r * 2 + k, 1), c]).then_inc(up_done[k], 1)

            norm1(LAST, 3, 0)
            norm1(LAST, 3, 1)
            split_x1(LAST, 3, 0)
            split_x1(LAST, 3, 1)
            sum_norm(0)
            gelu(LAST, 3, 0, LAST)
            norm2(LAST, 2, 0)
            gelu(LAST, 3, 1, LAST)
            expert_norm(0)
            sum_norm(1)
            split_rows(0)
            expert_norm(1)

            def exponentials(p):
                act.wait_ge(r_sub, p + 1)
                a.activation(ex[:, :, :], ex[:, :, :], ACT.Exp, scale=INV_TEMP).then_inc(r_ex, 1)

            act.wait_ge(eb_done, 1)
            wait(act, w2_mm, upto(LAST, 3, 1))
            silu(0, 0, 0, 0)
            norm2(LAST, 2, 1)
            split_rows(1)
            act.wait_ge(eb_done, 2)
            silu(0, 1, 0, 1)
            sum_norm(2)
            sum_norm(3)
            expert_norm(2)
            exponentials(0)
            norm2(LAST, 3, 0)
            norm2(LAST, 3, 1)
            act.wait_ge(down_mm[0], 1)
            silu(0, 0, 1, 0)
            split_rows(2)
            expert_norm(3)
            act.wait_ge(down_mm[1], 1)
            silu(0, 1, 1, 1)
            split_rows(3)
            sum_norm(4)
            for u in range(2, HALVES):
                if u % 2 == 0:
                    exponentials(u // 2)
                if u + 2 < HALVES:
                    expert_norm(u + 2)
                act.wait_ge(down_mm[0], u)
                silu(0, 0, u, 0)
                act.wait_ge(down_mm[1], u)
                silu(0, 1, u, 1)
                if u + 2 < HALVES:
                    split_rows(u + 2)
                if u + 3 < HALVES:
                    sum_norm(u + 3)

            def silu_sweep(r, k):
                wait(act, eb_done, r * 2 + (k + 1))
                before = (lambda n: r * HALVES + (n - HALVES)) if k == 0 else (lambda n: r * HALVES + n)
                for u in range(HALVES):
                    if u == 0 and k == 0:
                        wait(act, down_mm[0], r * HALVES)
                    if u < 2:
                        wait(act, down_mm[1 - k], before(HALVES - 1 + u))
                    else:
                        wait(act, down_mm[k], r * HALVES + (u - 1))
                    silu(r, k, u, u % 2)

            with act.Fori(1, EXPERTS // 2) as r:
                silu_sweep(r, 0)
                silu_sweep(r, 1)

        @block.vector
        def _(dve):
            d = nc.vector
            stats = [0]

            def moments(i, src, stats, mvs, count):
                for t in range(T):
                    ins = d.bn_stats(stat[i][:, t, :], src[:, t, :])
                ins.then_inc(stats, 1)
                wait_apart(dve, stats, count, dve_passed)
                for t in range(T):
                    ins = d.bn_aggr(mv[i][:, t, :], stat[i][:, t, :])
                ins.then_inc(mvs, 1)

            def keys_values(l, s, h):
                wait(dve, kvp_mm, upto(l, s, h))
                wait(dve, kvm_mm, upto(l, s - 1, h))
                for half in two:
                    b = (1, 4)[h] + half
                    src = ps(b).rearrange("p (t n) -> p t n", t=2)
                    bias = row[:, bass.ds(l, 1), R_BK:R_BK + 2, :]
                    ins = d.tensor_tensor(kt[h][:, 2 * half:2 * half + 2, :], src[:, :, 0:P],
                                          bias[:, 0, 0:1, :].to_broadcast([P, 2, P]), ALU.add)
                ins.then_inc(kt_done, 1)
                for half in two:
                    b = (1, 4)[h] + half
                    src = ps(b).rearrange("p (t n) -> p t n", t=2)
                    bias = row[:, bass.ds(l, 1), R_BK:R_BK + 2, :]
                    ins = d.tensor_tensor(v[h][:, 2 * half:2 * half + 2, 0:P], src[:, :, P:2 * P],
                                          bias[:, 0, 1:2, :].to_broadcast([P, 2, P]), ALU.add)
                ins.then_inc(v_done, 1)

            def queries(l, s, h):
                wait(dve, q_exp, upto(l, s, h))
                wait(dve, att_mm, upto(l, s - 1, h))
                d.scalar_tensor_tensor(out=qt[h][:, :], in0=ps(3 * h), scalar=bq_one[:, bass.ds(l, 1)],
                                       in1=eq[h][:, :], op0=ALU.add, op1=ALU.max).then_inc(qt_done, 1)

            def keys(l, s, h):
                wait(dve, k_exp, upto(l, s, h))
                d.scalar_tensor_tensor(out=kt[h][:, :, :], in0=kt[h][:, :, :], scalar=1.0,
                                       in1=ek[h][:, :, :], op0=ALU.add, op1=ALU.max).then_inc(k_done, 1)

            def mask_kv(l, s, h):
                wait(dve, kvm_mm, upto(l, s, h))
                wait(dve, att_mm, upto(l, s - 1, h))
                src = ps(1 + h).rearrange("p (q n) -> p q n", q=2)
                d.tensor_tensor(kv[h][:, :, 0:P], src[:, :, 0:P],
                                mask[:, 0:P].unsqueeze(1).to_broadcast([P, 2, P]), ALU.mult)
                for q in two:
                    ins = d.tensor_scalar(kv[h][:, q, P:KVW], mask[:, P:KVW], src[:, q, P:P + 1], None, ALU.mult)
                ins.then_inc(kv_done, 1)

            def attend(l, s, h):
                wait(dve, att_mm, upto(l, s, h))
                wait(dve, attt_mm, upto(l, s - 1, h))
                src = bank[h][:, :, 0:2 * KVW].rearrange("p b (t n) -> p b t n", t=2)
                d.tensor_scalar(den[h][:, :, :].rearrange("p (b t) c -> p b t c", b=2), src[:, :, :, P:KVW], DEN_EPS, None,
                                ALU.add).then_inc(den_done, 1)
                wait(dve, den_done, upto(l, s, h))
                d.reciprocal(rec[h][:, :, :], den[h][:, :, :]).then_inc(rec_done, 1)
                wait(dve, rec_done, upto(l, s, h))
                for b in two:
                    ins = d.tensor_tensor(
                        att[h][:, 2 * b:2 * b + 2, :].rearrange("p t (a c) -> p t a c", c=HEAD),
                        src[:, b, :, 0:P].rearrange("p t (a c) -> p t a c", c=HEAD),
                        rec[h][:, 2 * b:2 * b + 2, :].unsqueeze(3).to_broadcast([P, 2, HEADS, HEAD]), ALU.mult)
                ins.then_inc(att_done, 1)

            def add_res1(l, s, h):
                u = (2 * s + h) % HALVES
                wait(dve, wo_mm, upto(l, s, h))
                wait(dve, resa_done, upto(l, s, h))
                wait(dve, t1_mm, upto(l, s - 1, h))
                wait(dve, resf_mul, upto(l, s - 1, h))
                d.tensor_tensor(s1[h][:, :, :], ps(7 - h).rearrange("p (t n) -> p t n", t=T), res_a[:, u],
                                ALU.add).then_inc(s1_done, 1)

            def moments1(l, s, h):
                wait(dve, s1_done, upto(l, s, h))
                wait(dve, rstd1_done, upto(l, s - 1, h))
                moments(h, s1[h], stat1_done, mv1_done, upto(l, s, h))

            def lo_x1(l, s, h):
                wait(dve, x1_hi_done, upto(l, s, h))
                wait(dve, w1_mm, upto(l, s - 1, h, per=FF))
                d.tensor_tensor(x1_lo[h][:, :], ps(7 if h == 0 else 0), x1_hi[h][:, :].bitcast(F32),
                                ALU.subtract).then_inc(x1_lo_done, 1)

            def add_res2(l, s, h, last=False):
                wait(dve, w2_mm, upto(l, s, h))
                wait(dve, resf_done, upto(l, s, h))
                if not (last and s >= 1):
                    wait(dve, t2_mm, upto(l, s - 1, h, base=8))
                wait(dve, resa_mul, upto(l, s - 1, h))
                d.tensor_tensor(s2[h][:, :, :], ps(3 if h == 0 else 6).rearrange("p (t n) -> p t n", t=T),
                                res_f[h][:, :, :], ALU.add).then_inc(s2_done, 1)

            def moments2(l, s, h):
                wait(dve, s2_done, upto(l, s, h))
                wait(dve, rstd2_done, upto(l, s - 1, h, base=8))
                moments(2 + h, s2[h], stat2_done, mv2_done, upto(l, s, h, base=8))

            def lo_xt(l, s, h, b=None):
                u = (2 * s + h) % HALVES
                wait(dve, xt_hi_done, upto(l, s, h, base=8))
                d.tensor_tensor(xt_lo[:, u], ps(4 + h if b is None else b), xt_hi[:, u].bitcast(F32), ALU.subtract).then_inc(xt_lo_done, 1)

            def biases(l):
                wait(dve, bias_mm, l * 8 + 8)
                wait(dve, row_in, l * 16 + 16)
                b = ps(1)
                kvb = row[:, bass.ds(l, 1), R_BK:R_BK + 2, :].rearrange("p l a n -> p (l a) n")
                bq = col[:, bass.ds(l + C_BQ, 1)]
                c1 = col[:, bass.ds(l * FF + C_C1, FF)]
                d.tensor_tensor(kvb, b[:, 0:2 * P].rearrange("p (a b) -> p a b", a=2), kvb, ALU.add)
                d.scalar_tensor_tensor(out=bq_neg[:, bass.ds(l, 1)], in0=b[:, 256:257], scalar=-1.0, in1=bq,
                                       op0=ALU.mult, op1=ALU.subtract)
                d.scalar_tensor_tensor(out=bq_one[:, bass.ds(l, 1)], in0=b[:, 256:257], scalar=1.0, in1=bq,
                                       op0=ALU.add, op1=ALU.add)
                d.tensor_tensor(c1, b[:, 260:260 + FF], c1, ALU.add).then_inc(bias_done, 8)

            def start(u):
                dve.wait_ge(x_in[u], 16)
                moments(2 + u, x_all[:, u], stat2_done, mv2_done, u + 1)

            def start_lo(u):
                lo_xt(-1, u // 2, u % 2, b=START_BANK[u])

            start(0)
            start(1)
            dve.wait_ge(qkv_split, 4)
            d.tensor_tensor(this_qkv[:, 1, :], raw_qkv[:, :], this_qkv[:, 0, :].bitcast(F32),
                            ALU.subtract).then_inc(qkv_split, 4)
            start(2)
            start(3)
            start_lo(0)
            start_lo(1)
            biases(0)
            start(4)
            start(5)
            start(6)

            def final_moments(k, u, src):
                i = final_set(k, u)
                for t in range(T):
                    ins = d.bn_stats(stat[i][:, t, :], src[:, t, :])
                stats[0] += 1
                ins.then_inc(f_stat, 1)
                dve.wait_ge(f_stat, stats[0])
                for t in range(T):
                    ins = d.bn_aggr(mv[i][:, t, :], stat[i][:, t, :])
                ins.then_inc(f_mv[k], 1)

            def stack_moments(u):
                wait(dve, resa_done, upto(LAST, 0, u, base=8))
                final_moments(0, u, res_a[:, u])

            def slot(l, s, first, last):
                p1, p2 = not first or s >= 1, not first or s >= 2
                if s == 0:
                    wait(dve, bias_done, l * 8 + 8)
                keys_values(l, s, 0)
                if p1:
                    moments1(l, s - 1, 1)
                queries(l, s, 0)
                keys(l, s, 0)
                keys_values(l, s, 1)
                queries(l, s, 1)
                if p1:
                    lo_x1(l, s - 1, 0)
                if p2:
                    add_res2(l, s - 2, 1, last)
                mask_kv(l, s, 0)
                keys(l, s, 1)
                if first and s == 0:
                    start(7)
                if p2:
                    moments2(l, s - 2, 0)
                if p1:
                    lo_x1(l, s - 1, 1)
                if first and s == 0:
                    start_lo(2)
                    start_lo(3)
                mask_kv(l, s, 1)
                attend(l, s, 0)
                attend(l, s, 1)
                if first and s == 0:
                    start_lo(4)
                    start_lo(5)
                if p2:
                    moments2(l, s - 2, 1)
                if s == 2 and not last:
                    biases(l + 1)
                if s == 2 and last:
                    dve.wait_ge(rb_mm, 1)
                    dve.wait_ge(eb_mm, 1)
                    d.tensor_copy(r_bias[:, :], ps(1)[:, 0:EXPERTS]).then_inc(rb_done, 1)
                    d.tensor_copy(e_bias[:, 0, :], ps(1)[:, 260:260 + FF]).then_inc(eb_done, 1)
                if last and s == 3:
                    stack_moments(0)
                    stack_moments(1)
                if p2 and not (last and s >= 2):
                    lo_xt(l, s - 2, 0)
                if p1:
                    add_res2(l, s - 1, 0, last)
                add_res1(l, s, 0)
                add_res1(l, s, 1)
                moments1(l, s, 0)
                if first and s == 0:
                    start_lo(6)
                    start_lo(7)
                if p2 and not (last and s >= 2):
                    lo_xt(l, s - 2, 1)

            for s in range(SLOTS):
                slot(0, s, True, False)
            with dve.Fori(1, LAST) as l:
                for s in range(SLOTS):
                    slot(l, s, False, False)
            for s in range(SLOTS):
                slot(LAST, s, False, True)

            def outer_residual(u):
                i = final_set(0, u)
                dve.wait_ge(f_rstd[0], u + 1)
                dve.wait_ge(f_offset, u + 1)
                y = kt[u % 2]
                for t in range(T):
                    ins = d.scalar_tensor_tensor(out=y[:, t, :], in0=res_a[:, u, t, :], scalar=mv[i][:, t, 0:1],
                                                 in1=row[:, LAYERS, R_G1, :], op0=ALU.subtract, op1=ALU.mult)
                ins.then_inc(f_gain, 1)
                dve.wait_ge(f_gain, u + 1)
                for t in range(T):
                    ins = d.scalar_tensor_tensor(out=x_all[:, u, t, :], in0=y[:, t, :], scalar=rstd[i][:, t:t + 1],
                                                 in1=x_all[:, u, t, :], op0=ALU.mult, op1=ALU.add)
                ins.then_inc(f_sum, 1)
                dve.wait_ge(f_sum, u + 1)
                final_moments(1, u, x_all[:, u])

            def expert_moments(u):
                dve.wait_ge(f_norm[1], u + 1)
                final_moments(2, u, outer_rows(u))

            def lo_rows(u):
                dve.wait_ge(xn_hi, u + 1)
                d.tensor_tensor(xt_lo[:, u], ps(7), xt_hi[:, u].bitcast(F32), ALU.subtract).then_inc(xn_lo, 1)

            steps = [0]

            def link(ins):
                steps[0] += 1
                ins.then_inc(r_step, 1)
                dve.wait_ge(r_step, steps[0])

            def logits(p):
                dve.wait_ge(r_mm, p + 1)
                link(d.tensor_tensor(ex[:, :, :], ps(6)[:, 0:2 * T * EXPERTS].rearrange("p (t e) -> p t e", t=2 * T),
                                     r_bias[:, :].unsqueeze(1).to_broadcast([P, 2 * T, EXPERTS]), ALU.add))
                link(d.tensor_reduce(mx[:, :], ex[:, :, :], AX.X, ALU.max))
                d.tensor_tensor(ex[:, :, :], ex[:, :, :], mx[:, :].unsqueeze(2).to_broadcast([P, 2 * T, EXPERTS]),
                                ALU.subtract).then_inc(r_sub, 1)

            def over_experts(x):
                return x[:, :].unsqueeze(2).to_broadcast([P, 2 * T, EXPERTS])

            def choose(src, k):
                link(d.tensor_reduce(mx[:, :], src[:, :, :], AX.X, ALU.max))
                link(d.tensor_tensor(key[:, :, :], src[:, :, :], over_experts(mx), ALU.is_equal))
                link(d.tensor_tensor(key[:, :, :], key[:, :, :],
                                     order[:, :].unsqueeze(1).to_broadcast([P, 2 * T, EXPERTS]), ALU.mult))
                link(d.tensor_reduce(mx[:, :], key[:, :, :], AX.X, ALU.max))
                link(d.tensor_tensor(best[k][:, :, :], key[:, :, :], over_experts(mx), ALU.is_equal))

            def routing(p):
                dve.wait_ge(r_ex, p + 1)
                choose(ex, 0)
                link(d.scalar_tensor_tensor(out=rest[:, :, :], in0=best[0][:, :, :], scalar=-2.0, in1=ex[:, :, :],
                                            op0=ALU.mult, op1=ALU.add))
                choose(rest, 1)
                d.tensor_reduce(total[:, :], ex[:, :, :], AX.X, ALU.add)
                link(d.tensor_tensor(best[0][:, :, :], best[0][:, :, :], best[1][:, :, :], ALU.add))
                link(d.reciprocal(total[:, :], total[:, :]))
                link(d.tensor_tensor(best[0][:, :, :], best[0][:, :, :], ex[:, :, :], ALU.mult))
                d.tensor_tensor(gate[:, :, 2 * T * p:2 * T * p + 2 * T].rearrange("p e t -> p t e"), best[0][:, :, :],
                                over_experts(total), ALU.mult).then_inc(gate_done, 1)

            def combine(r, k, u, b):
                wait(dve, down_mm[k], r * HALVES + (u + 1))
                for t in range(T):
                    ins = d.scalar_tensor_tensor(
                        out=res_a[:, u, t, :], in0=ps(b)[:, t * P:(t + 1) * P],
                        scalar=gate[:, bass.ds(r * 2 + k, 1), T * u + t], in1=res_a[:, u, t, :],
                        op0=ALU.mult, op1=ALU.add)
                ins.then_inc(comb[k], 1)

            moments1(LAST, 3, 1)
            add_res2(LAST, 2, 1, True)
            outer_residual(0)
            lo_x1(LAST, 3, 0)
            lo_x1(LAST, 3, 1)
            moments2(LAST, 2, 0)
            expert_moments(0)
            outer_residual(1)
            add_res2(LAST, 3, 0, True)
            stack_moments(2)
            expert_moments(1)
            stack_moments(3)
            moments2(LAST, 2, 1)
            lo_rows(0)
            outer_residual(2)
            dve.wait_ge(eb_mm, 2)
            d.tensor_copy(e_bias[:, 1, :], ps(5)[:, 0:FF]).then_inc(eb_done, 1)
            outer_residual(3)
            lo_rows(1)
            add_res2(LAST, 3, 1, True)
            moments2(LAST, 3, 0)
            expert_moments(2)
            moments2(LAST, 3, 1)
            stack_moments(4)

            def weigh(k, u):
                if k == 0:
                    dve.wait_ge(gate_done, u // 2 + 1)
                    dve.wait_ge(acc_done, u + 1)
                else:
                    dve.wait_ge(comb[0], u + 1)
                combine(0, k, u, 4 + k)

            logits(0)
            expert_moments(3)
            routing(0)
            weigh(0, 0)
            weigh(1, 0)
            stack_moments(5)
            lo_rows(2)
            outer_residual(4)
            lo_rows(3)
            weigh(0, 1)
            expert_moments(4)
            for u in range(2, HALVES):
                if u % 2 == 0:
                    logits(u // 2)
                if u + 4 < HALVES:
                    stack_moments(u + 4)
                if u % 2 == 0:
                    routing(u // 2)
                weigh(1, u - 1)
                if u + 3 < HALVES:
                    outer_residual(u + 3)
                if u + 2 < HALVES:
                    lo_rows(u + 2)
                if u + 3 < HALVES:
                    expert_moments(u + 3)
                if u == HALVES - 1:
                    dve.wait_ge(eb_mm, 3)
                    d.tensor_copy(e_bias[:, 2, :], ps(7)[:, 0:FF]).then_inc(eb_done, 1)
                weigh(0, u)
            dve.wait_ge(comb[0], HALVES)
            combine(0, 1, HALVES - 1, 5)

            def combine_sweep(r, k, last=False):
                for u in range(HALVES):
                    if u == 0:
                        wait(dve, comb[1 - k], r * HALVES + (HALVES if k == 1 else 0))
                    combine(r, k, u, 4 + u % 2)
                    if u == 3 and not last:
                        wait(dve, eb_mm, r * 2 + (k + 2))
                        d.tensor_copy(e_bias[:, bass.ds(r * 2 + (k + 1), 1), :],
                                      ps(7)[:, 0:FF].unsqueeze(1)).then_inc(eb_done, 1)

            with dve.Fori(1, EXPERTS // 2 - 1) as r:
                combine_sweep(r, 0)
                combine_sweep(r, 1)
            combine_sweep(EXPERTS // 2 - 1, 0)
            combine_sweep(EXPERTS // 2 - 1, 1, last=True)

        @block.tensor
        def _(pe):
            t_ = nc.tensor

            def three(out_, a_hi, a_lo, b_hi, b_lo):
                t_.matmul(out_, a_hi, b_hi, start=True, stop=False)
                t_.matmul(out_, a_hi, b_lo, start=False, stop=False)
                return t_.matmul(out_, a_lo, b_hi, start=False, stop=True)

            def project(l, s, h, first, last):
                u = (2 * s + h) % HALVES
                if s == 0 and h == 0:
                    if first:
                        pe.wait_ge(qkv_split, 8)
                    else:
                        wait(pe, qkv_in, l * 16)
                wait(pe, xt_lo_done, upto(l, s, h))
                if h == 1:
                    wait(pe, s2_done, upto(l, s - 2, 0))
                three(ps(3 * h), this_qkv[:, 0, 0:P], this_qkv[:, 1, 0:P], xt_hi[:, u], xt_lo[:, u]).then_inc(q_mm, 1)
                if h == 1 and not (last and s == 3):
                    wait(pe, xt_lo_done, (2 if s == 0 else HALVES) if first and s < 3 else upto(l, s - 3, 1, base=8))
                elif h == 0 and ((s == 3 and not last) or (first and s == 0)):
                    wait(pe, bias_done, l * 8 + (16 if s == 3 else 8))
                elif h == 0 and s == 3:
                    wait(pe, eb_done, 1)
                for t in range(T):
                    b = ps((1, 4)[h] + t // 2)[:, (t % 2) * 256:(t % 2) * 256 + 256]
                    tile = slice(t * P, (t + 1) * P)
                    ins = three(b, xt_hi[:, u, tile], xt_lo[:, u, tile], this_qkv[:, 0, P:QKV], this_qkv[:, 1, P:QKV])
                ins.then_inc(kvp_mm, 1)

            def key_value(l, s, h):
                wait(pe, k_done, upto(l, s, h))
                wait(pe, v_done, upto(l, s, h))
                for q in two:
                    for t in two:
                        ins = t_.matmul(ps(1 + h)[:, q * 256:q * 256 + P + 1], kt[h][:, 2 * q + t, :],
                                        v[h][:, 2 * q + t, 0:P + 1], start=t == 0, stop=t == 1)
                ins.then_inc(kvm_mm, 1)

            def attention(l, s, h, first):
                wait(pe, kv_done, upto(l, s, h))
                wait(pe, qt_done, upto(l, s, h))
                if h == 0:
                    wait(pe, x1_lo_done, upto(l, s - 1, 1))
                else:
                    wait(pe, hid_done, upto(l, s - 1, 0, per=FF) - 3)
                for t in range(T):
                    ins = t_.matmul(bank[h][:, t // 2, (t % 2) * KVW:(t % 2 + 1) * KVW], qt[h][:, t * P:(t + 1) * P],
                                    kv[h][:, t // 2, :], start=True, stop=True)
                ins.then_inc(att_mm, 1)

            def flip(b, src):
                for t in range(T):
                    ins = t_.transpose(ps(b)[:, t * P:(t + 1) * P], src[:, t, :], ident[:, :])
                return ins

            def flip_att(l, s, h):
                wait(pe, att_done, upto(l, s, h))
                flip(2 * h, att[h]).then_inc(attt_mm, 1)

            def out_proj(l, s, h):
                if s == 0 and h == 0:
                    wait(pe, wo_in, l * 16 + 16)
                wait(pe, attt_sb, upto(l, s, h))
                wait(pe, hid_done, upto(l, s - 1, 1, per=FF) - h)
                for t in range(T):
                    ins = t_.matmul(ps(7 - h)[:, t * P:(t + 1) * P], att_t[h][:, t * P:(t + 1) * P], this_wo[:, :],
                                    start=True, stop=True)
                ins.then_inc(wo_mm, 1)

            def flip_x1(l, s, h, tail=False):
                wait(pe, x1_done, upto(l, s, h))
                if h == 1 and not tail:
                    wait(pe, qt_done, upto(l, s + 1, 0))
                flip(7 if h == 0 else 0, s1[h]).then_inc(t1_mm, 1)

            def ff_up(l, s, h, lw, between=None):
                if s % SLOTS == 0 and h == 0:
                    wait(pe, w1_in, lw * 16 + 16)
                wait(pe, x1_lo_done, upto(l, s, h))
                for c in range(FF):
                    chunk = slice(c * P, (c + 1) * P)
                    if h == 0 and c == 3:
                        wait(pe, s2_done, upto(l, s - 1, 1))
                    if h == 1 and c < 3:
                        wait(pe, hid_done, upto(l, s, 0, per=FF) - 2 + c)
                    three(ps(3 + h + c), this_w1[:, 0, chunk], this_w1[:, 1, chunk], x1_hi[h][:, :], x1_lo[h][:, :]
                          ).then_inc(w1_mm, 1)
                    if c == 1 and between is not None:
                        between()

            def ff_down(l, s, h, lw, between=None):
                if s % SLOTS == 0 and h == 0:
                    wait(pe, w2_in, lw * 16 + 16)
                wait(pe, hid_done, upto(l, s, h, per=FF))
                if h == 1:
                    wait(pe, s1_done, upto(l, s + 1, 1) if not (isinstance(l, int) and l == LAST and s == 3)
                         else upto(l, s, 1))
                for t in range(T):
                    for c in range(FF):
                        ins = t_.matmul(ps(3 if h == 0 else 6)[:, t * P:(t + 1) * P], hid[h][:, c, t * P:(t + 1) * P],
                                        this_w2[:, c, :], start=c == 0, stop=c == FF - 1)
                    if t == 1 and between is not None:
                        between()
                ins.then_inc(w2_mm, 1)

            def flip_x2(l, s, h):
                wait(pe, x2_done, upto(l, s, h, base=8))
                wait(pe, hid_done, upto(l, s + 1, 1, per=FF) - 3 + h)
                flip(4 + h, s2[h]).then_inc(t2_mm, 1)

            def bias_products(l):
                if isinstance(l, int) and l == 0:
                    pe.wait_ge(col_in, 16)
                wait(pe, raw_in, l * 32 + 32)
                wait(pe, boff_done, l * 8 + 8)
                b = ps(1)
                t_.matmul(b[:, 0:2 * P], boff[:, :], raw_qkv[:, P:QKV], start=True, stop=True)
                t_.matmul(b[:, 256:257], raw_qkv[:, 0:P], col[:, bass.ds(l + C_BIN, 1)], start=True, stop=True)
                for c in range(FF):
                    ins = t_.matmul(b[:, 260 + c:261 + c], raw_w1[:, c * P:(c + 1) * P], col[:, bass.ds(l + C_B1, 1)],
                                    start=True, stop=True)
                ins.then_inc(bias_mm, 8)

            def router_bias():
                pe.wait_ge(r_prep, 4)
                t_.matmul(ps(1)[:, 0:EXPERTS], boff[:, :], r_raw[:, :], start=True, stop=True).then_inc(rb_mm, 1)

            def expert_bias(e, b, at):
                wait(pe, raw_in, 32 * LAYERS + (e * 16 + 16))
                for c in range(FF):
                    ins = t_.matmul(ps(b)[:, at + c:at + c + 1], raw_w1[:, c * P:(c + 1) * P],
                                    col[:, C_BETA:C_BETA + 1], start=True, stop=True)
                ins.then_inc(eb_mm, 1)

            pe.wait_ge(const_done, 1)
            def start(u):
                pe.wait_ge(x2_done, u + 1)
                if 4 <= u < 6:
                    pe.wait_ge(xt_lo_done, u - 1)
                elif u >= 6:
                    pe.wait_ge(v_done, 2)
                flip(START_BANK[u], first_norm(u)).then_inc(t2_mm, 1)

            start(0)
            start(1)
            bias_products(0)

            def slot(l, s, first, last):
                p1, p2 = not first or s >= 1, not first or s >= 2
                lw1 = l if s >= 1 else l - 1
                lw2 = l if s >= 2 else l - 1
                project(l, s, 0, first, last)
                project(l, s, 1, first, last)
                if first and s == 0:
                    start(2)
                    start(3)
                if p2:
                    ff_down(l, s - 2, 1, lw2, between=lambda: flip_x1(l, s - 1, 0))
                elif p1:
                    flip_x1(l, s - 1, 0)
                key_value(l, s, 0)
                if p1:
                    ff_up(l, s - 1, 0, lw1, between=lambda: flip_x1(l, s - 1, 1))
                key_value(l, s, 1)
                attention(l, s, 0, first)
                attention(l, s, 1, first)
                if p1:
                    ff_up(l, s - 1, 1, lw1)
                if first and s == 0:
                    start(4)
                    start(5)
                flip_att(l, s, 0)
                if p2 and not (last and s >= 2):
                    flip_x2(l, s - 2, 0)
                flip_att(l, s, 1)
                if s == 2 and not last:
                    bias_products(l + 1)
                if s == 2 and last:
                    router_bias()
                    expert_bias(0, 1, 260)
                if p1:
                    ff_down(l, s - 1, 0, lw1)
                if first and s == 0:
                    pe.wait_ge(xt_lo_done, 6)
                out_proj(l, s, 0)
                out_proj(l, s, 1)
                if first and s == 0:
                    start(6)
                    start(7)
                if p2 and not (last and s >= 2):
                    flip_x2(l, s - 2, 1)

            for s in range(SLOTS):
                slot(0, s, True, False)
            with pe.Fori(1, LAST) as l:
                for s in range(SLOTS):
                    slot(l, s, False, False)
            for s in range(SLOTS):
                slot(LAST, s, False, True)
            ff_down(LAST, 2, 1, LAST)
            flip_x1(LAST, 3, 0, tail=True)
            flip_x1(LAST, 3, 1, tail=True)
            ff_up(LAST, 3, 0, LAST)
            ff_up(LAST, 3, 1, LAST)
            ff_down(LAST, 3, 0, LAST)
            ff_down(LAST, 3, 1, LAST)

            def flip_rows(u):
                pe.wait_ge(f_norm[2], u + 1)
                wait(pe, xn_lo, u)
                flip(7, expert_rows(u)).then_inc(ft_mm, 1)

            def route(p):
                pe.wait_ge(xn_lo, 2 * p + 2)
                pe.wait_ge(rb_done, 1)
                wait(pe, r_sub, p)
                for j in range(2 * T):
                    u, tile = 2 * p + j // T, slice(j % T * P, (j % T + 1) * P)
                    ins = three(ps(6)[:, j * EXPERTS:(j + 1) * EXPERTS], xt_hi[:, u, tile], xt_lo[:, u, tile],
                                r_hi[:, :], r_lo[:, :])
                ins.then_inc(r_mm, 1)

            def up(r, k, u):
                w = w1_set[k]
                for c in range(FF):
                    chunk = slice(c * P, (c + 1) * P)
                    if isinstance(r, int) and r == 0:
                        wait(pe, up_done[1 - k], FF * (u - 1 + k) + c + 1)
                    elif u > 0:
                        wait(pe, up_done[k], r * (FF * HALVES) + (FF * (u - 1) + c + 1))
                    else:
                        wait(pe, up_done[1 - k], r * (FF * HALVES) + (FF * HALVES * k - FF + c + 1))
                    three(ps(c), w[:, 0, chunk], w[:, 1, chunk], xt_hi[:, u], xt_lo[:, u]).then_inc(up_mm[k], 1)

            def down(r, k, u, buf, b):
                if u == 0:
                    wait(pe, w2e_in[k], r * 16 + 16)
                wait(pe, up_done[k], r * (FF * HALVES) + FF * (u + 1))
                for t in range(T):
                    for c in range(FF):
                        ins = t_.matmul(ps(b)[:, t * P:(t + 1) * P], hid[buf][:, c, t * P:(t + 1) * P],
                                        w2_set[k][:, c, :], start=c == 0, stop=c == FF - 1)
                ins.then_inc(down_mm[k], 1)

            flip_rows(0)
            expert_bias(1, 5, 0)
            pe.wait_ge(xn_lo, 1)
            pe.wait_ge(e_split, 2)
            pe.wait_ge(s2_done, upto(LAST, 3, 0))
            up(0, 0, 0)
            flip_rows(1)
            pe.wait_ge(e_split, 4)
            up(0, 1, 0)
            pe.wait_ge(eb_done, 2)
            down(0, 0, 0, 0, 4)
            pe.wait_ge(s2_done, upto(LAST, 3, 1))
            route(0)
            for u in range(1, HALVES):
                if u >= 2:
                    if u % 2 == 0:
                        route(u // 2)
                    pe.wait_ge(comb[1], u - 1)
                down(0, 1, u - 1, 1, 5)
                if u == 1:
                    flip_rows(2)
                up(0, 0, u)
                up(0, 1, u)
                if u + 2 < HALVES:
                    flip_rows(u + 2)
                elif u == HALVES - 1:
                    pe.wait_ge(xn_lo, HALVES)
                    expert_bias(2, 7, 0)
                pe.wait_ge(comb[0], u)
                down(0, 0, u, 0, 4)

            def sweep(r, k, last=False):
                for u in range(HALVES):
                    if u == 0:
                        wait(pe, e_split, r * 4 + (2 * k + 2))
                    up(r, k, u)
                    if u == 0:
                        prev = (r - 1, 1) if k == 0 else (r, 0)
                        wait(pe, comb[prev[1]], prev[0] * HALVES + (HALVES - 1 - k))
                        down(prev[0], prev[1], HALVES - 1, 1, 5)
                    else:
                        if u <= 2:
                            if k == 0 and u == 1:
                                wait(pe, comb[0], r * HALVES)
                            wait(pe, comb[1 - k], r * HALVES + (HALVES * k - HALVES + HALVES - 2 + u))
                        else:
                            wait(pe, comb[k], r * HALVES + (u - 2))
                        down(r, k, u - 1, (u - 1) % 2, 4 + (u - 1) % 2)
                    if u == 3 and not last:
                        wait(pe, eb_done, r * 2 + (k + 1))
                        expert_bias(r * 2 + (k + 1), 7, 0)

            with pe.Fori(1, EXPERTS // 2 - 1) as r:
                sweep(r, 0)
                sweep(r, 1)
            sweep(EXPERTS // 2 - 1, 0)
            sweep(EXPERTS // 2 - 1, 1, last=True)
            wait(pe, comb[1], (EXPERTS // 2 - 1) * HALVES + HALVES - 2)
            down(EXPERTS // 2 - 1, 1, HALVES - 1, 1, 5)


def kernel(**inputs):
    import concourse.bacc as _bacc
    from concourse.bass_utils import run_bass_kernel_spmd as _run

    a = {k: np.ascontiguousarray(np.asarray(v)) for k, v in inputs.items()}
    ones, zeros = np.ones((1, P), np.float32), np.zeros((1, P), np.float32)
    A = "L0_attn_"

    def halves(y):
        return np.ascontiguousarray(y.reshape(HALVES, T, P, P).transpose(0, 2, 1, 3))

    gin, bin_ = np.concatenate([ones, a[A + "g2"]]), np.concatenate([zeros, a[A + "be2"]])
    rows = np.stack([gin, bin_, np.concatenate([a[A + "bo"], zeros]),
                     np.concatenate([a[A + "g1"], a[A + "gf"][None]]), np.concatenate([a[A + "be1"], a[A + "bef"][None]]),
                     np.concatenate([a[A + "c2"], zeros]), np.concatenate([a[A + "bk"], zeros]),
                     np.concatenate([a[A + "bv"], zeros])], axis=1).reshape(LAYERS + 1, ROWS * P)
    cols = np.concatenate([gin[:LAYERS], bin_[:LAYERS], a[A + "g1"], a[A + "be1"], a[A + "bq"],
                           a[A + "c1"].reshape(LAYERS * FF, P), a["L0_ffn_gamma"][None], a["L0_ffn_beta"][None]]).T
    arrays = {
        "x": halves(a[A + "x"].reshape(-1, P)),
        "rows": rows,
        "cols": cols,
        "wqkv": np.concatenate([a[A + "Wq"], a[A + "Wk"], a[A + "Wv"]], axis=2),
        "wo": a[A + "Wo"],
        "w1": np.concatenate([a[A + "W1"], a["L0_ffn_W1"]]),
        "w2": np.concatenate([a[A + "W2"], a["L0_ffn_W2"]]),
        "router": a["L0_ffn_router_w"].T,
    }
    arrays = {k: np.ascontiguousarray(v) for k, v in arrays.items()}
    nc = _bacc.Bacc("TRN2", target_bir_lowering=False, num_devices=1)
    args = [nc.dram_tensor(k, v.shape, mybir.dt.from_np(v.dtype), kind="ExternalInput").ap() for k, v in arrays.items()]
    out = nc.dram_tensor("out", (HALVES, P, T, P), F32, kind="ExternalOutput").ap()
    build(nc, *args, out)
    r = _run(nc, [arrays], core_ids=[0])
    got = r.results[0]["out"]
    return np.ascontiguousarray(got.transpose(0, 2, 1, 3)).reshape(16, 256, P)
```
